# Optimizing a Trainium2 kernel written in Bass

```python
import numpy as np
import jax
import jax.numpy as jnp

def _softmax(x, axis=-1):
    return jax.nn.softmax(x, axis=axis)

def _gelu(x):
    return jax.nn.gelu(x, approximate=True)

def _silu(x):
    return jax.nn.silu(x)

def _sigmoid(x):
    return jax.nn.sigmoid(x)

def _layernorm(x, axis=-1, eps=1e-05):
    m = jnp.mean(x, axis=axis, keepdims=True)
    v = jnp.var(x, axis=axis, keepdims=True)
    return (x - m) / jnp.sqrt(v + eps)

def _scatter_add(tgt, idx, src, axis=0):
    return tgt.at[idx].add(src)

def _segment_sum(src, seg, n):
    return jax.ops.segment_sum(src, seg, n)
kernel_name = 'mk_gnn_preln_d2_gnn_r32_00f11a'

def setup_inputs(seed: int=0):
    np.random.seed(seed)
    _w = jnp.asarray

    def _rec_inputs():
        import jax
        import jax.numpy as jnp
        _gk = jax.random.key(seed)
        x = -8.776e-05 + 1 * jax.random.normal(jax.random.fold_in(_gk, 1), (3125, 256), jnp.float32)
        _s = jax.random.randint(jax.random.fold_in(_gk, 2), (25000,), 0, 3125, jnp.int32)
        _d = jax.random.randint(jax.random.fold_in(_gk, 3), (25000,), 0, 3125, jnp.int32)
        _loop = jnp.arange(3125, dtype=jnp.int32)
        src = jnp.concatenate([_s, _d, _loop])
        dst = jnp.concatenate([_d, _s, _loop])
        _o = jnp.argsort(dst, stable=True)
        src = src[_o]
        dst = dst[_o]
        edge_attr_64 = jax.random.uniform(jax.random.fold_in(_gk, 12), (53125, 64), jnp.float32, 0.0, 1)
        edge_weight = jax.random.uniform(jax.random.fold_in(_gk, 14), (53125,), jnp.float32, 0.0, 0.999995)
        return (x, src, dst, edge_attr_64, edge_weight)
    x, src, dst, edge_attr_64, edge_weight = _rec_inputs()

    def _L0_gnn_setup():
        import jax, jax.numpy as jnp
        import numpy as np
        N = 625
        E = 7500
        H = 256
        NH = 8
        HD = H // NH
        NRBF = 64
        EPS = 1e-05
        key = jax.random.key(seed)
        ks = jax.random.split(key, 20)
        s = 0.05
        return {'x': jax.random.normal(ks[0], (N, H), jnp.float32), 'edge_index': jax.random.randint(ks[1], (2, E), 0, N, dtype=jnp.int64), 'rbf': jax.random.uniform(ks[2], (E, NRBF), jnp.float32), 'cutoff': jax.random.uniform(ks[3], (E,), jnp.float32), 'w1': jax.random.normal(ks[4], (NRBF, H), jnp.float32) * s, 'b1': jnp.zeros((H,), jnp.float32), 'w2': jax.random.normal(ks[5], (H, H), jnp.float32) * s, 'b2': jnp.zeros((H,), jnp.float32), 'ln_w': jnp.ones((H,), jnp.float32), 'ln_b': jnp.zeros((H,), jnp.float32), 'wq': jax.random.normal(ks[6], (H, H), jnp.float32) * s, 'bq': jnp.zeros((H,), jnp.float32), 'wk': jax.random.normal(ks[7], (H, H), jnp.float32) * s, 'bk': jnp.zeros((H,), jnp.float32), 'wv': jax.random.normal(ks[8], (H, H), jnp.float32) * s, 'bv': jnp.zeros((H,), jnp.float32), 'wo': jax.random.normal(ks[9], (H, H), jnp.float32) * s, 'bo': jnp.zeros((H,), jnp.float32), 'gate': jnp.array([0.1], jnp.float32)}
    _L0_gnn_all = _L0_gnn_setup()
    _L0_gnn_in = {k: v for k, v in _L0_gnn_all.items() if k in ('w1', 'b1', 'w2', 'b2', 'ln_w', 'ln_b', 'wq', 'bq', 'wk', 'bk', 'wv', 'bv', 'wo', 'bo', 'gate')}
    del _L0_gnn_all

    def _L1_gnn_setup():
        import jax, jax.numpy as jnp
        import numpy as np
        N_NODES = 3125
        N_EDGES = 50000
        IN_FEATS = 256
        OUT_FEATS = 64
        NHEAD = 4
        ALPHA = 0.2
        key = jax.random.key(seed)
        k1, k2, k3, k4, k5, k6 = jax.random.split(key, 6)
        stdv_w = np.sqrt(6.0 / (IN_FEATS + OUT_FEATS * NHEAD))
        stdv_a = np.sqrt(6.0 / (NHEAD + OUT_FEATS))
        return {'x': jax.random.normal(k1, (N_NODES, IN_FEATS), dtype=jnp.float32), 'W': jax.random.uniform(k2, (IN_FEATS, OUT_FEATS * NHEAD), minval=-stdv_w, maxval=stdv_w, dtype=jnp.float32), 'a_l': jax.random.uniform(k3, (1, NHEAD, OUT_FEATS), minval=-stdv_a, maxval=stdv_a, dtype=jnp.float32), 'a_r': jax.random.uniform(k4, (1, NHEAD, OUT_FEATS), minval=-stdv_a, maxval=stdv_a, dtype=jnp.float32), 'row': jax.random.randint(k5, (N_EDGES,), 0, N_NODES, dtype=jnp.int32), 'col': jax.random.randint(k6, (N_EDGES,), 0, N_NODES, dtype=jnp.int32)}
    _L1_gnn_all = _L1_gnn_setup()
    _L1_gnn_in = {k: v for k, v in _L1_gnn_all.items() if k in ('W', 'a_l', 'a_r')}
    del _L1_gnn_all
    return {'x': x, 'src': src, 'dst': dst, 'edge_attr_64': edge_attr_64, 'edge_weight': edge_weight, 'L0_gnn_w1': _L0_gnn_in['w1'], 'L0_gnn_b1': _L0_gnn_in['b1'], 'L0_gnn_w2': _L0_gnn_in['w2'], 'L0_gnn_b2': _L0_gnn_in['b2'], 'L0_gnn_ln_w': _L0_gnn_in['ln_w'], 'L0_gnn_ln_b': _L0_gnn_in['ln_b'], 'L0_gnn_wq': _L0_gnn_in['wq'], 'L0_gnn_bq': _L0_gnn_in['bq'], 'L0_gnn_wk': _L0_gnn_in['wk'], 'L0_gnn_bk': _L0_gnn_in['bk'], 'L0_gnn_wv': _L0_gnn_in['wv'], 'L0_gnn_bv': _L0_gnn_in['bv'], 'L0_gnn_wo': _L0_gnn_in['wo'], 'L0_gnn_bo': _L0_gnn_in['bo'], 'L0_gnn_gate': _L0_gnn_in['gate'], 'L1_gnn_W': _L1_gnn_in['W'], 'L1_gnn_a_l': _L1_gnn_in['a_l'], 'L1_gnn_a_r': _L1_gnn_in['a_r']}

def reference(x, src, dst, edge_attr_64, edge_weight, L0_gnn_w1, L0_gnn_b1, L0_gnn_w2, L0_gnn_b2, L0_gnn_ln_w, L0_gnn_ln_b, L0_gnn_wq, L0_gnn_bq, L0_gnn_wk, L0_gnn_bk, L0_gnn_wv, L0_gnn_bv, L0_gnn_wo, L0_gnn_bo, L0_gnn_gate, L1_gnn_W, L1_gnn_a_l, L1_gnn_a_r):
    import jax
    import jax.numpy as jnp

    def _L0_gnn_ref(x, edge_index, rbf, cutoff, w1, b1, w2, b2, ln_w, ln_b, wq, bq, wk, bk, wv, bv, wo, bo, gate):
        import jax, jax.numpy as jnp
        import numpy as np
        N = 625
        E = 7500
        H = 256
        NH = 8
        HD = H // NH
        NRBF = 64
        EPS = 1e-05
        row, col = (edge_index[0], edge_index[1])
        n = x.shape[0]
        mu = jnp.mean(x, axis=-1, keepdims=True)
        var = jnp.mean((x - mu) ** 2, axis=-1, keepdims=True)
        xn = (x - mu) * jax.lax.rsqrt(var + EPS) * ln_w + ln_b
        w_phys = (jax.nn.silu(rbf @ w1 + b1) @ w2 + b2) * cutoff[:, None]
        msg_phys = xn[col] * w_phys
        Q = (xn @ wq + bq).reshape(n, NH, HD)
        K = (xn @ wk + bk).reshape(n, NH, HD)
        V = (xn @ wv + bv).reshape(n, NH, HD)
        q_e, k_e, v_e = (Q[row], K[col], V[col])
        scores = jnp.sum(q_e * k_e, axis=-1) / np.sqrt(HD)
        scores = scores * cutoff[:, None]
        attn = jax.nn.softmax(scores, axis=1)
        msg_attn = (attn[..., None] * v_e).reshape(-1, H)
        combined = msg_phys + gate * msg_attn
        aggr = jax.ops.segment_sum(combined, row, num_segments=n)
        return x + aggr @ wo + bo

    def _L1_gnn_ref(x, W, a_l, a_r, row, col):
        import jax, jax.numpy as jnp
        import numpy as np
        N_NODES = 3125
        N_EDGES = 50000
        IN_FEATS = 256
        OUT_FEATS = 64
        NHEAD = 4
        ALPHA = 0.2
        n = x.shape[0]
        h = (x @ W).reshape(n, NHEAD, OUT_FEATS)
        h = jnp.where(jnp.isnan(h), 0.0, h)
        h_l = (a_l * h).sum(-1)
        h_r = (a_r * h).sum(-1)
        e = h_l[row] + h_r[col]
        e = jnp.where(e > 0, e, ALPHA * e)
        m = jax.ops.segment_max(e, row, num_segments=n)
        m = jnp.where(jnp.isfinite(m), m, 0.0)
        ex = jnp.exp(e - m[row])
        denom = jax.ops.segment_sum(ex, row, num_segments=n)
        att = ex / (denom[row] + 1e-16)
        msg = att[:, :, None] * h[col]
        out = jax.ops.segment_sum(msg, row, num_segments=n)
        return out.reshape(n, NHEAD * OUT_FEATS)
    edge_index = jnp.stack([src, dst])
    h = jnp.maximum(_layernorm(x, axis=-1), 0.0)
    x = x + _L0_gnn_ref(h, edge_index, edge_attr_64, edge_weight, L0_gnn_w1, L0_gnn_b1, L0_gnn_w2, L0_gnn_b2, L0_gnn_ln_w, L0_gnn_ln_b, L0_gnn_wq, L0_gnn_bq, L0_gnn_wk, L0_gnn_bk, L0_gnn_wv, L0_gnn_bv, L0_gnn_wo, L0_gnn_bo, L0_gnn_gate)
    h = jnp.maximum(_layernorm(x, axis=-1), 0.0)
    x = x + _L1_gnn_ref(h, L1_gnn_W, L1_gnn_a_l, L1_gnn_a_r, src, dst)
    return x

_drawn_inputs = setup_inputs


def setup_inputs(seed=0):
    import zlib

    import numpy as np

    out = dict(_drawn_inputs(seed))
    spreads = {'L0_gnn_b1': (0.0, 0.1),
     'L0_gnn_b2': (0.0, 0.1),
     'L0_gnn_ln_w': (1.0, 0.2),
     'L0_gnn_ln_b': (0.0, 0.1),
     'L0_gnn_bq': (0.0, 2.0),
     'L0_gnn_bk': (0.0, 2.0),
     'L0_gnn_bv': (0.0, 0.741),
     'L0_gnn_bo': (0.0, 0.1)}
    factors = {'L0_gnn_wq': 6.764, 'L0_gnn_wk': 6.803}
    for name, (base, spread) in spreads.items():
        noise = np.random.default_rng([zlib.crc32(name.encode()), seed]).standard_normal(out[name].shape)
        drawn = base * np.exp(spread * noise) if base else spread * noise
        out[name] = jnp.asarray(drawn.astype(out[name].dtype))
    for name, factor in factors.items():
        out[name] = (out[name] * factor).astype(out[name].dtype)
    return out
```

```python
from contextlib import ExitStack

import numpy as np

import concourse.bass as bass
from concourse import mybir

ALU = mybir.AluOpType
ACT = mybir.ActivationFunctionType
AX = mybir.AxisListType
F32 = mybir.dt.float32
BF16 = mybir.dt.bfloat16
I32 = mybir.dt.int32

P = 128
EPS = 1e-5
BIG = 2.0 ** 100
SLOPE = 0.2
TINY = 1e-16


class Step:

    def __init__(self, k, u, unroll, total):
        self.k, self.u, self.unroll, self.total = k, u, unroll, total

    def back(self, d):
        return Step(self.k, self.u - d, self.unroll, self.total)

    @property
    def n(self):
        return self.k * self.unroll + self.u

    def real(self):
        return not isinstance(self.k, int) or 0 <= self.n < self.total

    def first(self, count):
        return isinstance(self.k, int) and self.n < count

    def slot(self, ring):
        return self.u % ring

    def turn(self, ring):
        return self.k * (self.unroll // ring) + self.u // ring


def run(eng, total, unroll, lag, body):
    head = -(-(lag + 4) // unroll) * unroll
    tail = total // unroll * unroll
    for t in range(min(head, tail)):
        body(Step(t // unroll, t % unroll, unroll, total))
    if tail > head:
        with eng.Fori(head // unroll, tail // unroll) as k:
            for u in range(unroll):
                body(Step(k, u, unroll, total))
    for t in range(max(tail, min(head, tail)), total + lag):
        body(Step(t // unroll, t % unroll, unroll, total))


def gnn_kernel(nc, x, src, dst, edge_attr_64, edge_weight, w1, b1, w2, b2, ln_w, ln_b, wq, bq, wk, bk,
               wv, bv, wo, bo, gate, W, a_l, a_r, out):
    N, H = x.shape
    E, RBF = edge_attr_64.shape
    NH0 = 8
    HD0 = H // NH0
    _, NH1, HD1 = a_l.shape
    HE = HD1 + 1
    NT = -(-N // P)
    NLAST = N - (NT - 1) * P
    COLS = 16
    NBLK = -(-E // (P * COLS))
    CC = NBLK * COLS
    REST = E - (NBLK - 1) * P * COLS
    RP, RR = REST // COLS, REST % COLS
    QUADS = CC // 4
    GJ = 2
    GE = GJ * P
    NG = (E + NT * (GE - 1)) // GE
    NG = -(-NG // 4) * 4
    NS = NG * GE
    MINUSED = -(-E // GE)
    REC = H + 4
    KVX = 3 * H
    ROW1 = NH1 * HE + NH1
    SKIP = 65536.0
    assert NS < SKIP and N < NT * P and QUADS % 4 == 0 and NT % 2 == 1

    rec_dram = nc.dram_tensor("sorted_edges", [NS + NT * GE, REC], F32, kind="Internal").ap()
    kvx_dram = nc.dram_tensor("node_kvx", [N, KVX], F32, kind="Internal").ap()
    row1_dram = nc.dram_tensor("node_row1", [N, ROW1], F32, kind="Internal").ap()

    with ExitStack() as ctx:
        def sb(name, shape, dt=F32):
            return ctx.enter_context(nc.sbuf_tensor(name, shape, dt))

        def sem(name):
            return ctx.enter_context(nc.semaphore(name))

        iota1 = sb("iota1", [P, P])
        iota_g = sb("iota_g", [P, NG])
        row_no = sb("row_no", [P, 1])
        ident = sb("ident", [P, P])
        ident_b = sb("ident_b", [P, P], BF16)
        upper = sb("upper", [P, P])
        ones = sb("ones", [P, P])
        w1_sb = sb("w1_sb", [P, H])
        w2_sb = sb("w2_sb", [P, 2, H])
        wqkv = sb("wqkv", [P, 2, KVX])
        wo_sb = sb("wo_sb", [P, 2, H])
        W_sb = sb("W_sb", [P, 2, H])
        b1_sb = sb("b1_sb", [P, 2])
        bqkv = sb("bqkv", [P, KVX])
        b2_bc = sb("b2_bc", [P, H])
        lnw_bc = sb("lnw_bc", [P, H])
        lnb_bc = sb("lnb_bc", [P, H])
        bo_bc = sb("bo_bc", [P, H])
        al_bc = sb("al_bc", [P, H])
        ar_bc = sb("ar_bc", [P, H])
        gate_bc = sb("gate_bc", [P, 1])

        xs = sb("xs", [P, NT, H])
        hq = sb("hq", [P, NT, H])
        mv = sb("mv", [P, NT, 2])
        rstd = sb("rstd", [P, NT])
        nmr = sb("nmr", [P, NT])
        st6 = sb("st6", [P, NT, 6])
        work = sb("work", [P, NT * CC + NT * CC // 2])
        oh = work[:, NT * CC:].bitcast(BF16).rearrange("p (b c) -> p b c", b=NT)
        rank = work[:, 0:NT * CC].rearrange("p (b c) -> p b c", b=NT)
        acc0 = work[:, 0:NT * H].rearrange("p (t n) -> p t n", t=NT)
        acc1 = work[:, NT * H:NT * (H + NH1 * HE)].rearrange("p (t n) -> p t n", t=NT)
        hl = sb("hl", [P, NT, NH1])
        hrmax = sb("hrmax", [P, NT, NH1])
        mrun = sb("mrun", [P, NT, NH1])
        den = sb("den", [P, NT, NH1])

        tile_f = sb("tile_f", [P, CC])
        meta_in = sb("meta_in", [P, CC, 4])
        pos_i = sb("pos_i", [P, CC], I32)
        cnt = sb("cnt", [P, NT])
        tot_i = sb("tot_i", [P, NT], I32)
        nch = sb("nch", [P, NT])
        gend = sb("gend", [P, NT])
        off = sb("off", [P, NT])
        zg_f = sb("zg_f", [P, 3 * NT])
        zg_i = sb("zg_i", [P, NT], I32)
        gt_f = sb("gt_f", [P, NG])
        gt_i = sb("gt_i", [P, NG], I32)
        meta_s = sb("meta_s", [P, NG, GJ, 2])

        arena_n = 10900
        arena = sb("arena", [P, arena_n])
        at = [0]

        def carve(n):
            v = arena[:, at[0]:at[0] + n]
            at[0] += n
            assert at[0] <= arena_n, at[0]
            return v

        kvx_st = carve(2 * KVX).rearrange("p (s n) -> p s n", s=2)
        xnT = carve(2 * H).rearrange("p (s c e) -> p s c e", s=2, c=2)
        at[0] = 0
        rbf = carve(2 * COLS * RBF).rearrange("p (s c n) -> p s c n", s=2, c=COLS)
        rbfT = carve(2 * 2 * P).rearrange("p (s c e) -> p s c e", s=2, c=2)
        hidT = carve(2 * 4 * 2 * P).rearrange("p (s m h e) -> p s m h e", s=2, m=2, h=2)
        recA = carve(4 * 4 * REC).rearrange("p (s c n) -> p s c n", s=4, c=4)
        src_i = carve(CC).bitcast(I32)
        dst_i = carve(CC).bitcast(I32)
        cut_in = carve(CC)
        part_i = carve(CC).bitcast(I32)
        pos_f = carve(CC)
        at[0] = 0
        recB = carve(4 * GJ * REC).rearrange("p (s c n) -> p s c n", s=4, c=GJ)
        kvx_g = carve(4 * GJ * KVX).rearrange("p (s c n) -> p s c n", s=4, c=GJ)
        prod = carve(GJ * H).rearrange("p (c n) -> p c n", c=GJ)
        msgP = carve(2 * GJ * H).rearrange("p (s c n) -> p s c n", s=2, c=GJ)
        msgA = carve(2 * GJ * H).rearrange("p (s c n) -> p s c n", s=2, c=GJ)
        at[0] = 0
        aT = carve(2 * H).rearrange("p (s c e) -> p s c e", s=2, c=2)
        h2 = carve(2 * H).rearrange("p (s n) -> p s n", s=2)
        h2c = carve(2 * H).rearrange("p (s n) -> p s n", s=2)
        isnum = carve(H).bitcast(I32)
        row1 = carve(2 * ROW1).rearrange("p (s n) -> p s n", s=2)
        hal = carve(2 * H).rearrange("p (s n) -> p s n", s=2)
        har = carve(2 * H).rearrange("p (s n) -> p s n", s=2)
        row1_g = carve(4 * GJ * ROW1).rearrange("p (s c n) -> p s c n", s=4, c=GJ)
        msg1 = carve(2 * GJ * NH1 * HE).rearrange("p (s c n) -> p s c n", s=2, c=GJ)
        pen = carve(2 * GJ * P // 2).bitcast(BF16).rearrange("p (s n) -> p s n", s=2)
        outb = carve(2 * H).rearrange("p (s n) -> p s n", s=2)

        zrows = sb("zrows", [P, GJ * REC])
        idxA = sb("idxA", [P, 4, 4], I32)
        idxB = sb("idxB", [P, 4, GJ], I32)
        srcB = sb("srcB", [P, 4, GJ])
        oneh = sb("oneh", [P, 4, GJ, P])
        onehT = sb("onehT", [P, 2, GJ, P])
        sc = sb("sc", [P, 2, GJ, NH0])
        smax = sb("smax", [P, GJ])
        pe_ = sb("pe_", [P, 2, GJ, NH0])
        psum_ = sb("psum_", [P, GJ])
        prec = sb("prec", [P, GJ])
        attn = sb("attn", [P, GJ, NH0])
        gmax = sb("gmax", [P, NH1])
        zz = sb("zz", [P, NH1])
        hm = sb("hm", [P, 4, 2 * NH1])
        mdiff = sb("mdiff", [P, 2, NH1])
        mscale = sb("mscale", [P, 4, NH1])
        ez = sb("ez", [P, GJ, NH1])
        el = sb("el", [P, GJ, NH1])
        es = sb("es", [P, GJ, NH1])
        em = sb("em", [P, 2, GJ, NH1])
        ew = sb("ew", [P, 2, GJ, NH1])

        ps = ctx.enter_context(nc.psum_tensor("ps", [P, 8, 512], F32))
        tr = (ps[:, 0, 0:2 * P], ps[:, 7, 0:2 * P])

        S = {}

        def s(name):
            if name not in S:
                S[name] = sem(name)
            return S[name]

        block = ctx.enter_context(nc.Block())

        def alone(eng):
            eng.sem_inc(s("waited_" + ("pool" if eng is nc.gpsimd else "dve")), 1)

        def row_bc(v, n):
            return v.partition_broadcast(P)

        @block.sync
        def _(sp):
            def chunks(w):
                return w.rearrange("(c p) n -> p c n", p=P)

            sp.wait_ge(s("edge_fill"), 3)
            whole = (NBLK - 1) * P * COLS
            for t, v in ((src_i, src), (dst_i, dst), (cut_in, edge_weight)):
                tv = t[:, :].rearrange("p (b j) -> p b j", j=COLS)
                sp.dma_start(tv[:, 0:NBLK - 1, :],
                             v[0:whole].rearrange("(b p j) -> p b j", p=P, j=COLS)).then_inc(s("edges_in"), 16)
                sp.dma_start(tv[0:RP, NBLK - 1, :],
                             v[whole:whole + RP * COLS].rearrange("(p j) -> p j", j=COLS)).then_inc(s("edges_in"), 16)
                sp.dma_start(tv[RP:RP + 1, NBLK - 1, 0:RR],
                             v[whole + RP * COLS:E].rearrange("(p j) -> p j", p=1)).then_inc(s("edges_in"), 16)
            sp.wait_ge(s("x_fill"), 1)
            sp.dma_start(xs[:, 0:NT - 1, :], x[0:(NT - 1) * P, :].rearrange("(t p) n -> p t n", p=P)).then_inc(s("x_in"), 16)
            sp.dma_start(xs[0:NLAST, NT - 1, :], x[(NT - 1) * P:N, :]).then_inc(s("x_in"), 16)
            for i, w in enumerate((wk, wv, wq)):
                sp.dma_start(wqkv[:, :, i * H:(i + 1) * H], chunks(w)).then_inc(s("w_in"), 16)
            for i, v in enumerate((bk, bv, bq)):
                sp.dma_start(bqkv[:, i * H:(i + 1) * H], row_bc(v, H)).then_inc(s("w_in"), 16)
            for t, v in ((b2_bc, b2), (lnw_bc, ln_w), (lnb_bc, ln_b), (bo_bc, bo)):
                sp.dma_start(t[:, :], row_bc(v, H)).then_inc(s("w_in"), 16)
            for t, v in ((al_bc, a_l), (ar_bc, a_r)):
                sp.dma_start(t[:, :], row_bc(v.rearrange("a h d -> (a h d)"), H)).then_inc(s("w_in"), 16)
            for t, w in ((w2_sb, w2), (wo_sb, wo), (W_sb, W)):
                sp.dma_start(t[:, :, :], chunks(w)).then_inc(s("w_in"), 16)
            for half in range(2):
                sp.dma_start(w1_sb[half * RBF:(half + 1) * RBF, :], w1[:, :]).then_inc(s("w_in"), 16)
            with nc.allow_non_contiguous_dma(reason="256 values, once"):
                sp.dma_start(b1_sb[:, :], b1.rearrange("(c p) -> p c", p=P)).then_inc(s("w_in"), 16)
            sp.dma_start(gate_bc[:, :], row_bc(gate, 1)).then_inc(s("w_in"), 16)

            def store_kvx(st):
                i = st.n
                sp.wait_ge(s("xn_ready"), i + 1)
                sp.wait_ge(s("kv_ready"), i + 1)
                rows = NLAST if isinstance(i, int) and i == NT - 1 else P
                sp.dma_start(kvx_dram[bass.ds(i * P, rows), :], kvx_st[0:rows, st.slot(2), :]).then_inc(
                    s(f"kvx_out{st.slot(2)}"), 16)

            run(sp, NT, 2, 0, lambda st: store_kvx(st) if st.real() else None)

            sp.wait_ge(s("const"), 3)
            sp.dma_start(rec_dram[MINUSED * GE:NS, :].rearrange("(g p j) n -> p g (j n)", p=P, j=GJ),
                         zrows[:, :].unsqueeze(1).to_broadcast([P, NG - MINUSED, GJ * REC])).then_inc(s("zeroed"), 16)
            sp.wait_ge(s("zg_ready"), 1)

            def zero_group(st):
                g = sp.value_load(zg_i[0:1, bass.ds(st.n, 1)], min_val=0, max_val=NG + NT - 1)
                sp.dma_start(rec_dram[bass.ds(g * GE, GE), :].rearrange("(p j) n -> p (j n)", j=GJ),
                             zrows[:, :]).then_inc(s("zeroed"), 16)

            run(sp, NT, 1, 0, zero_group)

            sp.wait_ge(s("kvx_out0"), 16 * (NT - NT // 2))
            sp.wait_ge(s("kvx_out1"), 16 * (NT // 2))
            sp.wait_ge(s("q_ready"), NT)

            def load_rbf(st):
                if not st.first(2):
                    sp.wait_ge(s("rbf_used"), 4 * st.n - 4)
                sp.dma_start(rbf[:, st.slot(2), :, :],
                             edge_attr_64[bass.ds(st.n * (P * COLS), P * COLS), :].rearrange(
                                 "(p j) n -> p j n", j=COLS)).then_inc(s(f"rbf_in{st.slot(2)}"), 16)

            run(sp, NBLK - 1, 2, 0, load_rbf)
            last = (NBLK - 1) % 2
            sp.wait_ge(s("rbf_used"), 4 * (NBLK - 1) - 4)
            sp.dma_start(rbf[0:RP, last, :, :],
                         edge_attr_64[whole:whole + RP * COLS, :].rearrange("(p j) n -> p j n", j=COLS)).then_inc(
                             s(f"rbf_in{last}"), 16)
            sp.dma_start(rbf[RP:RP + 1, last, 0:RR, :],
                         edge_attr_64[whole + RP * COLS:E, :].rearrange("(p j) n -> p j n", p=1)).then_inc(
                             s(f"rbf_in{last}"), 16)

            for r in range(4):
                sp.wait_ge(s(f"scattered{r}"), 16 * 4 * (QUADS // 4))

            def load_rec(st):
                if not st.first(4):
                    sp.wait_ge(s("rec_used"), st.n - 3)
                sp.dma_start(recB[:, st.slot(4), :, :].rearrange("p c n -> p (c n)"),
                             rec_dram[bass.ds(st.n * GE, GE), :].rearrange("(p j) n -> p (j n)", j=GJ)).then_inc(
                                 s(f"rec_in{st.slot(4)}"), 16)

            run(sp, NG, 4, 0, load_rec)

            def store_row1(st):
                i = st.n
                sp.wait_ge(s("hr_ready"), i + 1)
                rows = NLAST if isinstance(i, int) and i == NT - 1 else P
                sp.dma_start(row1_dram[bass.ds(i * P, rows), :], row1[0:rows, st.slot(2), :]).then_inc(
                    s(f"row1_out{st.slot(2)}"), 16)

            run(sp, NT, 2, 0, lambda st: store_row1(st) if st.real() else None)

            def store_out(st):
                i = st.n
                sp.wait_ge(s("out_ready"), i + 1)
                rows = NLAST if isinstance(i, int) and i == NT - 1 else P
                sp.dma_start(out[bass.ds(i * P, rows), :], outb[0:rows, st.slot(2), :]).then_inc(
                    s(f"out_stored{st.slot(2)}"), 16)

            run(sp, NT, 2, 0, lambda st: store_out(st) if st.real() else None)
            sp.wait_ge(s("out_stored0"), 16 * (NT - NT // 2))
            sp.wait_ge(s("out_stored1"), 16 * (NT // 2))

        @block.gpsimd
        def _(pool):
            pool.memset(src_i[:, :], NT * P + P).then_inc(s("edge_fill"), 1)
            pool.memset(dst_i[:, :], 0).then_inc(s("edge_fill"), 1)
            pool.memset(cut_in[:, :], 0.0).then_inc(s("edge_fill"), 1)
            pool.memset(xs[:, NT - 1, :], 0.0).then_inc(s("x_fill"), 1)
            pool.iota(iota1[:, :], [[1, P]], base=1, channel_multiplier=0,
                      allow_small_or_imprecise_dtypes=True).then_inc(s("iota"), 1)
            pool.iota(row_no[:, :], [[0, 1]], base=1, channel_multiplier=1,
                      allow_small_or_imprecise_dtypes=True).then_inc(s("iota"), 1)
            pool.iota(iota_g[:, :], [[1, NG]], base=0, channel_multiplier=0,
                      allow_small_or_imprecise_dtypes=True).then_inc(s("iota"), 1)
            pool.memset(ones[:, :], 1.0).then_inc(s("const"), 1)
            pool.memset(zrows[:, :], 0.0).then_inc(s("const"), 1)
            pool.memset(meta_in[:, :, :], 0.0).then_inc(s("const"), 1)

            pool.wait_ge(s("w_in"), 16 * 19)

            def residual(st):
                i = st.n
                pool.wait_ge(s("h_ready"), i + 1)
                alone(pool)
                pool.tensor_tensor(xs[:, bass.ds(i, 1), :].rearrange("p a n -> p (a n)"),
                                   xs[:, bass.ds(i, 1), :].rearrange("p a n -> p (a n)"),
                                   hq[:, bass.ds(i, 1), :].rearrange("p a n -> p (a n)"), ALU.add).then_inc(
                                       s("xh"), 1)
                pool.wait_ge(s("xh"), i + 1)
                alone(pool)
                pool.tensor_tensor(xs[:, bass.ds(i, 1), :].rearrange("p a n -> p (a n)"),
                                   xs[:, bass.ds(i, 1), :].rearrange("p a n -> p (a n)"),
                                   bo_bc[:, :], ALU.add).then_inc(s("xhb"), 1)

            run(pool, NT, 1, 0, residual)

            def affine(st):
                i = st.n
                xn = kvx_st[:, st.slot(2), 2 * H:3 * H]
                pool.wait_ge(s("xn_norm"), i + 1)
                alone(pool)
                pool.tensor_tensor(xn, xn, lnw_bc[:, :], ALU.mult).then_inc(s("xn_w"), 1)
                pool.wait_ge(s("xn_w"), i + 1)
                alone(pool)
                pool.tensor_tensor(xn, xn, lnb_bc[:, :], ALU.add).then_inc(s("xn_ready"), 1)

            run(pool, NT, 2, 0, lambda st: affine(st) if st.real() else None)

            pool.wait_ge(s("zeroed"), 16 * (NT + 1))

            def scatter(st):
                st = st.back(2)
                if not st.real():
                    return
                pool.wait_ge(s("idxA_ready"), st.n + 1)
                pool.wait_ge(s("metaA_ready"), st.n + 1)
                pool.wait_ge(s("recA_ready"), 2 * st.n + 2)
                alone(pool)
                for c in range(4):
                    pool.indirect_dma_start(
                        rec_dram[:, :], bass.IndirectOffsetOnAxis(ap=idxA[:, st.slot(4), c:c + 1], axis=0),
                        recA[:, st.slot(4), c, :], None, bounds_check=NS - 1, oob_is_err=False).then_inc(
                            s(f"scattered{st.slot(4)}"), 16)

            run(pool, QUADS, 4, 2, scatter)

            pool.memset(acc0[:, :, :], 0.0).then_inc(s("acc_zero"), 1)
            pool.memset(acc1[:, :, :], 0.0).then_inc(s("acc_zero"), 1)
            pool.memset(hrmax[:, :, :], -BIG).then_inc(s("acc_zero"), 1)
            pool.memset(mrun[:, :, :], -BIG).then_inc(s("acc_zero"), 1)

            pool.wait_ge(s("kvx_out0"), 16 * (NT - NT // 2))
            pool.wait_ge(s("kvx_out1"), 16 * (NT // 2))
            for r in range(4):
                pool.wait_ge(s(f"scattered{r}"), 16 * 4 * (QUADS // 4))

            def one_hot(st, used, made):
                if used is not None:
                    pool.wait_ge(*used)
                alone(pool)
                for j in range(GJ):
                    pool.tensor_scalar(oneh[:, st.slot(4), j, :], iota1[:, :], srcB[:, st.slot(4), j:j + 1],
                                       None, ALU.is_equal).then_inc(made, 1)

            def gather0(st):
                pool.wait_ge(s("idxB_ready"), st.n + 1)
                pool.wait_ge(s("srcB_ready"), st.n + 1)
                if not st.first(4):
                    pool.wait_ge(s("rec_used"), st.n - 3)
                    pool.wait_ge(s("msgA_ready"), st.n - 3)
                alone(pool)
                for j in range(GJ):
                    pool.indirect_dma_start(
                        kvx_g[:, st.slot(4), j, :], None, kvx_dram[:, :],
                        bass.IndirectOffsetOnAxis(ap=idxB[:, st.slot(4), j:j + 1], axis=0)).then_inc(
                            s(f"kvx_in{st.slot(4)}"), 16)
                one_hot(st, None if st.first(4) else (s("agg0_ready"), st.n - 3), s("oneh0"))

            run(pool, NG, 4, 0, gather0)

            pool.wait_ge(s("acc0_done"), NG)
            for r in range(2):
                v = row1[:, r, 0:NH1 * HE]
                pool.memset(v, 0.0).then_inc(s("row1_zero"), 1)
                pool.wait_ge(s("row1_zero"), r + 1)
                pool.memset(v.rearrange("p (h d) -> p h d", d=HE)[:, :, HD1:HE], 1.0).then_inc(s("row1_one"), 1)

            def products(st):
                i, r = st.n, st.slot(2)
                if not st.first(2):
                    pool.wait_ge(s("hr_ready"), i - 1)
                pool.wait_ge(s("row1_ready"), i + 1)
                heads = row1[:, r, 0:NH1 * HE].rearrange("p (h d) -> p h d", d=HE)[:, :, 0:HD1]
                alone(pool)
                for t, w in ((hal, al_bc), (har, ar_bc)):
                    pool.tensor_tensor(t[:, r, :].rearrange("p (h d) -> p h d", d=HD1), heads,
                                       w[:, :].rearrange("p (h d) -> p h d", d=HD1), ALU.mult).then_inc(
                                           s("ha_ready"), 1)
                if isinstance(i, int) and i + 2 >= NT:
                    return
                pool.wait_ge(s(f"row1_out{r}"), 16 * st.turn(2) + 16)
                pool.wait_ge(s("ha_ready"), 2 * i + 2)
                alone(pool)
                pool.memset(heads, 0.0).then_inc(s("row1_zero"), 1)

            run(pool, NT, 2, 0, lambda st: products(st) if st.real() else None)

            pool.wait_ge(s("row1_out0"), 16 * (NT - NT // 2))
            pool.wait_ge(s("row1_out1"), 16 * (NT // 2))

            def gather1(st):
                pool.wait_ge(s("idxC_ready"), st.n + 1)
                pool.wait_ge(s("srcC_ready"), st.n + 1)
                if not st.first(4):
                    pool.wait_ge(s("msg1_ready"), st.n - 3)
                alone(pool)
                for j in range(GJ):
                    pool.indirect_dma_start(
                        row1_g[:, st.slot(4), j, :], None, row1_dram[:, :],
                        bass.IndirectOffsetOnAxis(ap=idxB[:, st.slot(4), j:j + 1], axis=0)).then_inc(
                            s(f"row1_in{st.slot(4)}"), 16)
                one_hot(st, None if st.first(4) else (s("agg1_ready"), st.n - 3), s("oneh1"))

            run(pool, NG, 4, 0, gather1)

        @block.scalar
        def _(act):
            act.wait_ge(s("var1"), 1)
            act.activation(rstd[:, :], rstd[:, :], ACT.Sqrt).then_inc(s("std1"), 1)
            act.wait_ge(s("nmr1"), 1)

            def relu_h(st):
                i = st.n
                act.activation(hq[:, bass.ds(i, 1), :].rearrange("p a n -> p (a n)"),
                               xs[:, bass.ds(i, 1), :].rearrange("p a n -> p (a n)"), ACT.Relu,
                               bias=nmr[:, bass.ds(i, 1)], scale=rstd[:, bass.ds(i, 1)]).then_inc(s("h_ready"), 1)

            run(act, NT, 1, 0, relu_h)
            act.wait_ge(s("var2"), 1)
            act.activation(rstd[:, :], rstd[:, :], ACT.Sqrt).then_inc(s("std2"), 1)

            def copy_xnT(st):
                act.wait_ge(s("xn_tr"), st.n + 1)
                if not st.first(2):
                    act.wait_ge(s("qkv_mm"), st.n - 1)
                act.copy(xnT[:, st.slot(2), :, :], tr[st.slot(2)].rearrange(
                    "p (c e) -> p c e", c=2)).then_inc(s("xnT"), 1)

            run(act, NT, 2, 0, lambda st: copy_xnT(st) if st.real() else None)

            act.wait_ge(s("pos_ready"), 1)

            def mlp(st):
                if st.real():
                    if not st.first(4):
                        act.wait_ge(s(f"scattered{st.slot(4)}"), 64 * st.turn(4))
                    act.copy(idxA[:, st.slot(4), :], pos_i[:, bass.ds(st.n * 4, 4)]).then_inc(s("idxA_ready"), 1)
                st = st.back(1)
                if st.real():
                    act.wait_ge(s("hid_mm"), st.n + 1)
                    if not st.first(2):
                        act.wait_ge(s("row_mm"), 2 * st.n - 2)
                    for m in range(2):
                        bank = 1 + 2 * st.slot(2)
                        act.activation(hidT[:, st.slot(2), m, :, :], ps[:, bank:bank + 2, m * 256:m * 256 + 256],
                                       ACT.Silu, bias=b1_sb[:, m:m + 1]).then_inc(s("hidT"), 1)

            run(act, QUADS, 4, 1, mlp)

            def layer0(st):
                if st.real():
                    r = st.slot(4)
                    act.wait_ge(s(f"rec_in{r}"), 16 * st.turn(4) + 16)
                    if not st.first(4):
                        act.wait_ge(s(f"kvx_in{r}"), 32 * st.turn(4))
                        act.wait_ge(s("oneh0"), 2 * st.n - 6)
                    act.copy(idxB[:, r, :], recB[:, r, :, H + 2]).then_inc(s("idxB_ready"), 1)
                    act.copy(srcB[:, r, :], recB[:, r, :, H + 1]).then_inc(s("srcB_ready"), 1)
                    act.copy(meta_s[:, bass.ds(st.n, 1), :, :].rearrange("p a c n -> p (a c) n"),
                             recB[:, r, :, H + 1:H + 3]).then_inc(s("meta_s"), 1)
                st1 = st.back(1)
                if st1.real():
                    act.wait_ge(s("oneh_tr0"), st1.n + 1)
                    if not st1.first(2):
                        act.wait_ge(s("qe_ready"), st1.n - 1)
                    r = st1.slot(2)
                    act.copy(onehT[:, r, :, :], tr[r].rearrange(
                        "p (c e) -> p c e", c=GJ)).then_inc(s("onehT0"), 1)
                st2 = st.back(2)
                if st2.real():
                    act.wait_ge(s("sc_ready"), st2.n + 1)
                    if not st2.first(2):
                        act.wait_ge(s("attn"), st2.n - 1)
                    r = st2.slot(2)
                    act.activation(pe_[:, r, :, :], sc[:, r, :, :], ACT.Exp, scale=float(HD0) ** -0.5).then_inc(
                        s("exp0"), 1)

            run(act, NG, 4, 2, layer0)

            def copy_aT(st):
                act.wait_ge(s("a_tr"), st.n + 1)
                if not st.first(2):
                    act.wait_ge(s("wo_mm"), st.n - 1)
                act.copy(aT[:, st.slot(2), :, :], tr[st.slot(2)].rearrange(
                    "p (c e) -> p c e", c=2)).then_inc(s("aT"), 1)

            run(act, NT, 2, 0, lambda st: copy_aT(st) if st.real() else None)
            act.wait_ge(s("var3"), 1)
            act.activation(rstd[:, :], rstd[:, :], ACT.Sqrt).then_inc(s("std3"), 1)
            act.wait_ge(s("nmr3"), 1)

            def node1(st):
                if st.real():
                    i, r = st.n, st.slot(2)
                    if not st.first(2):
                        act.wait_ge(s("h2_tr"), i - 1)
                    act.activation(h2[:, r, :], xs[:, bass.ds(i, 1), :].rearrange("p a n -> p (a n)"), ACT.Relu,
                                   bias=nmr[:, bass.ds(i, 1)], scale=rstd[:, bass.ds(i, 1)]).then_inc(s("h2"), 1)
                    act.wait_ge(s("h2_tr"), i + 1)
                    if not st.first(2):
                        act.wait_ge(s("w_mm"), i - 1)
                    act.copy(aT[:, r, :, :], tr[r].rearrange(
                        "p (c e) -> p c e", c=2)).then_inc(s("h2T"), 1)
                st = st.back(1)
                if st.real():
                    i, r = st.n, st.slot(2)
                    act.wait_ge(s("w_mm"), i + 1)
                    if not st.first(2):
                        act.wait_ge(s("row1_ready"), i - 1)
                    act.copy(h2c[:, r, :], ps[:, 1 + r, 0:H]).then_inc(s("h2c"), 1)

            run(act, NT, 2, 1, node1)

            def layer1(st):
                if st.real():
                    r = st.slot(4)
                    if not st.first(4):
                        act.wait_ge(s(f"row1_in{r}"), 32 * st.turn(4))
                        act.wait_ge(s("oneh1"), 2 * st.n - 6)
                    m = meta_s[:, bass.ds(st.n, 1), :, :].rearrange("p a c n -> p (a c) n")
                    act.copy(srcB[:, r, :], m[:, :, 0]).then_inc(s("srcC_ready"), 1)
                    act.copy(idxB[:, r, :], m[:, :, 1]).then_inc(s("idxC_ready"), 1)
                st1 = st.back(1)
                if st1.real():
                    r = st1.slot(2)
                    act.wait_ge(s("oneh_tr1"), st1.n + 1)
                    if not st1.first(2):
                        act.wait_ge(s("hm_mm"), st1.n - 1)
                        act.wait_ge(s("hr_mm"), st1.n - 1)
                    act.activation(pen[:, r, :], tr[r], ACT.Copy, bias=-BIG, scale=BIG).then_inc(s("pen"), 1)
                    act.copy(onehT[:, r, :, :], tr[r].rearrange("p (c e) -> p c e", c=GJ)).then_inc(s("onehT1"), 1)
                st2 = st.back(2)
                if st2.real():
                    act.wait_ge(s("mdiff"), st2.n + 1)
                    if not st2.first(4):
                        act.wait_ge(s("acc1_scaled"), st2.n - 3)
                    act.activation(mscale[:, st2.slot(4), :], mdiff[:, st2.slot(2), :], ACT.Exp).then_inc(
                        s("mscale"), 1)
                st3 = st.back(3)
                if st3.real():
                    act.wait_ge(s("em"), st3.n + 1)
                    if not st3.first(2):
                        act.wait_ge(s("msg1_ready"), st3.n - 1)
                    r = st3.slot(2)
                    act.activation(ew[:, r, :, :], em[:, r, :, :], ACT.Exp).then_inc(s("exp1"), 1)

            run(act, NG, 4, 3, layer1)

        @block.vector
        def _(dve):
            made = [0]

            def link(ins):
                made[0] += 1
                ins.then_inc(s("chain"), 1)
                dve.wait_ge(s("chain"), made[0])

            dve.wait_ge(s("iota"), 3)
            dve.tensor_scalar(ident[:, :], iota1[:, :], row_no[:, 0:1], None, ALU.is_equal).then_inc(s("ident"), 1)
            dve.tensor_scalar(ident_b[:, :], iota1[:, :], row_no[:, 0:1], None, ALU.is_equal).then_inc(s("ident"), 1)
            dve.tensor_scalar(upper[:, :], iota1[:, :], row_no[:, 0:1], None, ALU.is_gt).then_inc(s("ident"), 1)

            def tile(t, i):
                return t[:, bass.ds(i, 1), :].rearrange("p a n -> p (a n)")

            def stats(name, source, ready):
                def one(st):
                    if ready is not None:
                        dve.wait_ge(ready, st.n + 1)
                    dve.bn_stats(tile(st6, st.n), tile(source, st.n)).then_inc(s(name + "_st"), 1)

                run(dve, NT, 1, 0, one)
                dve.wait_ge(s(name + "_st"), NT)
                for i in range(NT):
                    ins = dve.bn_aggr(mv[:, i, :], st6[:, i, :])
                link(ins)

            def rstds(n):
                dve.tensor_scalar(rstd[:, :], mv[:, :, 1], EPS, None, ALU.add).then_inc(s(f"var{n}"), 1)
                dve.wait_ge(s(f"std{n}"), 1)
                link(dve.reciprocal(rstd[:, :], rstd[:, :]))
                dve.scalar_tensor_tensor(nmr[:, :], mv[:, :, 0], -1.0, rstd[:, :], ALU.mult, ALU.mult).then_inc(
                    s(f"nmr{n}"), 1)
                dve.wait_ge(s(f"nmr{n}"), 1)

            dve.wait_ge(s("x_in"), 32)
            stats("x", xs, None)
            rstds(1)
            stats("h", hq, s("h_ready"))
            dve.wait_ge(s("h_ready"), NT)
            rstds(2)
            dve.wait_ge(s("w_in"), 16 * 19)
            dve.wait_ge(s("xh"), NT)

            def node0(st):
                if st.real():
                    i, r = st.n, st.slot(2)
                    if not st.first(2):
                        dve.wait_ge(s(f"kvx_out{r}"), 16 * st.turn(2))
                    dve.tensor_scalar(kvx_st[:, r, 2 * H:3 * H], tile(hq, i), rstd[:, bass.ds(i, 1)],
                                      nmr[:, bass.ds(i, 1)], ALU.mult, ALU.add).then_inc(s("xn_norm"), 1)
                st = st.back(1)
                if st.real():
                    i, r = st.n, st.slot(2)
                    dve.wait_ge(s("qkv_mm"), i + 1)
                    dve.tensor_tensor(kvx_st[:, r, 0:2 * H], ps[:, 1 + r, :], bqkv[:, 0:2 * H], ALU.add).then_inc(
                        s("kv_ready"), 1)
                    dve.tensor_tensor(tile(hq, i), ps[:, 3 + r, 0:H], bqkv[:, 2 * H:3 * H], ALU.add).then_inc(
                        s("q_ready"), 1)

            run(dve, NT, 2, 1, node0)

            dve.wait_ge(s("edges_in"), 16 * 9)
            dve.wait_ge(s("const"), 3)
            link(dve.tensor_single_scalar(part_i[:, :], src_i[:, :], 7, ALU.arith_shift_right))
            link(dve.tensor_copy(tile_f[:, :], part_i[:, :]))
            link(dve.tensor_single_scalar(part_i[:, :], src_i[:, :], P - 1, ALU.bitwise_and))
            dve.tensor_scalar(meta_in[:, :, 1], part_i[:, :], 1.0, None, ALU.add).then_inc(s("meta_in"), 1)
            dve.tensor_copy(meta_in[:, :, 2], dst_i[:, :]).then_inc(s("meta_in"), 1)
            dve.tensor_copy(meta_in[:, :, 0], cut_in[:, :]).then_inc(s("meta_in"), 1)
            for b in range(NT):
                ins = dve.tensor_scalar(oh[:, b, :], tile_f[:, :], float(b), None, ALU.is_equal)
            link(ins)
            link(dve.reduce_sum(cnt[:, :], oh[:, :, :], axis=AX.X))
            dve.sem_inc(s("cnt_ready"), 1)
            dve.wait_ge(s("cnt_mm"), 1)
            tot, pre = ps[:, 5, 0:NT], ps[:, 5, NT:2 * NT]
            link(dve.tensor_scalar(tot_i[:, :], tot, float(GE - 1), None, ALU.add))
            link(dve.tensor_single_scalar(tot_i[:, :], tot_i[:, :], 8, ALU.arith_shift_right))
            link(dve.tensor_copy(nch[:, :], tot_i[:, :]))
            link(dve.tensor_tensor_scan(gend[:, :], nch[:, :], nch[:, :], 0.0, ALU.add, ALU.max))
            link(dve.tensor_tensor(off[:, :], gend[:, :], nch[:, :], ALU.subtract))
            link(dve.scalar_tensor_tensor(off[:, :], off[:, :], float(GE), pre, ALU.mult, ALU.add))
            spare, keep = zg_f[:, NT:2 * NT], zg_f[:, 2 * NT:3 * NT]
            dve.tensor_scalar(spare, iota_g[:, 0:NT], float(NG), None, ALU.add)
            dve.tensor_scalar(keep, nch[:, :], 1.0, None, ALU.min)
            link(dve.tensor_scalar(zg_f[:, 0:NT], gend[:, :], -1.0, None, ALU.add))
            link(dve.scalar_tensor_tensor(keep, zg_f[:, 0:NT], float(MINUSED), keep, ALU.is_lt, ALU.mult))
            link(dve.tensor_tensor(zg_f[:, 0:NT], zg_f[:, 0:NT], spare, ALU.subtract))
            link(dve.tensor_tensor(zg_f[:, 0:NT], zg_f[:, 0:NT], keep, ALU.mult))
            dve.tensor_tensor(zg_i[:, :], zg_f[:, 0:NT], spare, ALU.add).then_inc(s("zg_ready"), 1)
            cmp = rank[:, :, 0:NG]
            for b in range(NT):
                ins = dve.tensor_scalar(cmp[:, b, :], iota_g[:, :], gend[:, b:b + 1], None, ALU.is_ge)
            link(ins)
            link(dve.reduce_sum(gt_f[:, :], cmp.rearrange("p b g -> p g b"), axis=AX.X))
            dve.tensor_scalar(gt_i[:, :], gt_f[:, :], float(NT - 1), None, ALU.min).then_inc(s("gt_ready"), 1)
            dve.wait_ge(s("gt_ready"), 1)
            for b in range(NT):
                ins = dve.tensor_tensor_scan(rank[:, b, :], oh[:, b, :], oh[:, b, :], off[:, b:b + 1],
                                             ALU.add, ALU.max)
            link(ins)
            link(dve.tensor_tensor(rank[:, :, :], rank[:, :, :], oh[:, :, :], ALU.mult))
            link(dve.reduce_sum(pos_f[:, :], rank.rearrange("p b c -> p c b"), axis=AX.X))
            link(dve.tensor_scalar(tile_f[:, :], tile_f[:, :], float(NT) - 0.5, SKIP, ALU.is_gt, ALU.mult))
            dve.scalar_tensor_tensor(pos_i[:, :], pos_f[:, :], -1.0, tile_f[:, :], ALU.add, ALU.add).then_inc(
                s("pos_ready"), 1)

            def mlp(st):
                if st.real():
                    r = st.slot(2)
                    dve.wait_ge(s("rbf_used"), st.n + 1)
                    if not st.first(2):
                        dve.wait_ge(s("hid_mm"), st.n - 1)
                    dve.tensor_copy(rbfT[:, r, :, :], tr[r].rearrange(
                        "p (c e) -> p c e", c=2)).then_inc(s("rbfT"), 1)
                st = st.back(2)
                if st.real():
                    r = st.slot(4)
                    if not st.first(4):
                        dve.wait_ge(s(f"scattered{r}"), 64 * st.turn(4))
                    dve.tensor_copy(recA[:, r, :, H:REC], meta_in[:, bass.ds(st.n * 4, 4), :]).then_inc(
                        s("metaA_ready"), 1)
                    for t in range(2):
                        dve.wait_ge(s("row_mm"), 2 * st.n + t + 1)
                        dve.tensor_tensor(recA[:, r, 2 * t:2 * t + 2, 0:H],
                                          ps[:, 5 + t, :].rearrange("p (c n) -> p c n", c=2),
                                          b2_bc[:, :].unsqueeze(1).to_broadcast([P, 2, H]),
                                          ALU.add).then_inc(s("recA_ready"), 1)

            dve.wait_ge(s("meta_in"), 3)
            run(dve, QUADS, 4, 2, mlp)

            dve.wait_ge(s("acc_zero"), 4)

            def heads(v):
                return v.rearrange("p c (h d) -> p c h d", d=HD0)

            def layer0(st):
                a = st.back(2)
                if a.real():
                    r, r4, n = a.slot(2), a.slot(4), a.n
                    dve.wait_ge(s("qe_ready"), n + 1)
                    dve.wait_ge(s(f"kvx_in{r4}"), 32 * a.turn(4) + 32)
                    dve.tensor_tensor(prod[:, :, :], ps[:, 1 + r, :].rearrange("p (c n) -> p c n", c=GJ),
                                      kvx_g[:, r4, :, 0:H], ALU.mult).then_inc(s("qk"), 1)
                    dve.wait_ge(s("qk"), n + 1)
                    dve.reduce_sum(sc[:, r, :, :], heads(prod), axis=AX.X).then_inc(s("qk_sum"), 1)
                    dve.wait_ge(s(f"rec_in{r4}"), 16 * a.turn(4) + 16)
                    dve.wait_ge(s("qk_sum"), n + 1)
                    dve.tensor_tensor(sc[:, r, :, :], sc[:, r, :, :],
                                      recB[:, r4, :, H:H + 1].to_broadcast([P, GJ, NH0]), ALU.mult).then_inc(
                                          s("qk_cut"), 1)
                    dve.wait_ge(s("qk_cut"), n + 1)
                    dve.reduce_max(smax[:, :], sc[:, r, :, :], axis=AX.X).then_inc(s("qk_max"), 1)
                    dve.wait_ge(s("qk_max"), n + 1)
                    dve.tensor_tensor(sc[:, r, :, :], sc[:, r, :, :],
                                      smax[:, :].unsqueeze(2).to_broadcast([P, GJ, NH0]), ALU.subtract).then_inc(
                                          s("sc_ready"), 1)
                b = st.back(3)
                if b.real():
                    r, r4, n = b.slot(2), b.slot(4), b.n
                    if not b.first(2):
                        dve.wait_ge(s("agg0_ready"), n - 1)
                    for j in range(GJ):
                        ins = dve.scalar_tensor_tensor(msgP[:, r, j, :], recB[:, r4, j, 0:H],
                                                       recB[:, r4, j, H:H + 1], kvx_g[:, r4, j, 2 * H:3 * H],
                                                       ALU.mult, ALU.mult)
                    ins.then_inc(s("rec_used"), 1)
                    dve.wait_ge(s("exp0"), n + 1)
                    dve.reduce_sum(psum_[:, :], pe_[:, r, :, :], axis=AX.X).then_inc(s("psum"), 1)
                    dve.wait_ge(s("psum"), n + 1)
                    dve.reciprocal(prec[:, :], psum_[:, :]).then_inc(s("prec"), 1)
                    dve.wait_ge(s("prec"), n + 1)
                    if not b.first(1):
                        dve.wait_ge(s("msgA_ready"), n)
                    dve.scalar_tensor_tensor(attn[:, :, :], pe_[:, r, :, :], gate_bc[:, 0:1],
                                             prec[:, :].unsqueeze(2).to_broadcast([P, GJ, NH0]),
                                             ALU.mult, ALU.mult).then_inc(s("attn"), 1)
                    dve.wait_ge(s("attn"), n + 1)
                    dve.tensor_tensor(heads(msgA[:, r, :, :]), heads(kvx_g[:, r4, :, H:2 * H]),
                                      attn[:, :, :].unsqueeze(3).to_broadcast([P, GJ, NH0, HD0]),
                                      ALU.mult).then_inc(s("msgA_ready"), 1)
                c = st.back(4)
                if c.real():
                    t = dve.value_load(gt_i[0:1, bass.ds(c.n, 1)], min_val=0, max_val=NT - 1)
                    dve.wait_ge(s("agg0_ready"), c.n + 1)
                    if not c.first(1):
                        dve.wait_ge(s("acc0_done"), c.n)
                    dve.tensor_tensor(tile(acc0, t), tile(acc0, t), ps[:, 3 + c.slot(2), 0:H], ALU.add).then_inc(
                        s("acc0_done"), 1)

            run(dve, NG, 4, 4, layer0)

            def node1(st):
                i = st.n
                dve.wait_ge(s("wo_mm"), i + 1)
                dve.tensor_tensor(tile(xs, i), tile(xs, i), ps[:, 1 + st.slot(2), 0:H], ALU.add).then_inc(s("x1"), 1)

            run(dve, NT, 2, 0, lambda st: node1(st) if st.real() else None)
            stats("x1", xs, s("x1"))
            rstds(3)

            def node2(st):
                i, r = st.n, st.slot(2)
                dve.wait_ge(s("h2c"), i + 1)
                dve.tensor_tensor(isnum, h2c[:, r, :], h2c[:, r, :], ALU.is_equal).then_inc(s("isnum"), 1)
                dve.wait_ge(s("isnum"), i + 1)
                dve.wait_ge(s("row1_zero"), i + 1)
                dve.wait_ge(s("row1_one"), 2)
                alone(dve)
                dve.copy_predicated(row1[:, r, 0:NH1 * HE].rearrange("p (h d) -> p h d", d=HE)[:, :, 0:HD1],
                                    isnum.rearrange("p (h d) -> p h d", d=HD1),
                                    h2c[:, r, :].rearrange("p (h d) -> p h d", d=HD1)).then_inc(s("row1_ready"), 1)
                dve.wait_ge(s("ha_ready"), 2 * i + 2)
                dve.reduce_sum(tile(hl, i), hal[:, r, :].rearrange("p (h d) -> p h d", d=HD1), axis=AX.X).then_inc(
                    s("hl_ready"), 1)
                dve.reduce_sum(row1[:, r, NH1 * HE:ROW1], har[:, r, :].rearrange("p (h d) -> p h d", d=HD1),
                               axis=AX.X).then_inc(s("hr_ready"), 1)

            run(dve, NT, 2, 0, lambda st: node2(st) if st.real() else None)
            dve.wait_ge(s("hl_ready"), NT)

            def layer1(st):
                a = st.back(2)
                if a.real():
                    n, r = a.n, a.slot(2)
                    t = dve.value_load(gt_i[0:1, bass.ds(n, 1)], min_val=0, max_val=NT - 1)
                    dve.wait_ge(s("hr_mm"), n + 1)
                    if not a.first(1):
                        dve.wait_ge(s("hrmax"), n)
                    dve.tensor_reduce(gmax[:, :], ps[:, 1:3, :].rearrange(
                        "p j (h e) -> p h j e", h=NH1), AX.XY, ALU.max).then_inc(s("gmax"), 1)
                    if not a.first(4):
                        dve.wait_ge(s("hm_mm"), n - 3)
                    dve.tensor_copy(hm[:, a.slot(4), 0:NH1], tile(hl, t)).then_inc(s("hm_hl"), 1)
                    dve.wait_ge(s("gmax"), n + 1)
                    dve.tensor_tensor(tile(hrmax, t), tile(hrmax, t), gmax[:, :], ALU.max).then_inc(s("hrmax"), 1)
                    dve.wait_ge(s("hrmax"), n + 1)
                    dve.tensor_tensor(zz[:, :], tile(hrmax, t), tile(hl, t), ALU.add).then_inc(s("zz"), 1)
                    dve.wait_ge(s("zz"), n + 1)
                    dve.scalar_tensor_tensor(hm[:, a.slot(4), NH1:2 * NH1], zz[:, :], SLOPE, zz[:, :],
                                             ALU.mult, ALU.max).then_inc(s("hm_ready"), 1)
                    dve.wait_ge(s("hm_ready"), n + 1)
                    if not a.first(2):
                        dve.wait_ge(s("mscale"), n - 1)
                    if not a.first(1):
                        dve.wait_ge(s("mrun"), n)
                    dve.tensor_tensor(mdiff[:, r, :], tile(mrun, t), hm[:, a.slot(4), NH1:2 * NH1],
                                      ALU.subtract).then_inc(s("mdiff"), 1)
                    dve.wait_ge(s("mdiff"), n + 1)
                    alone(dve)
                    dve.tensor_copy(tile(mrun, t), hm[:, a.slot(4), NH1:2 * NH1]).then_inc(s("mrun"), 1)
                b = st.back(3)
                if b.real():
                    n, r, r4 = b.n, b.slot(2), b.slot(4)
                    dve.wait_ge(s("hm_mm"), n + 1)
                    hme = ps[:, 3 + r, 0:2 * GJ * NH1].rearrange("p (c n) -> p c n", c=GJ)
                    dve.tensor_tensor(ez[:, :, :], hme[:, :, 0:NH1], row1_g[:, r4, :, NH1 * HE:ROW1],
                                      ALU.add).then_inc(s("ez"), 1)
                    dve.wait_ge(s("ez"), n + 1)
                    dve.scalar_tensor_tensor(el[:, :, :], ez[:, :, :], SLOPE, ez[:, :, :], ALU.mult,
                                             ALU.max).then_inc(s("el"), 1)
                    dve.wait_ge(s("el"), n + 1)
                    dve.tensor_tensor(es[:, :, :], el[:, :, :], hme[:, :, NH1:2 * NH1], ALU.subtract).then_inc(
                        s("es"), 1)
                    dve.wait_ge(s("es"), n + 1)
                    if not b.first(2):
                        dve.wait_ge(s("exp1"), n - 1)
                    dve.tensor_scalar(em[:, r, :, :], es[:, :, :], 0.0, None, ALU.min).then_inc(s("em"), 1)
                c = st.back(4)
                if c.real():
                    n, r, r4 = c.n, c.slot(2), c.slot(4)
                    dve.wait_ge(s("exp1"), n + 1)
                    if not c.first(2):
                        dve.wait_ge(s("agg1_ready"), n - 1)
                    dve.tensor_tensor(msg1[:, r, :, :].rearrange("p c (h d) -> p c h d", d=HE),
                                      row1_g[:, r4, :, 0:NH1 * HE].rearrange("p c (h d) -> p c h d", d=HE),
                                      ew[:, r, :, :].unsqueeze(3).to_broadcast([P, GJ, NH1, HE]),
                                      ALU.mult).then_inc(s("msg1_ready"), 1)
                    t = dve.value_load(gt_i[0:1, bass.ds(n, 1)], min_val=0, max_val=NT - 1)
                    dve.wait_ge(s("mscale"), n + 1)
                    if not c.first(1):
                        dve.wait_ge(s("acc1_done"), n)
                    at1 = tile(acc1, t)
                    dve.tensor_tensor(at1.rearrange("p (h d) -> p h d", d=HE), at1.rearrange("p (h d) -> p h d", d=HE),
                                      mscale[:, r4, :].unsqueeze(2).to_broadcast([P, NH1, HE]), ALU.mult).then_inc(
                                          s("acc1_scaled"), 1)
                    dve.wait_ge(s("acc1_scaled"), n + 1)
                    dve.wait_ge(s("agg1_ready"), n + 1)
                    dve.tensor_tensor(at1, at1, ps[:, 5 + r, 0:NH1 * HE], ALU.add).then_inc(s("acc1_done"), 1)

            run(dve, NG, 4, 4, layer1)
            dve.wait_ge(s("acc1_done"), NG)

            accv = acc1.rearrange("p t (h d) -> p t h d", d=HE)
            link(dve.tensor_scalar(den[:, :, :], accv[:, :, :, HD1], TINY, None, ALU.add))
            link(dve.reciprocal(den[:, :, :], den[:, :, :]))

            def finish(st):
                i, r = st.n, st.slot(2)
                if not st.first(2):
                    dve.wait_ge(s(f"out_stored{r}"), 16 * st.turn(2))
                ob = outb[:, r, :]
                dve.tensor_tensor(ob.rearrange("p (h d) -> p h d", d=HD1),
                                  tile(acc1, i).rearrange("p (h d) -> p h d", d=HE)[:, :, 0:HD1],
                                  tile(den, i).unsqueeze(2).to_broadcast([P, NH1, HD1]), ALU.mult).then_inc(
                                      s("out_div"), 1)
                dve.wait_ge(s("out_div"), i + 1)
                dve.tensor_tensor(ob, ob, tile(xs, i), ALU.add).then_inc(s("out_ready"), 1)

            run(dve, NT, 2, 0, lambda st: finish(st) if st.real() else None)

        @block.tensor
        def _(pe):
            def transposes(r, a, b, done):
                pe.transpose(tr[r][:, 0:P], a, ident[:, :])
                pe.transpose(tr[r][:, P:2 * P], b, ident[:, :]).then_inc(done, 1)

            pe.wait_ge(s("ident"), 3)
            pe.wait_ge(s("w_in"), 16 * 19)

            def node0(st):
                if st.real():
                    i, r = st.n, st.slot(2)
                    pe.wait_ge(s("xn_ready"), i + 1)
                    if not st.first(2):
                        pe.wait_ge(s("xnT"), i - 1)
                    xn = kvx_st[:, r, 2 * H:3 * H]
                    transposes(r, xn[:, 0:P], xn[:, P:2 * P], s("xn_tr"))
                st = st.back(1)
                if st.real():
                    i, r = st.n, st.slot(2)
                    pe.wait_ge(s("xnT"), i + 1)
                    if not st.first(2):
                        pe.wait_ge(s("q_ready"), i - 1)
                    for c in range(2):
                        pe.matmul(ps[:, 1 + r, :], xnT[:, r, c, :], wqkv[:, c, 0:2 * H], start=c == 0, stop=c == 1)
                    for c in range(2):
                        ins = pe.matmul(ps[:, 3 + r, 0:H], xnT[:, r, c, :], wqkv[:, c, 2 * H:3 * H],
                                        start=c == 0, stop=c == 1)
                    ins.then_inc(s("qkv_mm"), 1)

            run(pe, NT, 2, 1, node0)

            pe.wait_ge(s("cnt_ready"), 1)
            pe.wait_ge(s("const"), 3)
            pe.matmul(ps[:, 5, 0:NT], ones[:, :], cnt[:, :], start=True, stop=True)
            pe.matmul(ps[:, 5, NT:2 * NT], upper[:, :], cnt[:, :], start=True, stop=True).then_inc(s("cnt_mm"), 1)

            pe.wait_ge(s("q_ready"), NT)
            pe.wait_ge(s("pos_ready"), 1)

            def mlp8(k2, u):
                st = Step(k2, u, 8, QUADS)
                q = st
                if q.real():
                    n, r = q.n, q.slot(2)
                    par, qq = u // 4 % 2, u % 4
                    if qq == 0:
                        last = isinstance(k2, int) and n == QUADS - 4
                        pe.wait_ge(s(f"rbf_in{par}"), k2 * 16 + 16 + (16 if last else 0))
                    if not q.first(2):
                        pe.wait_ge(s("rbfT"), n - 1)
                    transposes(r, rbf[:, par, 4 * qq:4 * qq + 2, :].rearrange("p c n -> p (c n)"),
                               rbf[:, par, 4 * qq + 2:4 * qq + 4, :].rearrange("p c n -> p (c n)"), s("rbf_used"))
                mlp_rest(st)

            def mlp_rest(st):
                st1 = st.back(1)
                if st1.real():
                    n, r = st1.n, st1.slot(2)
                    pe.wait_ge(s("rbfT"), n + 1)
                    if not st1.first(2):
                        pe.wait_ge(s("hidT"), 2 * n - 2)
                    for m in range(2):
                        for half in range(2):
                            rows = slice(half * RBF, (half + 1) * RBF)
                            ins = pe.matmul(ps[:, 1 + 2 * r + half, m * 256:m * 256 + 256],
                                            w1_sb[rows, m * P:(m + 1) * P],
                                            rbfT[rows, r, :, :].rearrange("p c e -> p (c e)"),
                                            start=True, stop=True)
                    ins.then_inc(s("hid_mm"), 1)
                st2 = st.back(2)
                if st2.real():
                    n, r = st2.n, st2.slot(2)
                    pe.wait_ge(s("hidT"), 2 * n + 2)
                    for t in range(2):
                        if not st2.first(1):
                            pe.wait_ge(s("recA_ready"), 2 * n + t - 1)
                        for half in range(2):
                            for m in range(2):
                                ins = pe.matmul(ps[:, 5 + t, half * H:(half + 1) * H],
                                                hidT[:, r, m, half, t * P:(t + 1) * P], w2_sb[:, m, :],
                                                start=m == 0, stop=m == 1)
                        ins.then_inc(s("row_mm"), 1)

            run8(pe, QUADS, mlp8)

            pe.wait_ge(s("recA_ready"), 2 * QUADS)
            pe.wait_ge(s("hidT"), 2 * QUADS)
            pe.wait_ge(s("gt_ready"), 1)

            def one_hot_T(st, made, copied, done):
                n, r, r4 = st.n, st.slot(2), st.slot(4)
                pe.wait_ge(made, 2 * n + 2)
                if not st.first(2):
                    pe.wait_ge(copied, n - 1)
                transposes(r, oneh[:, r4, 0, :], oneh[:, r4, 1, :], done)

            def layer0(st):
                a = st.back(1)
                if a.real():
                    one_hot_T(a, s("oneh0"), s("onehT0"), s("oneh_tr0"))
                b = st.back(2)
                if b.real():
                    n, r = b.n, b.slot(2)
                    t = pe.value_load(gt_i[0:1, bass.ds(n, 1)], min_val=0, max_val=NT - 1)
                    pe.wait_ge(s("onehT0"), n + 1)
                    if not b.first(2):
                        pe.wait_ge(s("qk"), n - 1)
                    for j in range(GJ):
                        ins = pe.matmul(ps[:, 1 + r, j * H:(j + 1) * H], onehT[:, r, j, :],
                                        hq[:, bass.ds(t, 1), :].rearrange("p a n -> p (a n)"), start=True, stop=True)
                    ins.then_inc(s("qe_ready"), 1)
                c = st.back(4)
                if c.real():
                    n, r, r4 = c.n, c.slot(2), c.slot(4)
                    pe.wait_ge(s("rec_used"), n + 1)
                    if not c.first(2):
                        pe.wait_ge(s("acc0_done"), n - 1)
                    for j in range(GJ):
                        pe.matmul(ps[:, 3 + r, 0:H], oneh[:, r4, j, :], msgP[:, r, j, :], start=j == 0, stop=False)
                    pe.wait_ge(s("msgA_ready"), n + 1)
                    for j in range(GJ):
                        ins = pe.matmul(ps[:, 3 + r, 0:H], oneh[:, r4, j, :], msgA[:, r, j, :], start=False,
                                        stop=j == GJ - 1)
                    ins.then_inc(s("agg0_ready"), 1)

            run(pe, NG, 4, 4, layer0)

            pe.wait_ge(s("acc0_done"), NG)

            def proj(src_of, tr_ready, copied, tr_done, w, mm_done, bank_free):
                def body(st):
                    if st.real():
                        i, r = st.n, st.slot(2)
                        if tr_ready is not None:
                            pe.wait_ge(tr_ready, i + 1)
                        if not st.first(2):
                            pe.wait_ge(copied, i - 1)
                        v = src_of(st)
                        transposes(r, v[0], v[1], tr_done)
                    st = st.back(1)
                    if st.real():
                        i, r = st.n, st.slot(2)
                        pe.wait_ge(copied, i + 1)
                        if not st.first(2):
                            pe.wait_ge(bank_free, i - 1)
                        for c in range(2):
                            ins = pe.matmul(ps[:, 1 + r, 0:H], aT[:, r, c, :], w[:, c, :], start=c == 0, stop=c == 1)
                        ins.then_inc(mm_done, 1)
                return body

            def h2_of(st):
                return h2[:, st.slot(2), 0:P], h2[:, st.slot(2), P:2 * P]

            def transpose_acc(st):
                i = st.n
                return acc0[:, i, 0:P], acc0[:, i, P:2 * P]

            body = proj(transpose_acc, None, s("aT"), s("a_tr"), wo_sb, s("wo_mm"), s("x1"))
            for i in range(NT + 1):
                body(Step(i // 2, i % 2, 2, NT))
            pe.wait_ge(s("x1"), NT)
            run(pe, NT, 2, 1, proj(h2_of, s("h2"), s("h2T"), s("h2_tr"), W_sb, s("w_mm"), s("h2c")))

            pe.wait_ge(s("h2c"), NT)

            def layer1(st):
                a = st.back(1)
                if a.real():
                    one_hot_T(a, s("oneh1"), s("onehT1"), s("oneh_tr1"))
                b = st.back(2)
                if b.real():
                    n, r, r4 = b.n, b.slot(2), b.slot(4)
                    pe.wait_ge(s(f"row1_in{r4}"), 32 * b.turn(4) + 32)
                    pe.wait_ge(s("pen"), n + 1)
                    if not b.first(1):
                        pe.wait_ge(s("gmax"), n)
                    for j in range(GJ):
                        bank = ps[:, 1 + j, :]
                        for h in range(NH1):
                            hr = row1_g[:, r4, j, NH1 * HE + h:NH1 * HE + h + 1].to_broadcast([P, P])
                            pe.matmul(bank[:, h * P:(h + 1) * P], hr, ident[:, :], start=h == 0, stop=False)
                        ins = pe.matmul(bank.rearrange("p (h e) -> p h e", h=NH1), ident_b[:, :],
                                        pen[:, r, j * P:(j + 1) * P].unsqueeze(1).to_broadcast([P, NH1, P]),
                                        start=False, stop=True)
                    ins.then_inc(s("hr_mm"), 1)
                c = st.back(3)
                if c.real():
                    n, r, r4 = c.n, c.slot(2), c.slot(4)
                    pe.wait_ge(s("onehT1"), n + 1)
                    pe.wait_ge(s("hm_ready"), n + 1)
                    if not c.first(2):
                        pe.wait_ge(s("es"), n - 1)
                    for j in range(GJ):
                        ins = pe.matmul(ps[:, 3 + r, j * 8:j * 8 + 8], onehT[:, r, j, :],
                                        hm[:, r4, :], start=True, stop=True)
                    ins.then_inc(s("hm_mm"), 1)
                d = st.back(4)
                if d.real():
                    n, r, r4 = d.n, d.slot(2), d.slot(4)
                    pe.wait_ge(s("msg1_ready"), n + 1)
                    if not d.first(2):
                        pe.wait_ge(s("acc1_done"), n - 1)
                    for j in range(GJ):
                        ins = pe.matmul(ps[:, 5 + r, 0:NH1 * HE], oneh[:, r4, j, :], msg1[:, r, j, :],
                                        start=j == 0, stop=j == GJ - 1)
                    ins.then_inc(s("agg1_ready"), 1)

            run(pe, NG, 4, 4, layer1)


def run8(eng, total, body):
    for u in range(8):
        body(0, u)
    with eng.Fori(1, total // 8 - 1) as k:
        for u in range(8):
            body(k, u)
    for t in range(total // 8 * 8 - 8, total + 2):
        body(t // 8, t % 8)


_INS = ["x", "src", "dst", "edge_attr_64", "edge_weight", "L0_gnn_w1", "L0_gnn_b1", "L0_gnn_w2", "L0_gnn_b2",
        "L0_gnn_ln_w", "L0_gnn_ln_b", "L0_gnn_wq", "L0_gnn_bq", "L0_gnn_wk", "L0_gnn_bk", "L0_gnn_wv",
        "L0_gnn_bv", "L0_gnn_wo", "L0_gnn_bo", "L0_gnn_gate", "L1_gnn_W", "L1_gnn_a_l", "L1_gnn_a_r"]


def kernel(**inputs):
    import concourse.bacc as _bacc
    from concourse.bass_utils import run_bass_kernel_spmd as _run

    nc = _bacc.Bacc("TRN2", target_bir_lowering=False, num_devices=1)
    arrays, args = {}, []
    for name in _INS:
        a = np.ascontiguousarray(inputs[name])
        arrays[f"in_{name}"] = a
        args.append(nc.dram_tensor(f"in_{name}", a.shape, mybir.dt.from_np(a.dtype), kind="ExternalInput").ap())
    shape = inputs["x"].shape
    o = nc.dram_tensor("out_0", shape, F32, kind="ExternalOutput").ap()
    gnn_kernel(nc, *args, o)
    r = _run(nc, [arrays], core_ids=[0])
    return r.results[0]["out_0"]
```

```python
from contextlib import ExitStack

import numpy as np

import concourse.bass as bass
from concourse import mybir

ALU = mybir.AluOpType
ACT = mybir.ActivationFunctionType
AX = mybir.AxisListType
DVE = mybir.EngineType.DVE
PE = mybir.EngineType.PE
ACT_ENGINE = mybir.EngineType.Activation
F32 = mybir.dt.float32
BF16 = mybir.dt.bfloat16
I32 = mybir.dt.int32

P = 128
EPS = 1e-5
BIG = 2.0 ** 100
SLOPE = 0.2
TINY = 1e-16


class Step:

    def __init__(self, k, u, unroll, total):
        self.k, self.u, self.unroll, self.total = k, u, unroll, total

    def back(self, d):
        return Step(self.k, self.u - d, self.unroll, self.total)

    @property
    def n(self):
        return self.k * self.unroll + self.u

    def real(self):
        return not isinstance(self.k, int) or 0 <= self.n < self.total

    def first(self, count):
        return isinstance(self.k, int) and self.n < count

    def slot(self, ring):
        return self.u % ring

    def turn(self, ring):
        return self.k * (self.unroll // ring) + self.u // ring


def run(eng, total, unroll, lag, body, block=None):
    head = min(-(-(lag + max(unroll, 4)) // unroll), total // unroll)
    tail = total // unroll

    def turn(k, steps):
        if block is not None:
            block(k)
        for u in range(steps):
            body(Step(k, u, unroll, total))

    for k in range(head):
        turn(k, unroll)
    if tail > head:
        with eng.Fori(head, tail) as k:
            turn(k, unroll)
    for k in range(tail, -(-(total + lag) // unroll)):
        turn(k, min(unroll, total + lag - k * unroll))


def gnn_kernel(nc, x, src, dst, edge_attr_64, edge_weight, w1, b1, w2, b2, ln_w, ln_b, wq, bq, wk, bk,
               wv, bv, wo, bo, gate, W, a_l, a_r, out):
    N, H = x.shape
    E, RBF = edge_attr_64.shape
    NH0 = 8
    HD0 = H // NH0
    _, NH1, HD1 = a_l.shape
    HE = HD1 + 1
    NT = -(-N // P)
    NLAST = N - (NT - 1) * P
    COLS = 16
    NBLK = -(-E // (P * COLS))
    CC = NBLK * COLS
    REST = E - (NBLK - 1) * P * COLS
    RP, RR = REST // COLS, REST % COLS
    QUADS = CC // 4
    GJ = 2
    GE = GJ * P
    NG = (E + NT * (GE - 1)) // GE
    NG = -(-NG // 4) * 4
    NS = NG * GE
    MINUSED = -(-E // GE)
    REC = H + 4
    KVX = 3 * H
    HR = NH1 * HE
    HP = HR + NH1
    ROW1 = HP + 3 * NH1 // 2
    SKIP = 65536.0
    assert NS < SKIP and N < NT * P and QUADS % 4 == 0 and NT % 2 == 1

    rec_dram = nc.dram_tensor("sorted_edges", [NS + NT * GE, REC], F32, kind="Internal").ap()
    kvx_dram = nc.dram_tensor("node_kvx", [N, KVX], F32, kind="Internal").ap()
    row1_dram = nc.dram_tensor("node_row1", [N, ROW1], F32, kind="Internal").ap()

    with ExitStack() as ctx:
        def sb(name, shape, dt=F32):
            return ctx.enter_context(nc.sbuf_tensor(name, shape, dt))

        def sem(name):
            return ctx.enter_context(nc.semaphore(name))

        iota1 = sb("iota1", [P, P])
        iota_g = sb("iota_g", [P, NG])
        row_no = sb("row_no", [P, 1])
        ident = sb("ident", [P, P])
        ident_b = sb("ident_b", [P, P], BF16)
        upper = sb("upper", [P, P])
        ones = sb("ones", [P, P])
        w1_sb = sb("w1_sb", [P, H])
        w2_sb = sb("w2_sb", [P, 2, H])
        wqkv = sb("wqkv", [P, 2, KVX])
        wo_sb = sb("wo_sb", [P, 2, H])
        W_sb = sb("W_sb", [P, 2, H])
        b1_sb = sb("b1_sb", [P, 2])
        bqkv = sb("bqkv", [P, KVX])
        b2_bc = sb("b2_bc", [P, H])
        lnw_bc = sb("lnw_bc", [P, H])
        lnb_bc = sb("lnb_bc", [P, H])
        bo_bc = sb("bo_bc", [P, H])
        al_bc = sb("al_bc", [P, H])
        ar_bc = sb("ar_bc", [P, H])
        gate_bc = sb("gate_bc", [P, 1])

        xs = sb("xs", [P, NT, H])
        hq = sb("hq", [P, NT, H])
        mv = sb("mv", [P, NT, 2])
        rstd = sb("rstd", [P, NT])
        nmr = sb("nmr", [P, NT])
        st6 = sb("st6", [P, NT, 6])
        work = sb("work", [P, NT * CC + NT * CC // 2])
        oh = work[:, NT * CC:].bitcast(BF16).rearrange("p (b c) -> p b c", b=NT)
        rank = work[:, 0:NT * CC].rearrange("p (b c) -> p b c", b=NT)
        acc0 = work[:, 0:NT * H].rearrange("p (t n) -> p t n", t=NT)
        acc1 = work[:, NT * H:NT * (H + NH1 * HE)].rearrange("p (t n) -> p t n", t=NT)
        hl = sb("hl", [P, NT, NH1])
        hrmax = sb("hrmax", [P, NT, NH1])
        mrun = sb("mrun", [P, NT, NH1])
        den = sb("den", [P, NT, NH1])

        tile_f = sb("tile_f", [P, CC])
        pos_i = sb("pos_i", [P, CC], I32)
        cnt = sb("cnt", [P, NT])
        tot_i = sb("tot_i", [P, NT], I32)
        nch = sb("nch", [P, NT])
        gend = sb("gend", [P, NT])
        off = sb("off", [P, NT])
        zg_f = sb("zg_f", [P, 3 * NT])
        zg_i = sb("zg_i", [P, NT], I32)
        gt_f = sb("gt_f", [P, NG])
        gt_i = sb("gt_i", [P, 8 + NG + 8], I32)
        meta_s = sb("meta_s", [P, NG, GJ, 2])

        arena_n = 13056
        arena = sb("arena", [P, arena_n])
        at = [0]

        def carve(n):
            v = arena[:, at[0]:at[0] + n]
            at[0] += n
            assert at[0] <= arena_n, at[0]
            return v

        kvx_st = carve(4 * KVX).rearrange("p (s n) -> p s n", s=4)
        xnT = carve(2 * H).rearrange("p (s c e) -> p s c e", s=2, c=2)
        at[0] = 0
        rbf = carve(2 * COLS * RBF).rearrange("p (s c n) -> p s c n", s=2, c=COLS)
        rbfT = carve(2 * 2 * P).rearrange("p (s c e) -> p s c e", s=2, c=2)
        hidT = carve(2 * 4 * 2 * P).rearrange("p (s m h e) -> p s m h e", s=2, m=2, h=2)
        recA = carve(4 * 4 * REC).rearrange("p (s c n) -> p s c n", s=4, c=4)
        src_i = carve(CC).bitcast(I32)
        dst_i = carve(CC).bitcast(I32)
        cut_in = carve(CC)
        part_i = carve(CC).bitcast(I32)
        pos_f = carve(CC)
        zrows = carve(GJ * REC)
        meta_in = carve(4 * CC).rearrange("p (c n) -> p c n", n=4)
        at[0] = 0
        recB = carve(8 * GJ * REC).rearrange("p (s c n) -> p s c n", s=8, c=GJ)
        kvx_g = carve(4 * GJ * KVX).rearrange("p (s c n) -> p s c n", s=4, c=GJ)
        prod = carve(GJ * H).rearrange("p (c n) -> p c n", c=GJ)
        msgP = carve(2 * GJ * H).rearrange("p (s c n) -> p s c n", s=2, c=GJ)
        msgA = carve(2 * GJ * H).rearrange("p (s c n) -> p s c n", s=2, c=GJ)
        at[0] = 0
        aT = carve(2 * H).rearrange("p (s c e) -> p s c e", s=2, c=2)
        h2 = carve(2 * H).rearrange("p (s n) -> p s n", s=2)
        h2c = carve(2 * H).rearrange("p (s n) -> p s n", s=2)
        isnum = carve(H).bitcast(I32)
        row1 = carve(2 * HR).rearrange("p (s n) -> p s n", s=2)
        hrp = carve(NT * (ROW1 - HR)).rearrange("p (t n) -> p t n", t=NT)
        hr_rest = carve(2 * NT * NH1).rearrange("p (s t n) -> p s t n", s=2, t=NT)
        hal = carve(2 * H).rearrange("p (s n) -> p s n", s=2)
        har = carve(2 * H).rearrange("p (s n) -> p s n", s=2)
        row1_g = carve(8 * GJ * ROW1).rearrange("p (s c n) -> p s c n", s=8, c=GJ)
        msg1 = carve(2 * GJ * NH1 * HE).rearrange("p (s c n) -> p s c n", s=2, c=GJ)
        pen = carve(2 * GJ * P // 2).bitcast(BF16).rearrange("p (s n) -> p s n", s=2)
        onehT4 = carve(4 * GJ * P).rearrange("p (s c n) -> p s c n", s=4, c=GJ)
        outb = carve(2 * H).rearrange("p (s n) -> p s n", s=2)

        idxA = sb("idxA", [P, 4, 4], I32)
        idxB = sb("idxB", [P, 4, GJ], I32)
        srcB = sb("srcB", [P, 4, GJ])
        behind = NT * (H + NH1 * HE)
        oneh = work[:, behind:behind + 8 * GJ * P].rearrange("p (s c n) -> p s c n", s=8, c=GJ)
        behind += 8 * GJ * P
        onehT = work[:, behind:behind + 2 * GJ * P].rearrange("p (s c n) -> p s c n", s=2, c=GJ)
        away = sb("away", [P, 2, GJ, P])
        sc = sb("sc", [P, 2, GJ, NH0])
        smax = sb("smax", [P, GJ])
        pe_ = sb("pe_", [P, 2, GJ, NH0])
        psum_ = sb("psum_", [P, GJ])
        prec = sb("prec", [P, GJ])
        attn = sb("attn", [P, GJ, NH0])
        gmax = sb("gmax", [P, GJ, NH1])
        zz = sb("zz", [P, NH1])
        hm = sb("hm", [P, 4, 2 * NH1])
        mdiff = sb("mdiff", [P, 8, NH1])
        mscale = sb("mscale", [P, 8, NH1])
        ez = sb("ez", [P, GJ, NH1])
        el = sb("el", [P, GJ, NH1])
        es = sb("es", [P, GJ, NH1])
        em = sb("em", [P, 2, GJ, NH1])
        ew = sb("ew", [P, 2, GJ, NH1])

        ps = ctx.enter_context(nc.psum_tensor("ps", [P, 8, 512], F32))
        tr = (ps[:, 0, 0:2 * P], ps[:, 7, 0:2 * P])

        S = {}

        def s(name):
            if name not in S:
                S[name] = sem(name)
            return S[name]

        block = ctx.enter_context(nc.Block())

        def alone(eng):
            eng.sem_inc(s("waited_" + ("pool" if eng is nc.gpsimd else "dve")), 1)

        def tiles_of(eng, k, lag, count=8):
            _, values = nc.values_load_multi_w_load_instructions(
                gt_i[0:1, bass.ds(k * 8 + (8 - lag), count)], engines=(eng,), min_val=0, max_val=NT - 1,
                skip_runtime_bounds_check_because="the table's values are bounded by the minimum with NT - 1")
            return values

        def row_bc(v, n):
            return v.partition_broadcast(P)

        @block.sync
        def _(sp):
            def chunks(w):
                return w.rearrange("(c p) n -> p c n", p=P)

            sp.wait_ge(s("edge_fill"), 3)
            whole = (NBLK - 1) * P * COLS
            for t, v in ((src_i, src), (dst_i, dst), (cut_in, edge_weight)):
                tv = t[:, :].rearrange("p (b j) -> p b j", j=COLS)
                sp.dma_start(tv[:, 0:NBLK - 1, :],
                             v[0:whole].rearrange("(b p j) -> p b j", p=P, j=COLS)).then_inc(s("edges_in"), 16)
                sp.dma_start(tv[0:RP, NBLK - 1, :],
                             v[whole:whole + RP * COLS].rearrange("(p j) -> p j", j=COLS)).then_inc(s("edges_in"), 16)
                sp.dma_start(tv[RP:RP + 1, NBLK - 1, 0:RR],
                             v[whole + RP * COLS:E].rearrange("(p j) -> p j", p=1)).then_inc(s("edges_in"), 16)
            sp.wait_ge(s("x_fill"), 1)
            sp.dma_start(xs[:, 0:NT - 1, :], x[0:(NT - 1) * P, :].rearrange("(t p) n -> p t n", p=P)).then_inc(s("x_in"), 16)
            sp.dma_start(xs[0:NLAST, NT - 1, :], x[(NT - 1) * P:N, :]).then_inc(s("x_in"), 16)
            for i, w in enumerate((wk, wv, wq)):
                sp.dma_start(wqkv[:, :, i * H:(i + 1) * H], chunks(w)).then_inc(s("w_in"), 16)
            for i, v in enumerate((bk, bv, bq)):
                sp.dma_start(bqkv[:, i * H:(i + 1) * H], row_bc(v, H)).then_inc(s("w_in"), 16)
            for t, v in ((b2_bc, b2), (lnw_bc, ln_w), (lnb_bc, ln_b), (bo_bc, bo)):
                sp.dma_start(t[:, :], row_bc(v, H)).then_inc(s("w_in"), 16)
            for t, v in ((al_bc, a_l), (ar_bc, a_r)):
                sp.dma_start(t[:, :], row_bc(v.rearrange("a h d -> (a h d)"), H)).then_inc(s("w_in"), 16)
            for t, w in ((w2_sb, w2), (wo_sb, wo), (W_sb, W)):
                sp.dma_start(t[:, :, :], chunks(w)).then_inc(s("w_in"), 16)
            for half in range(2):
                sp.dma_start(w1_sb[half * RBF:(half + 1) * RBF, :], w1[:, :]).then_inc(s("w_in"), 16)
            with nc.allow_non_contiguous_dma(reason="256 values, once"):
                sp.dma_start(b1_sb[:, :], b1.rearrange("(c p) -> p c", p=P)).then_inc(s("w_in"), 16)
            sp.dma_start(gate_bc[:, :], row_bc(gate, 1)).then_inc(s("w_in"), 16)

            def store_kvx(st):
                i = st.n
                sp.wait_ge(s("xn_ready"), i + 1)
                sp.wait_ge(s("kv_ready"), i + 1)
                rows = NLAST if isinstance(i, int) and i == NT - 1 else P
                sp.dma_start(kvx_dram[bass.ds(i * P, rows), :], kvx_st[0:rows, st.slot(4), :]).then_inc(
                    s(f"kvx_out{st.slot(4)}"), 16)

            run(sp, NT, 4, 0, lambda st: store_kvx(st) if st.real() else None)

            sp.wait_ge(s("const"), 3)
            sp.dma_start(rec_dram[MINUSED * GE:NS, :].rearrange("(g p j) n -> p g (j n)", p=P, j=GJ),
                         zrows[:, :].unsqueeze(1).to_broadcast([P, NG - MINUSED, GJ * REC])).then_inc(s("zeroed"), 16)
            sp.wait_ge(s("zg_ready"), 1)

            def zero_group(st):
                g = sp.value_load(zg_i[0:1, bass.ds(st.n, 1)], min_val=0, max_val=NG + NT - 1)
                sp.dma_start(rec_dram[bass.ds(g * GE, GE), :].rearrange("(p j) n -> p (j n)", j=GJ),
                             zrows[:, :]).then_inc(s("zeroed"), 16)

            run(sp, NT, 1, 0, zero_group)

            for r in range(4):
                sp.wait_ge(s(f"kvx_out{r}"), 16 * ((NT - r + 3) // 4))
            sp.wait_ge(s("q_ready"), NT)

            def load_rbf(st):
                if not st.first(2):
                    sp.wait_ge(s("rbf_used"), 4 * st.n - 4)
                sp.dma_start(rbf[:, st.slot(2), :, :],
                             edge_attr_64[bass.ds(st.n * (P * COLS), P * COLS), :].rearrange(
                                 "(p j) n -> p j n", j=COLS)).then_inc(s(f"rbf_in{st.slot(2)}"), 16)

            run(sp, NBLK - 1, 2, 0, load_rbf)
            last = (NBLK - 1) % 2
            sp.wait_ge(s("rbf_used"), 4 * (NBLK - 1) - 4)
            sp.dma_start(rbf[0:RP, last, :, :],
                         edge_attr_64[whole:whole + RP * COLS, :].rearrange("(p j) n -> p j n", j=COLS)).then_inc(
                             s(f"rbf_in{last}"), 16)
            sp.dma_start(rbf[RP:RP + 1, last, 0:RR, :],
                         edge_attr_64[whole + RP * COLS:E, :].rearrange("(p j) n -> p j n", p=1)).then_inc(
                             s(f"rbf_in{last}"), 16)

            for r in range(4):
                sp.wait_ge(s(f"scattered{r}"), 16 * 4 * (QUADS // 4))

            def load_rec(st):
                if not st.first(8):
                    sp.wait_ge(s("msgP0_ready"), st.n - 7)
                    sp.wait_ge(s("msgP1_ready"), st.n - 7)
                sp.dma_start(recB[:, st.slot(8), :, :].rearrange("p c n -> p (c n)"),
                             rec_dram[bass.ds(st.n * GE, GE), :].rearrange("(p j) n -> p (j n)", j=GJ)).then_inc(
                                 s(f"rec_in{st.slot(8)}"), 16)

            run(sp, NG, 8, 0, load_rec)

            def store_row1(st):
                i = st.n
                sp.wait_ge(s("row1_ready"), i + 1)
                rows = NLAST if isinstance(i, int) and i == NT - 1 else P
                sp.dma_start(row1_dram[bass.ds(i * P, rows), 0:HR], row1[0:rows, st.slot(2), :]).then_inc(
                    s(f"row1_out{st.slot(2)}"), 16)

            run(sp, NT, 2, 0, lambda st: store_row1(st) if st.real() else None)
            sp.wait_ge(s("hr_parts"), 1)
            sp.dma_start(row1_dram[0:(NT - 1) * P, HR:ROW1].rearrange("(t p) n -> p t n", p=P),
                         hrp[:, 0:NT - 1, :]).then_inc(s("hr_out"), 16)
            sp.dma_start(row1_dram[(NT - 1) * P:N, HR:ROW1], hrp[0:NLAST, NT - 1, :]).then_inc(s("hr_out"), 16)

            def store_out(st):
                i = st.n
                sp.wait_ge(s("out_ready"), i + 1)
                rows = NLAST if isinstance(i, int) and i == NT - 1 else P
                sp.dma_start(out[bass.ds(i * P, rows), :], outb[0:rows, st.slot(2), :]).then_inc(
                    s(f"out_stored{st.slot(2)}"), 16)

            run(sp, NT, 2, 0, lambda st: store_out(st) if st.real() else None)
            sp.wait_ge(s("out_stored0"), 16 * (NT - NT // 2))
            sp.wait_ge(s("out_stored1"), 16 * (NT // 2))

        @block.gpsimd
        def _(pool):
            pool.memset(src_i[:, :], NT * P + P).then_inc(s("edge_fill"), 1)
            pool.memset(dst_i[:, :], 0).then_inc(s("edge_fill"), 1)
            pool.memset(cut_in[:, :], 0.0).then_inc(s("edge_fill"), 1)
            pool.memset(xs[:, NT - 1, :], 0.0).then_inc(s("x_fill"), 1)
            pool.iota(iota1[:, :], [[1, P]], base=1, channel_multiplier=0,
                      allow_small_or_imprecise_dtypes=True).then_inc(s("iota"), 1)
            pool.iota(row_no[:, :], [[0, 1]], base=1, channel_multiplier=1,
                      allow_small_or_imprecise_dtypes=True).then_inc(s("iota"), 1)
            pool.iota(iota_g[:, :], [[1, NG]], base=0, channel_multiplier=0,
                      allow_small_or_imprecise_dtypes=True).then_inc(s("iota"), 1)
            pool.memset(ones[:, :], 1.0).then_inc(s("const"), 1)
            pool.memset(gt_i[:, :], 0).then_inc(s("gt_fill"), 1)
            pool.memset(zrows[:, :], 0.0).then_inc(s("const"), 1)
            pool.memset(meta_in[:, :, :], 0.0).then_inc(s("const"), 1)

            pool.wait_ge(s("w_in"), 16 * 19)

            def residual(st):
                i = st.n
                pool.wait_ge(s("h_ready"), i + 1)
                alone(pool)
                pool.tensor_tensor(xs[:, bass.ds(i, 1), :].rearrange("p a n -> p (a n)"),
                                   xs[:, bass.ds(i, 1), :].rearrange("p a n -> p (a n)"),
                                   hq[:, bass.ds(i, 1), :].rearrange("p a n -> p (a n)"), ALU.add).then_inc(
                                       s("xh"), 1)
                pool.wait_ge(s("xh"), i + 1)
                alone(pool)
                pool.tensor_tensor(xs[:, bass.ds(i, 1), :].rearrange("p a n -> p (a n)"),
                                   xs[:, bass.ds(i, 1), :].rearrange("p a n -> p (a n)"),
                                   bo_bc[:, :], ALU.add).then_inc(s("xhb"), 1)

            run(pool, NT, 1, 0, residual)

            def affine(st):
                i = st.n
                xn = kvx_st[:, st.slot(4), 2 * H:3 * H]
                pool.wait_ge(s("xn_norm"), i + 1)
                alone(pool)
                pool.tensor_tensor(xn, xn, lnw_bc[:, :], ALU.mult).then_inc(s("xn_w"), 1)
                pool.wait_ge(s("xn_w"), i + 1)
                alone(pool)
                pool.tensor_tensor(xn, xn, lnb_bc[:, :], ALU.add).then_inc(s("xn_ready"), 1)

            run(pool, NT, 4, 0, lambda st: affine(st) if st.real() else None)

            pool.wait_ge(s("zeroed"), 16 * (NT + 1))

            def scatter(st):
                st = st.back(2)
                if not st.real():
                    return
                pool.wait_ge(s("idxA_ready"), st.n + 1)
                pool.wait_ge(s("rows_cut"), st.n + 1)
                alone(pool)
                for c in range(4):
                    pool.indirect_dma_start(
                        rec_dram[:, :], bass.IndirectOffsetOnAxis(ap=idxA[:, st.slot(4), c:c + 1], axis=0),
                        recA[:, st.slot(4), c, :], None, bounds_check=NS - 1, oob_is_err=False).then_inc(
                            s(f"scattered{st.slot(4)}"), 16)

            run(pool, QUADS, 4, 2, scatter)

            pool.memset(acc0[:, :, :], 0.0).then_inc(s("acc_zero"), 1)
            pool.memset(acc1[:, :, :], 0.0).then_inc(s("acc_zero"), 1)
            pool.memset(hrmax[:, :, :], -BIG).then_inc(s("acc_zero"), 1)
            pool.memset(mrun[:, :, :], -BIG).then_inc(s("acc_zero"), 1)

            for r in range(4):
                pool.wait_ge(s(f"kvx_out{r}"), 16 * ((NT - r + 3) // 4))
            for r in range(4):
                pool.wait_ge(s(f"scattered{r}"), 16 * 4 * (QUADS // 4))

            def gather0(st):
                b = st.back(4)
                if b.real():
                    pool.wait_ge(s(f"kvx_in{b.slot(4)}"), 32 * b.turn(4) + 32)
                    if not b.first(2):
                        pool.wait_ge(s("agg0_ready"), b.n - 1)
                    alone(pool)
                    pool.tensor_tensor(msgP[:, b.slot(2), 1, :], recB[:, b.slot(8), 1, 0:H],
                                       kvx_g[:, b.slot(4), 1, 2 * H:3 * H], ALU.mult).then_inc(s("msgP1_ready"), 1)
                if not st.real():
                    return
                pool.wait_ge(s("idxB_ready"), st.n + 1)
                if not st.first(4):
                    pool.wait_ge(s("msgP0_ready"), st.n - 3)
                    pool.wait_ge(s("msgP1_ready"), st.n - 3)
                    pool.wait_ge(s("msgA_ready"), st.n - 3)
                alone(pool)
                for j in range(GJ):
                    pool.indirect_dma_start(
                        kvx_g[:, st.slot(4), j, :], None, kvx_dram[:, :],
                        bass.IndirectOffsetOnAxis(ap=idxB[:, st.slot(4), j:j + 1], axis=0)).then_inc(
                            s(f"kvx_in{st.slot(4)}"), 16)

            run(pool, NG, 8, 4, gather0)

            pool.wait_ge(s("acc0_done"), NG)
            for r in range(2):
                v = row1[:, r, 0:NH1 * HE]
                pool.memset(v, 0.0).then_inc(s("row1_zero"), 1)
                pool.wait_ge(s("row1_zero"), r + 1)
                pool.memset(v.rearrange("p (h d) -> p h d", d=HE)[:, :, HD1:HE], 1.0).then_inc(s("row1_one"), 1)

            def products(st):
                i, r = st.n, st.slot(2)
                if not st.first(2):
                    pool.wait_ge(s("hr_ready"), i - 1)
                pool.wait_ge(s("row1_ready"), i + 1)
                heads = row1[:, r, 0:NH1 * HE].rearrange("p (h d) -> p h d", d=HE)[:, :, 0:HD1]
                alone(pool)
                for t, w in ((hal, al_bc), (har, ar_bc)):
                    pool.tensor_tensor(t[:, r, :].rearrange("p (h d) -> p h d", d=HD1), heads,
                                       w[:, :].rearrange("p (h d) -> p h d", d=HD1), ALU.mult).then_inc(
                                           s("ha_ready"), 1)
                if isinstance(i, int) and i + 2 >= NT:
                    return
                pool.wait_ge(s(f"row1_out{r}"), 16 * st.turn(2) + 16)
                pool.wait_ge(s("ha_ready"), 2 * i + 2)
                alone(pool)
                pool.memset(heads, 0.0).then_inc(s("row1_zero"), 1)

            run(pool, NT, 2, 0, lambda st: products(st) if st.real() else None)

            pool.wait_ge(s("row1_out0"), 16 * (NT - NT // 2))
            pool.wait_ge(s("row1_out1"), 16 * (NT // 2))
            pool.wait_ge(s("hr_out"), 32)

            def gather1(st):
                c = st.back(7)
                if c.real():
                    pool.wait_ge(s("exp1"), c.n + 1)
                    if not c.first(2):
                        pool.wait_ge(s("agg1_ready"), c.n - 1)
                    alone(pool)
                    pool.tensor_tensor(msg1[:, c.slot(2), 1, :].rearrange("p (h d) -> p h d", d=HE),
                                       row1_g[:, c.slot(8), 1, 0:HR].rearrange("p (h d) -> p h d", d=HE),
                                       ew[:, c.slot(2), 1, :].unsqueeze(2).to_broadcast([P, NH1, HE]),
                                       ALU.mult).then_inc(s("msg1b_ready"), 1)
                if not st.real():
                    return
                pool.wait_ge(s("idxC_ready"), st.n + 1)
                if not st.first(8):
                    pool.wait_ge(s("msg1_ready"), st.n - 7)
                    pool.wait_ge(s("msg1b_ready"), st.n - 7)
                alone(pool)
                for j in range(GJ):
                    pool.indirect_dma_start(
                        row1_g[:, st.slot(8), j, :], None, row1_dram[:, :],
                        bass.IndirectOffsetOnAxis(ap=idxB[:, st.slot(4), j:j + 1], axis=0)).then_inc(
                            s(f"row1_in{st.slot(8)}"), 16)

            run(pool, NG, 8, 7, gather1)

        @block.scalar
        def _(act):
            act.wait_ge(s("var1"), 1)
            act.activation(rstd[:, :], rstd[:, :], ACT.Sqrt).then_inc(s("std1"), 1)
            act.wait_ge(s("nmr1"), 1)

            def relu_h(st):
                i = st.n
                act.activation(hq[:, bass.ds(i, 1), :].rearrange("p a n -> p (a n)"),
                               xs[:, bass.ds(i, 1), :].rearrange("p a n -> p (a n)"), ACT.Relu,
                               bias=nmr[:, bass.ds(i, 1)], scale=rstd[:, bass.ds(i, 1)]).then_inc(s("h_ready"), 1)

            run(act, NT, 1, 0, relu_h)
            act.wait_ge(s("var2"), 1)
            act.activation(rstd[:, :], rstd[:, :], ACT.Sqrt).then_inc(s("std2"), 1)

            def copy_xnT(st):
                act.wait_ge(s("xn_tr"), st.n + 1)
                if not st.first(2):
                    act.wait_ge(s("qkv_mm"), st.n - 1)
                act.copy(xnT[:, st.slot(2), :, :], tr[st.slot(2)].rearrange(
                    "p (c e) -> p c e", c=2)).then_inc(s("xnT"), 1)

            run(act, NT, 2, 0, lambda st: copy_xnT(st) if st.real() else None)

            act.wait_ge(s("pos_ready"), 1)

            def mlp(st):
                if st.real():
                    if not st.first(4):
                        act.wait_ge(s(f"scattered{st.slot(4)}"), 64 * st.turn(4))
                    act.copy(idxA[:, st.slot(4), :], pos_i[:, bass.ds(st.n * 4, 4)]).then_inc(s("idxA_ready"), 1)
                c = st.back(2)
                st = st.back(1)
                if st.real():
                    act.wait_ge(s("hid_mm"), st.n + 1)
                    if not st.first(2):
                        act.wait_ge(s("row_mm"), 2 * st.n - 2)
                    for m in range(2):
                        bank = 1 + 2 * st.slot(2)
                        act.activation(hidT[:, st.slot(2), m, :, :], ps[:, bank:bank + 2, m * 256:m * 256 + 256],
                                       ACT.Silu, bias=b1_sb[:, m:m + 1]).then_inc(s("hidT"), 1)
                if c.real():
                    act.wait_ge(s("metaA_ready"), c.n + 1)
                    for t in range(2):
                        act.wait_ge(s("recA_ready"), 2 * c.n + t + 1)
                        for i in (2 * t, 2 * t + 1):
                            row = recA[:, c.slot(4), i, :]
                            ins = act.activation(row[:, 0:H], row[:, 0:H], ACT.Copy, scale=row[:, H:H + 1])
                    ins.then_inc(s("rows_cut"), 1)

            run(act, QUADS, 4, 2, mlp)

            def one_hot_away(st, src_ready, away_ready):
                act.wait_ge(src_ready, st.n + 1)
                for j in range(GJ):
                    act.activation(away[:, st.slot(2), j, :], iota1[:, :], ACT.Abs, bias=srcB[:, st.slot(4), j:j + 1],
                                   scale=-1.0).then_inc(away_ready, 1)

            def one_hot_near(st, away_ready, made, used):
                act.wait_ge(away_ready, 2 * st.n + 2)
                if not st.first(8):
                    act.wait_ge(used, st.n - 7)
                act.activation(oneh[:, st.slot(8), :, :], away[:, st.slot(2), :, :], ACT.Relu, bias=1.0,
                               scale=-1.0).then_inc(made, 1)

            act.wait_ge(s("acc_zero"), 4)

            def layer0(st):
                e = st.back(4)
                if e.real():
                    act.wait_ge(s("sc_ready"), e.n + 1)
                    if not e.first(2):
                        act.wait_ge(s("attn"), e.n - 1)
                    r = e.slot(2)
                    act.activation(pe_[:, r, :, :], sc[:, r, :, :], ACT.Exp, scale=float(HD0) ** -0.5).then_inc(
                        s("exp0"), 1)
                if st.real():
                    r, r8 = st.slot(4), st.slot(8)
                    act.wait_ge(s(f"rec_in{r8}"), 16 * st.turn(8) + 16)
                    if not st.first(4):
                        act.wait_ge(s(f"kvx_in{r}"), 32 * st.turn(4))
                    act.copy(idxB[:, r, :], recB[:, r8, :, H + 2]).then_inc(s("idxB_ready"), 1)
                    act.copy(srcB[:, r, :], recB[:, r8, :, H + 1]).then_inc(s("srcB_ready"), 1)
                    act.copy(meta_s[:, bass.ds(st.n, 1), :, :].rearrange("p a c n -> p (a c) n"),
                             recB[:, r8, :, H + 1:H + 3]).then_inc(s("meta_s"), 1)
                    one_hot_away(st, s("srcB_ready"), s("away0"))
                    one_hot_near(st, s("away0"), s("oneh0"), s("agg0_ready"))
                c = st.back(1)
                if c.real():
                    act.wait_ge(s("oneh_tr0"), c.n + 1)
                    if not c.first(2):
                        act.wait_ge(s("qe_ready"), c.n - 1)
                    r = c.slot(2)
                    act.copy(onehT[:, r, :, :], tr[r].rearrange("p (c e) -> p c e", c=GJ)).then_inc(s("onehT0"), 1)

            run(act, NG, 8, 7, layer0)

            def copy_aT(st):
                act.wait_ge(s("a_tr"), st.n + 1)
                if not st.first(2):
                    act.wait_ge(s("wo_mm"), st.n - 1)
                act.copy(aT[:, st.slot(2), :, :], tr[st.slot(2)].rearrange(
                    "p (c e) -> p c e", c=2)).then_inc(s("aT"), 1)

            run(act, NT, 2, 0, lambda st: copy_aT(st) if st.real() else None)
            act.wait_ge(s("var3"), 1)
            act.activation(rstd[:, :], rstd[:, :], ACT.Sqrt).then_inc(s("std3"), 1)
            act.wait_ge(s("nmr3"), 1)

            def node1(st):
                if st.real():
                    i, r = st.n, st.slot(2)
                    if not st.first(2):
                        act.wait_ge(s("h2_tr"), i - 1)
                    act.activation(h2[:, r, :], xs[:, bass.ds(i, 1), :].rearrange("p a n -> p (a n)"), ACT.Relu,
                                   bias=nmr[:, bass.ds(i, 1)], scale=rstd[:, bass.ds(i, 1)]).then_inc(s("h2"), 1)
                    act.wait_ge(s("h2_tr"), i + 1)
                    if not st.first(2):
                        act.wait_ge(s("w_mm"), i - 1)
                    act.copy(aT[:, r, :, :], tr[r].rearrange(
                        "p (c e) -> p c e", c=2)).then_inc(s("h2T"), 1)
                st = st.back(1)
                if st.real():
                    i, r = st.n, st.slot(2)
                    act.wait_ge(s("w_mm"), i + 1)
                    if not st.first(2):
                        act.wait_ge(s("row1_ready"), i - 1)
                    act.copy(h2c[:, r, :], ps[:, 1 + r, 0:H]).then_inc(s("h2c"), 1)

            run(act, NT, 2, 1, node1)

            act.wait_ge(s("meta_s"), NG)

            act_tiles = {}

            def act_tiles1(k):
                act_tiles[8] = tiles_of(ACT_ENGINE, k, 8)

            def layer1(st):
                if st.real():
                    r = st.slot(4)
                    if not st.first(4):
                        old = st.back(4)
                        act.wait_ge(s(f"row1_in{old.slot(8)}"), 32 * old.turn(8) + 32)
                    m = meta_s[:, bass.ds(st.n, 1), :, :].rearrange("p a c n -> p (a c) n")
                    act.copy(idxB[:, r, :], m[:, :, 1]).then_inc(s("idxC_ready"), 1)
                    act.copy(srcB[:, r, :], m[:, :, 0]).then_inc(s("srcC_ready"), 1)
                e = st.back(6)
                if e.real():
                    act.wait_ge(s("em"), e.n + 1)
                    if not e.first(2):
                        act.wait_ge(s("msg1_ready"), e.n - 1)
                        act.wait_ge(s("msg1b_ready"), e.n - 1)
                    r = e.slot(2)
                    act.activation(ew[:, r, :, :], em[:, r, :, :], ACT.Exp).then_inc(s("exp1"), 1)
                if st.real():
                    one_hot_away(st, s("srcC_ready"), s("away1"))
                d = st.back(8)
                if d.real():
                    act.wait_ge(s("mscale"), d.n + 1)
                    if not d.first(1):
                        act.wait_ge(s("acc1_done"), d.n)
                    for h in range(NH1):
                        v = acc1[:, bass.ds(act_tiles[8][st.u], 1), h * HE:(h + 1) * HE].rearrange("p a n -> p (a n)")
                        ins = act.activation(v, v, ACT.Copy, scale=mscale[:, d.slot(8), h:h + 1])
                    ins.then_inc(s("acc1_scaled"), 1)
                if st.real():
                    one_hot_near(st, s("away1"), s("oneh1"), s("agg1_ready"))
                e = st.back(6)
                if e.real():
                    act.wait_ge(s("mdiff"), e.n + 1)
                    if not e.first(8):
                        act.wait_ge(s("acc1_scaled"), e.n - 7)
                    act.activation(mscale[:, e.slot(8), :], mdiff[:, e.slot(8), :], ACT.Exp).then_inc(
                        s("mscale"), 1)
                c = st.back(1)
                if c.real():
                    r = c.slot(2)
                    act.wait_ge(s("oneh_tr1"), c.n + 1)
                    if not c.first(2):
                        act.wait_ge(s("hr_mm"), 2 * c.n - 2)
                    act.activation(pen[:, r, :], tr[r], ACT.Copy, bias=-BIG, scale=BIG).then_inc(s("pen"), 1)
                    if not c.first(4):
                        act.wait_ge(s("hm_mm"), c.n - 3)
                    act.copy(onehT4[:, c.slot(4), :, :], tr[r].rearrange("p (c e) -> p c e", c=GJ)).then_inc(
                        s("onehT1"), 1)

            run(act, NG, 8, 8, layer1, act_tiles1)

        @block.vector
        def _(dve):
            made = [0]

            def link(ins):
                made[0] += 1
                ins.then_inc(s("chain"), 1)
                dve.wait_ge(s("chain"), made[0])

            dve.wait_ge(s("iota"), 3)
            dve.tensor_scalar(ident[:, :], iota1[:, :], row_no[:, 0:1], None, ALU.is_equal).then_inc(s("ident"), 1)
            dve.tensor_scalar(ident_b[:, :], iota1[:, :], row_no[:, 0:1], None, ALU.is_equal).then_inc(s("ident"), 1)
            dve.tensor_scalar(upper[:, :], iota1[:, :], row_no[:, 0:1], None, ALU.is_gt).then_inc(s("ident"), 1)

            def tile(t, i):
                return t[:, bass.ds(i, 1), :].rearrange("p a n -> p (a n)")

            def stats(name, source, ready):
                def one(st):
                    if ready is not None:
                        dve.wait_ge(ready, st.n + 1)
                    dve.bn_stats(tile(st6, st.n), tile(source, st.n)).then_inc(s(name + "_st"), 1)

                run(dve, NT, 1, 0, one)
                dve.wait_ge(s(name + "_st"), NT)
                for i in range(NT):
                    ins = dve.bn_aggr(mv[:, i, :], st6[:, i, :])
                link(ins)

            def rstds(n):
                dve.tensor_scalar(rstd[:, :], mv[:, :, 1], EPS, None, ALU.add).then_inc(s(f"var{n}"), 1)
                dve.wait_ge(s(f"std{n}"), 1)
                link(dve.reciprocal(rstd[:, :], rstd[:, :]))
                dve.scalar_tensor_tensor(nmr[:, :], mv[:, :, 0], -1.0, rstd[:, :], ALU.mult, ALU.mult).then_inc(
                    s(f"nmr{n}"), 1)
                dve.wait_ge(s(f"nmr{n}"), 1)

            dve.wait_ge(s("x_in"), 32)
            stats("x", xs, None)
            rstds(1)
            stats("h", hq, s("h_ready"))
            dve.wait_ge(s("h_ready"), NT)
            rstds(2)
            dve.wait_ge(s("w_in"), 16 * 19)
            dve.wait_ge(s("xh"), NT)

            def node0(st):
                if st.real():
                    i, r = st.n, st.slot(4)
                    if not st.first(4):
                        dve.wait_ge(s(f"kvx_out{r}"), 16 * st.turn(4))
                    dve.tensor_scalar(kvx_st[:, r, 2 * H:3 * H], tile(hq, i), rstd[:, bass.ds(i, 1)],
                                      nmr[:, bass.ds(i, 1)], ALU.mult, ALU.add).then_inc(s("xn_norm"), 1)
                st = st.back(3)
                if st.real():
                    i, r = st.n, st.slot(2)
                    dve.wait_ge(s("qkv_mm"), i + 1)
                    dve.tensor_tensor(kvx_st[:, st.slot(4), 0:2 * H], ps[:, 1 + r, :], bqkv[:, 0:2 * H],
                                      ALU.add).then_inc(s("kv_ready"), 1)
                    dve.tensor_tensor(tile(hq, i), ps[:, 3 + r, 0:H], bqkv[:, 2 * H:3 * H], ALU.add).then_inc(
                        s("q_ready"), 1)

            run(dve, NT, 4, 3, node0)

            dve.wait_ge(s("edges_in"), 16 * 9)
            dve.wait_ge(s("const"), 3)
            link(dve.tensor_single_scalar(part_i[:, :], src_i[:, :], 7, ALU.arith_shift_right))
            link(dve.tensor_copy(tile_f[:, :], part_i[:, :]))
            link(dve.tensor_single_scalar(part_i[:, :], src_i[:, :], P - 1, ALU.bitwise_and))
            dve.tensor_scalar(meta_in[:, :, 1], part_i[:, :], 1.0, None, ALU.add).then_inc(s("meta_in"), 1)
            dve.tensor_copy(meta_in[:, :, 2], dst_i[:, :]).then_inc(s("meta_in"), 1)
            dve.tensor_copy(meta_in[:, :, 0], cut_in[:, :]).then_inc(s("meta_in"), 1)
            for b in range(NT):
                ins = dve.tensor_scalar(oh[:, b, :], tile_f[:, :], float(b), None, ALU.is_equal)
            link(ins)
            link(dve.reduce_sum(cnt[:, :], oh[:, :, :], axis=AX.X))
            dve.sem_inc(s("cnt_ready"), 1)
            dve.wait_ge(s("cnt_mm"), 1)
            tot, pre = ps[:, 5, 0:NT], ps[:, 5, NT:2 * NT]
            link(dve.tensor_scalar(tot_i[:, :], tot, float(GE - 1), None, ALU.add))
            link(dve.tensor_single_scalar(tot_i[:, :], tot_i[:, :], 8, ALU.arith_shift_right))
            link(dve.tensor_copy(nch[:, :], tot_i[:, :]))
            link(dve.tensor_tensor_scan(gend[:, :], nch[:, :], nch[:, :], 0.0, ALU.add, ALU.max))
            link(dve.tensor_tensor(off[:, :], gend[:, :], nch[:, :], ALU.subtract))
            link(dve.scalar_tensor_tensor(off[:, :], off[:, :], float(GE), pre, ALU.mult, ALU.add))
            spare, keep = zg_f[:, NT:2 * NT], zg_f[:, 2 * NT:3 * NT]
            dve.tensor_scalar(spare, iota_g[:, 0:NT], float(NG), None, ALU.add)
            dve.tensor_scalar(keep, nch[:, :], 1.0, None, ALU.min)
            link(dve.tensor_scalar(zg_f[:, 0:NT], gend[:, :], -1.0, None, ALU.add))
            link(dve.scalar_tensor_tensor(keep, zg_f[:, 0:NT], float(MINUSED), keep, ALU.is_lt, ALU.mult))
            link(dve.tensor_tensor(zg_f[:, 0:NT], zg_f[:, 0:NT], spare, ALU.subtract))
            link(dve.tensor_tensor(zg_f[:, 0:NT], zg_f[:, 0:NT], keep, ALU.mult))
            dve.tensor_tensor(zg_i[:, :], zg_f[:, 0:NT], spare, ALU.add).then_inc(s("zg_ready"), 1)
            cmp = rank[:, :, 0:NG]
            for b in range(NT):
                ins = dve.tensor_scalar(cmp[:, b, :], iota_g[:, :], gend[:, b:b + 1], None, ALU.is_ge)
            link(ins)
            link(dve.reduce_sum(gt_f[:, :], cmp.rearrange("p b g -> p g b"), axis=AX.X))
            dve.wait_ge(s("gt_fill"), 1)
            dve.tensor_scalar(gt_i[:, 8:8 + NG], gt_f[:, :], float(NT - 1), None, ALU.min).then_inc(s("gt_ready"), 1)
            dve.wait_ge(s("gt_ready"), 1)
            for b in range(NT):
                ins = dve.tensor_tensor_scan(rank[:, b, :], oh[:, b, :], oh[:, b, :], off[:, b:b + 1],
                                             ALU.add, ALU.max)
            link(ins)
            link(dve.tensor_tensor(rank[:, :, :], rank[:, :, :], oh[:, :, :], ALU.mult))
            link(dve.reduce_sum(pos_f[:, :], rank.rearrange("p b c -> p c b"), axis=AX.X))
            link(dve.tensor_scalar(tile_f[:, :], tile_f[:, :], float(NT) - 0.5, SKIP, ALU.is_gt, ALU.mult))
            dve.scalar_tensor_tensor(pos_i[:, :], pos_f[:, :], -1.0, tile_f[:, :], ALU.add, ALU.add).then_inc(
                s("pos_ready"), 1)

            def mlp(st):
                if st.real():
                    r = st.slot(2)
                    dve.wait_ge(s("rbf_used"), st.n + 1)
                    if not st.first(2):
                        dve.wait_ge(s("hid_mm"), st.n - 1)
                    dve.tensor_copy(rbfT[:, r, :, :], tr[r].rearrange(
                        "p (c e) -> p c e", c=2)).then_inc(s("rbfT"), 1)
                st = st.back(2)
                if st.real():
                    r = st.slot(4)
                    if not st.first(4):
                        dve.wait_ge(s(f"scattered{r}"), 64 * st.turn(4))
                    dve.tensor_copy(recA[:, r, :, H:REC], meta_in[:, bass.ds(st.n * 4, 4), :]).then_inc(
                        s("metaA_ready"), 1)
                    for t in range(2):
                        dve.wait_ge(s("row_mm"), 2 * st.n + t + 1)
                        dve.tensor_tensor(recA[:, r, 2 * t:2 * t + 2, 0:H],
                                          ps[:, 5 + t, :].rearrange("p (c n) -> p c n", c=2),
                                          b2_bc[:, :].unsqueeze(1).to_broadcast([P, 2, H]),
                                          ALU.add).then_inc(s("recA_ready"), 1)

            dve.wait_ge(s("meta_in"), 3)
            run(dve, QUADS, 4, 2, mlp)

            dve.wait_ge(s("acc_zero"), 4)

            def heads(v):
                return v.rearrange("p c (h d) -> p c h d", d=HD0)

            tiles = {}

            def tiles0(k):
                tiles[6] = tiles_of(DVE, k, 6)

            def layer0(st):
                a, b, c = st.back(3), st.back(4), st.back(6)
                if a.real():
                    ra, na = a.slot(2), a.n
                    dve.wait_ge(s("qe_ready"), na + 1)
                    dve.wait_ge(s(f"kvx_in{a.slot(4)}"), 32 * a.turn(4) + 32)
                    dve.tensor_tensor(prod[:, :, :], ps[:, 1 + ra, :].rearrange("p (c n) -> p c n", c=GJ),
                                      kvx_g[:, a.slot(4), :, 0:H], ALU.mult).then_inc(s("qk"), 1)
                if b.real():
                    rb, nb = b.slot(2), b.n
                    v_b = kvx_g[:, b.slot(4), :, H:2 * H]
                    if not b.first(2):
                        dve.wait_ge(s("agg0_ready"), nb - 1)
                    dve.tensor_tensor(msgP[:, rb, 0, :], recB[:, b.slot(8), 0, 0:H], kvx_g[:, b.slot(4), 0, 2 * H:3 * H],
                                      ALU.mult).then_inc(s("msgP0_ready"), 1)
                    dve.wait_ge(s("exp0"), nb + 1)
                    dve.reduce_sum(psum_[:, :], pe_[:, rb, :, :], axis=AX.X).then_inc(s("psum"), 1)
                if a.real():
                    dve.wait_ge(s("qk"), na + 1)
                    dve.reduce_sum(sc[:, ra, :, :], heads(prod), axis=AX.X).then_inc(s("qk_sum"), 1)
                if b.real():
                    dve.wait_ge(s("psum"), nb + 1)
                    dve.reciprocal(prec[:, :], psum_[:, :]).then_inc(s("prec"), 1)
                if c.real():
                    acc = tile(acc0, tiles[6][st.u])
                    if not b.real():
                        dve.wait_ge(s("acc0_done"), c.n)
                    dve.wait_ge(s("agg0_ready"), c.n + 1)
                    dve.tensor_tensor(acc, acc, ps[:, 3 + c.slot(2), 0:H], ALU.add).then_inc(s("acc0_done"), 1)
                if a.real():
                    dve.wait_ge(s(f"rec_in{a.slot(8)}"), 16 * a.turn(8) + 16)
                    dve.wait_ge(s("qk_sum"), na + 1)
                    dve.tensor_tensor(sc[:, ra, :, :], sc[:, ra, :, :],
                                      recB[:, a.slot(8), :, H:H + 1].to_broadcast([P, GJ, NH0]),
                                      ALU.mult).then_inc(s("qk_cut"), 1)
                if b.real():
                    dve.wait_ge(s("prec"), nb + 1)
                    dve.scalar_tensor_tensor(attn[:, :, :], pe_[:, rb, :, :], gate_bc[:, 0:1],
                                             prec[:, :].unsqueeze(2).to_broadcast([P, GJ, NH0]),
                                             ALU.mult, ALU.mult).then_inc(s("attn"), 1)
                if a.real():
                    dve.wait_ge(s("qk_cut"), na + 1)
                    dve.reduce_max(smax[:, :], sc[:, ra, :, :], axis=AX.X).then_inc(s("qk_max"), 1)
                if b.real():
                    dve.wait_ge(s("attn"), nb + 1)
                    dve.tensor_tensor(heads(msgA[:, rb, :, :]), heads(v_b),
                                      attn[:, :, :].unsqueeze(3).to_broadcast([P, GJ, NH0, HD0]),
                                      ALU.mult).then_inc(s("msgA_ready"), 1)
                if a.real():
                    dve.wait_ge(s("qk_max"), na + 1)
                    dve.tensor_tensor(sc[:, ra, :, :], sc[:, ra, :, :],
                                      smax[:, :].unsqueeze(2).to_broadcast([P, GJ, NH0]), ALU.subtract).then_inc(
                                          s("sc_ready"), 1)

            run(dve, NG, 8, 7, layer0, tiles0)

            def node1(st):
                i = st.n
                dve.wait_ge(s("wo_mm"), i + 1)
                dve.tensor_tensor(tile(xs, i), tile(xs, i), ps[:, 1 + st.slot(2), 0:H], ALU.add).then_inc(s("x1"), 1)

            run(dve, NT, 2, 0, lambda st: node1(st) if st.real() else None)
            stats("x1", xs, s("x1"))
            rstds(3)

            def node2(st):
                i, r = st.n, st.slot(2)
                dve.wait_ge(s("h2c"), i + 1)
                dve.tensor_tensor(isnum, h2c[:, r, :], h2c[:, r, :], ALU.is_equal).then_inc(s("isnum"), 1)
                dve.wait_ge(s("isnum"), i + 1)
                dve.wait_ge(s("row1_zero"), i + 1)
                dve.wait_ge(s("row1_one"), 2)
                alone(dve)
                dve.copy_predicated(row1[:, r, 0:NH1 * HE].rearrange("p (h d) -> p h d", d=HE)[:, :, 0:HD1],
                                    isnum.rearrange("p (h d) -> p h d", d=HD1),
                                    h2c[:, r, :].rearrange("p (h d) -> p h d", d=HD1)).then_inc(s("row1_ready"), 1)
                dve.wait_ge(s("ha_ready"), 2 * i + 2)
                dve.reduce_sum(tile(hl, i), hal[:, r, :].rearrange("p (h d) -> p h d", d=HD1), axis=AX.X).then_inc(
                    s("hl_ready"), 1)
                dve.reduce_sum(hrp[:, bass.ds(i, 1), 0:NH1].rearrange("p a n -> p (a n)"), har[:, r, :].rearrange("p (h d) -> p h d", d=HD1),
                               axis=AX.X).then_inc(s("hr_ready"), 1)

            run(dve, NT, 2, 0, lambda st: node2(st) if st.real() else None)
            dve.wait_ge(s("hl_ready"), NT)
            dve.wait_ge(s("hr_ready"), NT)
            parts = hrp[:, :, NH1:ROW1 - HR].bitcast(BF16)
            left = hrp[:, :, 0:NH1]
            for part in range(3):
                piece = parts[:, :, part * NH1:(part + 1) * NH1]
                link(dve.tensor_copy(piece, left))
                if part < 2:
                    link(dve.tensor_tensor(hr_rest[:, part, :, :], left, piece, ALU.subtract))
                    left = hr_rest[:, part, :, :]
            dve.sem_inc(s("hr_parts"), 1)

            def tiles1(k):
                tiles[8] = tiles_of(DVE, k, 8, 13)

            def layer1(st):
                a, b, c, d = st.back(3), st.back(5), st.back(6), st.back(8)
                if a.real():
                    na, ta = a.n, tiles[8][st.u + 5]
                    m_a = hm[:, a.slot(4), NH1:2 * NH1]
                    dve.wait_ge(s("hr_mm"), 2 * na + 1)
                    dve.reduce_max(gmax[:, 0, :], ps[:, 1, :].rearrange("p (h e) -> p h e", h=NH1), axis=AX.X).then_inc(
                        s("gmax"), 1)
                p = st.back(4)
                if p.real():
                    dve.wait_ge(s("mdiff"), p.n + 1)
                if b.real():
                    nb, rb = b.n, b.slot(2)
                    hme = ps[:, 3 + rb, 0:2 * GJ * NH1].rearrange("p (c n) -> p c n", c=GJ)
                    dve.wait_ge(s("hm_mm"), nb + 1)
                    dve.tensor_tensor(ez[:, :, :], hme[:, :, 0:NH1], row1_g[:, b.slot(8), :, HR:HP],
                                      ALU.add).then_inc(s("ez"), 1)
                if p.real():
                    dve.tensor_copy(tile(mrun, tiles[8][st.u + 4]), hm[:, p.slot(4), NH1:2 * NH1]).then_inc(s("mrun"), 1)
                if a.real():
                    dve.tensor_copy(hm[:, a.slot(4), 0:NH1], tile(hl, ta)).then_inc(s("hm_hl"), 1)
                    dve.wait_ge(s("gmax"), 2 * na + 1)
                    dve.tensor_tensor(tile(hrmax, ta), tile(hrmax, ta), gmax[:, 0, :], ALU.max).then_inc(s("hrmax"), 1)
                if b.real():
                    dve.wait_ge(s("ez"), nb + 1)
                    dve.scalar_tensor_tensor(el[:, :, :], ez[:, :, :], SLOPE, ez[:, :, :], ALU.mult,
                                             ALU.max).then_inc(s("el"), 1)
                if a.real():
                    dve.wait_ge(s("hr_mm"), 2 * na + 2)
                    dve.reduce_max(gmax[:, 1, :], ps[:, 2, :].rearrange("p (h e) -> p h e", h=NH1), axis=AX.X).then_inc(
                        s("gmax"), 1)
                if b.real():
                    dve.wait_ge(s("el"), nb + 1)
                    dve.tensor_tensor(es[:, :, :], el[:, :, :], hme[:, :, NH1:2 * NH1], ALU.subtract).then_inc(
                        s("es"), 1)
                if a.real():
                    dve.wait_ge(s("gmax"), 2 * na + 2)
                    dve.tensor_tensor(tile(hrmax, ta), tile(hrmax, ta), gmax[:, 1, :], ALU.max).then_inc(s("hrmax"), 1)
                if b.real():
                    dve.wait_ge(s("es"), nb + 1)
                    dve.tensor_scalar(em[:, rb, :, :], es[:, :, :], 0.0, None, ALU.min).then_inc(s("em"), 1)
                if a.real():
                    dve.wait_ge(s("hrmax"), 2 * na + 2)
                    dve.tensor_tensor(zz[:, :], tile(hrmax, ta), tile(hl, ta), ALU.add).then_inc(s("zz"), 1)
                if d.real():
                    acc = tile(acc1, tiles[8][st.u])
                    dve.wait_ge(s("agg1_ready"), d.n + 1)
                    dve.wait_ge(s("acc1_scaled"), d.n + 1)
                    dve.tensor_tensor(acc, acc, ps[:, 5 + d.slot(2), 0:NH1 * HE], ALU.add).then_inc(
                        s("acc1_done"), 1)
                if a.real():
                    dve.wait_ge(s("zz"), na + 1)
                    dve.scalar_tensor_tensor(m_a, zz[:, :], SLOPE, zz[:, :], ALU.mult, ALU.max).then_inc(
                        s("hm_ready"), 1)
                if c.real():
                    dve.wait_ge(s("exp1"), c.n + 1)
                    dve.tensor_tensor(msg1[:, c.slot(2), 0, :].rearrange("p (h d) -> p h d", d=HE),
                                      row1_g[:, c.slot(8), 0, 0:HR].rearrange("p (h d) -> p h d", d=HE),
                                      ew[:, c.slot(2), 0, :].unsqueeze(2).to_broadcast([P, NH1, HE]),
                                      ALU.mult).then_inc(s("msg1_ready"), 1)
                if a.real():
                    dve.wait_ge(s("hm_ready"), na + 1)
                    dve.tensor_tensor(mdiff[:, a.slot(8), :], tile(mrun, ta), m_a, ALU.subtract).then_inc(
                        s("mdiff"), 1)

            run(dve, NG, 8, 8, layer1, tiles1)
            dve.wait_ge(s("acc1_done"), NG)

            accv = acc1.rearrange("p t (h d) -> p t h d", d=HE)
            link(dve.tensor_scalar(den[:, :, :], accv[:, :, :, HD1], TINY, None, ALU.add))
            link(dve.reciprocal(den[:, :, :], den[:, :, :]))

            def finish(st):
                i, r = st.n, st.slot(2)
                if not st.first(2):
                    dve.wait_ge(s(f"out_stored{r}"), 16 * st.turn(2))
                ob = outb[:, r, :]
                dve.tensor_tensor(ob.rearrange("p (h d) -> p h d", d=HD1),
                                  tile(acc1, i).rearrange("p (h d) -> p h d", d=HE)[:, :, 0:HD1],
                                  tile(den, i).unsqueeze(2).to_broadcast([P, NH1, HD1]), ALU.mult).then_inc(
                                      s("out_div"), 1)
                dve.wait_ge(s("out_div"), i + 1)
                dve.tensor_tensor(ob, ob, tile(xs, i), ALU.add).then_inc(s("out_ready"), 1)

            run(dve, NT, 2, 0, lambda st: finish(st) if st.real() else None)

        @block.tensor
        def _(pe):
            def transposes(r, a, b, done):
                pe.transpose(tr[r][:, 0:P], a, ident[:, :])
                pe.transpose(tr[r][:, P:2 * P], b, ident[:, :]).then_inc(done, 1)

            pe.wait_ge(s("ident"), 3)
            pe.wait_ge(s("w_in"), 16 * 19)

            def node0(st):
                if st.real():
                    i, r = st.n, st.slot(2)
                    pe.wait_ge(s("xn_ready"), i + 1)
                    if not st.first(2):
                        pe.wait_ge(s("xnT"), i - 1)
                    xn = kvx_st[:, st.slot(4), 2 * H:3 * H]
                    transposes(r, xn[:, 0:P], xn[:, P:2 * P], s("xn_tr"))
                st = st.back(1)
                if st.real():
                    i, r = st.n, st.slot(2)
                    pe.wait_ge(s("xnT"), i + 1)
                    if not st.first(2):
                        pe.wait_ge(s("q_ready"), i - 1)
                    for c in range(2):
                        pe.matmul(ps[:, 1 + r, :], xnT[:, r, c, :], wqkv[:, c, 0:2 * H], start=c == 0, stop=c == 1)
                    for c in range(2):
                        ins = pe.matmul(ps[:, 3 + r, 0:H], xnT[:, r, c, :], wqkv[:, c, 2 * H:3 * H],
                                        start=c == 0, stop=c == 1)
                    ins.then_inc(s("qkv_mm"), 1)

            run(pe, NT, 4, 1, node0)

            pe.wait_ge(s("cnt_ready"), 1)
            pe.wait_ge(s("const"), 3)
            pe.matmul(ps[:, 5, 0:NT], ones[:, :], cnt[:, :], start=True, stop=True)
            pe.matmul(ps[:, 5, NT:2 * NT], upper[:, :], cnt[:, :], start=True, stop=True).then_inc(s("cnt_mm"), 1)

            pe.wait_ge(s("q_ready"), NT)
            pe.wait_ge(s("pos_ready"), 1)

            def mlp8(k2, u):
                st = Step(k2, u, 8, QUADS)
                q = st
                if q.real():
                    n, r = q.n, q.slot(2)
                    par, qq = u // 4 % 2, u % 4
                    if qq == 0:
                        last = isinstance(k2, int) and n == QUADS - 4
                        pe.wait_ge(s(f"rbf_in{par}"), k2 * 16 + 16 + (16 if last else 0))
                    if not q.first(2):
                        pe.wait_ge(s("rbfT"), n - 1)
                    transposes(r, rbf[:, par, 4 * qq:4 * qq + 2, :].rearrange("p c n -> p (c n)"),
                               rbf[:, par, 4 * qq + 2:4 * qq + 4, :].rearrange("p c n -> p (c n)"), s("rbf_used"))
                mlp_rest(st)

            def mlp_rest(st):
                st1 = st.back(1)
                if st1.real():
                    n, r = st1.n, st1.slot(2)
                    pe.wait_ge(s("rbfT"), n + 1)
                    if not st1.first(2):
                        pe.wait_ge(s("hidT"), 2 * n - 2)
                    for m in range(2):
                        for half in range(2):
                            rows = slice(half * RBF, (half + 1) * RBF)
                            ins = pe.matmul(ps[:, 1 + 2 * r + half, m * 256:m * 256 + 256],
                                            w1_sb[rows, m * P:(m + 1) * P],
                                            rbfT[rows, r, :, :].rearrange("p c e -> p (c e)"),
                                            start=True, stop=True)
                    ins.then_inc(s("hid_mm"), 1)
                st2 = st.back(2)
                if st2.real():
                    n, r = st2.n, st2.slot(2)
                    pe.wait_ge(s("hidT"), 2 * n + 2)
                    for t in range(2):
                        if not st2.first(1):
                            pe.wait_ge(s("recA_ready"), 2 * n + t - 1)
                        for half in range(2):
                            for m in range(2):
                                ins = pe.matmul(ps[:, 5 + t, half * H:(half + 1) * H],
                                                hidT[:, r, m, half, t * P:(t + 1) * P], w2_sb[:, m, :],
                                                start=m == 0, stop=m == 1)
                        ins.then_inc(s("row_mm"), 1)

            run8(pe, QUADS, mlp8)

            pe.wait_ge(s("recA_ready"), 2 * QUADS)
            pe.wait_ge(s("hidT"), 2 * QUADS)
            pe.wait_ge(s("gt_ready"), 1)

            def one_hot_T(st, made, copied, done):
                n, r, r8 = st.n, st.slot(2), st.slot(8)
                pe.wait_ge(made, n + 1)
                if not st.first(2):
                    pe.wait_ge(copied, n - 1)
                transposes(r, oneh[:, r8, 0, :], oneh[:, r8, 1, :], done)

            def layer0(st):
                a = st.back(1)
                if a.real():
                    one_hot_T(a, s("oneh0"), s("onehT0"), s("oneh_tr0"))
                c = st.back(5)
                if c.real():
                    n, r, r8 = c.n, c.slot(2), c.slot(8)
                    pe.wait_ge(s("msgP0_ready"), n + 1)
                    pe.wait_ge(s("msgP1_ready"), n + 1)
                    if not c.first(2):
                        pe.wait_ge(s("acc0_done"), n - 1)
                    for j in range(GJ):
                        pe.matmul(ps[:, 3 + r, 0:H], oneh[:, r8, j, :], msgP[:, r, j, :], start=j == 0, stop=False)
                    pe.wait_ge(s("msgA_ready"), n + 1)
                    for j in range(GJ):
                        ins = pe.matmul(ps[:, 3 + r, 0:H], oneh[:, r8, j, :], msgA[:, r, j, :], start=False,
                                        stop=j == GJ - 1)
                    ins.then_inc(s("agg0_ready"), 1)
                b = st.back(2)
                if b.real():
                    n, r = b.n, b.slot(2)
                    t = q_tiles[0][st.u]
                    pe.wait_ge(s("onehT0"), n + 1)
                    if not b.first(2):
                        pe.wait_ge(s("qk"), n - 1)
                    for j in range(GJ):
                        ins = pe.matmul(ps[:, 1 + r, j * H:(j + 1) * H], onehT[:, r, j, :],
                                        hq[:, bass.ds(t, 1), :].rearrange("p a n -> p (a n)"), start=True, stop=True)
                    ins.then_inc(s("qe_ready"), 1)

            q_tiles = {}

            def tiles0(k):
                q_tiles[0] = tiles_of(PE, k, 2)

            run(pe, NG, 8, 7, layer0, tiles0)

            pe.wait_ge(s("acc0_done"), NG)

            def proj(src_of, tr_ready, copied, tr_done, w, mm_done, bank_free):
                def body(st):
                    if st.real():
                        i, r = st.n, st.slot(2)
                        if tr_ready is not None:
                            pe.wait_ge(tr_ready, i + 1)
                        if not st.first(2):
                            pe.wait_ge(copied, i - 1)
                        v = src_of(st)
                        transposes(r, v[0], v[1], tr_done)
                    st = st.back(1)
                    if st.real():
                        i, r = st.n, st.slot(2)
                        pe.wait_ge(copied, i + 1)
                        if not st.first(2):
                            pe.wait_ge(bank_free, i - 1)
                        for c in range(2):
                            ins = pe.matmul(ps[:, 1 + r, 0:H], aT[:, r, c, :], w[:, c, :], start=c == 0, stop=c == 1)
                        ins.then_inc(mm_done, 1)
                return body

            def h2_of(st):
                return h2[:, st.slot(2), 0:P], h2[:, st.slot(2), P:2 * P]

            def transpose_acc(st):
                i = st.n
                return acc0[:, i, 0:P], acc0[:, i, P:2 * P]

            body = proj(transpose_acc, None, s("aT"), s("a_tr"), wo_sb, s("wo_mm"), s("x1"))
            for i in range(NT + 1):
                body(Step(i // 2, i % 2, 2, NT))
            pe.wait_ge(s("x1"), NT)
            run(pe, NT, 2, 1, proj(h2_of, s("h2"), s("h2T"), s("h2_tr"), W_sb, s("w_mm"), s("h2c")))

            pe.wait_ge(s("h2c"), NT)

            def spread_hr(b, j):
                n, r, r8 = b.n, b.slot(2), b.slot(8)
                if j == 0:
                    pe.wait_ge(s(f"row1_in{r8}"), 32 * b.turn(8) + 32)
                    pe.wait_ge(s("pen"), n + 1)
                if not b.first(1):
                    pe.wait_ge(s("gmax"), 2 * n + j - 1)
                bank = ps[:, 1 + j, :]
                parts = row1_g[:, r8, j, HP:ROW1].bitcast(BF16)
                for h in range(NH1):
                    for part in range(3):
                        i = part * NH1 + h
                        pe.matmul(bank[:, h * P:(h + 1) * P], parts[:, i:i + 1].to_broadcast([P, P]), ident_b[:, :],
                                  start=h == 0 and part == 0, stop=False)
                pe.matmul(bank.rearrange("p (h e) -> p h e", h=NH1), ident_b[:, :],
                          pen[:, r, j * P:(j + 1) * P].unsqueeze(1).to_broadcast([P, NH1, P]),
                          start=False, stop=True).then_inc(s("hr_mm"), 1)

            def layer1(st):
                b = st.back(2)
                if b.real():
                    spread_hr(b, 0)
                a = st.back(1)
                if a.real():
                    one_hot_T(a, s("oneh1"), s("onehT1"), s("oneh_tr1"))
                c = st.back(4)
                if c.real():
                    n, r, r4 = c.n, c.slot(2), c.slot(4)
                    pe.wait_ge(s("onehT1"), n + 1)
                    pe.wait_ge(s("hm_ready"), n + 1)
                    if not c.first(2):
                        pe.wait_ge(s("es"), n - 1)
                    for j in range(GJ):
                        ins = pe.matmul(ps[:, 3 + r, j * 8:j * 8 + 8], onehT4[:, r4, j, :],
                                        hm[:, r4, :], start=True, stop=True)
                    ins.then_inc(s("hm_mm"), 1)
                if b.real():
                    spread_hr(b, 1)
                d = st.back(7)
                if d.real():
                    n, r, r8 = d.n, d.slot(2), d.slot(8)
                    pe.wait_ge(s("msg1_ready"), n + 1)
                    pe.wait_ge(s("msg1b_ready"), n + 1)
                    if not d.first(2):
                        pe.wait_ge(s("acc1_done"), n - 1)
                    for j in range(GJ):
                        ins = pe.matmul(ps[:, 5 + r, 0:NH1 * HE], oneh[:, r8, j, :], msg1[:, r, j, :],
                                        start=j == 0, stop=j == GJ - 1)
                    ins.then_inc(s("agg1_ready"), 1)

            run(pe, NG, 8, 8, layer1)


def run8(eng, total, body):
    for u in range(8):
        body(0, u)
    with eng.Fori(1, total // 8 - 1) as k:
        for u in range(8):
            body(k, u)
    for t in range(total // 8 * 8 - 8, total + 2):
        body(t // 8, t % 8)


_INS = ["x", "src", "dst", "edge_attr_64", "edge_weight", "L0_gnn_w1", "L0_gnn_b1", "L0_gnn_w2", "L0_gnn_b2",
        "L0_gnn_ln_w", "L0_gnn_ln_b", "L0_gnn_wq", "L0_gnn_bq", "L0_gnn_wk", "L0_gnn_bk", "L0_gnn_wv",
        "L0_gnn_bv", "L0_gnn_wo", "L0_gnn_bo", "L0_gnn_gate", "L1_gnn_W", "L1_gnn_a_l", "L1_gnn_a_r"]


def kernel(**inputs):
    import concourse.bacc as _bacc
    from concourse.bass_utils import run_bass_kernel_spmd as _run

    nc = _bacc.Bacc("TRN2", target_bir_lowering=False, num_devices=1)
    arrays, args = {}, []
    for name in _INS:
        a = np.ascontiguousarray(inputs[name])
        arrays[f"in_{name}"] = a
        args.append(nc.dram_tensor(f"in_{name}", a.shape, mybir.dt.from_np(a.dtype), kind="ExternalInput").ap())
    shape = inputs["x"].shape
    o = nc.dram_tensor("out_0", shape, F32, kind="ExternalOutput").ap()
    gnn_kernel(nc, *args, o)
    r = _run(nc, [arrays], core_ids=[0])
    return r.results[0]["out_0"]
```

```python
from contextlib import ExitStack

import numpy as np

import concourse.bass as bass
from concourse import mybir

ALU = mybir.AluOpType
ACT = mybir.ActivationFunctionType
AX = mybir.AxisListType
DVE = mybir.EngineType.DVE
PE = mybir.EngineType.PE
ACT_ENGINE = mybir.EngineType.Activation
F32 = mybir.dt.float32
BF16 = mybir.dt.bfloat16
I32 = mybir.dt.int32

P = 128
EPS = 1e-5
BIG = 2.0 ** 100
SLOPE = 0.2
TINY = 1e-16


class Step:

    def __init__(self, k, u, unroll, total):
        self.k, self.u, self.unroll, self.total = k, u, unroll, total

    def back(self, d):
        return Step(self.k, self.u - d, self.unroll, self.total)

    @property
    def n(self):
        return self.k * self.unroll + self.u

    def real(self):
        return not isinstance(self.k, int) or 0 <= self.n < self.total

    def first(self, count):
        return isinstance(self.k, int) and self.n < count

    def slot(self, ring):
        return self.u % ring

    def turn(self, ring):
        return self.k * (self.unroll // ring) + self.u // ring


def run(eng, total, unroll, lag, body):
    head = min(-(-(lag + max(unroll, 4)) // unroll), total // unroll)
    tail = total // unroll

    def turn(k, steps):
        for u in range(steps):
            body(Step(k, u, unroll, total))

    for k in range(head):
        turn(k, unroll)
    if tail > head:
        with eng.Fori(head, tail) as k:
            turn(k, unroll)
    for k in range(tail, -(-(total + lag) // unroll)):
        turn(k, min(unroll, total + lag - k * unroll))


def gnn_kernel(nc, x, src, dst, edge_attr_64, edge_weight, w1, b1, w2, b2, ln_w, ln_b, wq, bq, wk, bk,
               wv, bv, wo, bo, gate, W, a_l, a_r, out):
    N, H = x.shape
    E, RBF = edge_attr_64.shape
    NH0 = 8
    HD0 = H // NH0
    _, NH1, HD1 = a_l.shape
    HE = HD1 + 1
    NT = -(-N // P)
    NLAST = N - (NT - 1) * P
    COLS = 16
    NBLK = -(-E // (P * COLS))
    CC = NBLK * COLS
    REST = E - (NBLK - 1) * P * COLS
    RP, RR = REST // COLS, REST % COLS
    QUADS = CC // 4
    GJ = 2
    GE = GJ * P
    NG = (E + NT * (GE - 1)) // GE
    NG = -(-NG // 4) * 4
    NS = NG * GE
    MINUSED = -(-E // GE)
    REC = H + 4
    KVX = 3 * H
    HR = NH1 * HE
    HP = HR + NH1
    ROW1 = HP + 3 * NH1 // 2
    SKIP = 65536.0
    assert NS < SKIP and N < NT * P and QUADS % 8 == 0 and NT % 5 == 0 and NT % 4 == 1

    rec_dram = nc.dram_tensor("sorted_edges", [NS + NT * GE, REC], F32, kind="Internal").ap()
    kvx_dram = nc.dram_tensor("node_kvx", [N, KVX], F32, kind="Internal").ap()
    row1_dram = nc.dram_tensor("node_row1", [N, ROW1], F32, kind="Internal").ap()

    with ExitStack() as ctx:
        def sb(name, shape, dt=F32):
            return ctx.enter_context(nc.sbuf_tensor(name, shape, dt))

        def sem(name):
            return ctx.enter_context(nc.semaphore(name))

        iota1 = sb("iota1", [P, P])
        iota_g = sb("iota_g", [P, NG])
        row_no = sb("row_no", [P, 1])
        ident = sb("ident", [P, P])
        ident_b = sb("ident_b", [P, P], BF16)
        upper = sb("upper", [P, P])
        ones = sb("ones", [P, P])
        w1_sb = sb("w1_sb", [P, H])
        w2_sb = sb("w2_sb", [P, 2, H])
        wqkv = sb("wqkv", [P, 2, KVX])
        wo_sb = sb("wo_sb", [P, 2, H])
        W_sb = sb("W_sb", [P, 2, H])
        b1_sb = sb("b1_sb", [P, 2])
        bqkv = sb("bqkv", [P, KVX])
        b2_bc = sb("b2_bc", [P, H])
        lnw_bc = sb("lnw_bc", [P, H])
        lnb_bc = sb("lnb_bc", [P, H])
        bo_bc = sb("bo_bc", [P, H])
        al_bc = sb("al_bc", [P, H])
        ar_bc = sb("ar_bc", [P, H])
        gate_bc = sb("gate_bc", [P, 1])

        xs = sb("xs", [P, NT, H])
        hq = sb("hq", [P, NT, H])
        mv = sb("mv", [P, NT, 2])
        rstd = sb("rstd", [P, NT])
        nmr = sb("nmr", [P, NT])
        st6 = sb("st6", [P, NT, 6])
        work = sb("work", [P, NT * CC + NT * CC // 2])
        oh = work[:, NT * CC:].bitcast(BF16).rearrange("p (b c) -> p b c", b=NT)
        rank = work[:, 0:NT * CC].rearrange("p (b c) -> p b c", b=NT)
        acc0 = work[:, 0:NT * H].rearrange("p (t n) -> p t n", t=NT)
        acc1 = work[:, NT * H:NT * (H + NH1 * HE)].rearrange("p (t n) -> p t n", t=NT)
        hl = sb("hl", [P, NT, NH1])
        hrmax = sb("hrmax", [P, NT, NH1])
        mrun = sb("mrun", [P, NT, NH1])
        den = sb("den", [P, NT, NH1])

        tile_f = sb("tile_f", [P, CC])
        pos_i = sb("pos_i", [P, CC], I32)
        cnt = sb("cnt", [P, NT])
        tot_i = sb("tot_i", [P, NT], I32)
        nch = sb("nch", [P, NT])
        gend = sb("gend", [P, NT])
        off = sb("off", [P, NT])
        zg_f = sb("zg_f", [P, 3 * NT])
        zg_i = sb("zg_i", [P, NT], I32)
        gt_f = sb("gt_f", [P, NG])
        gt_i = sb("gt_i", [P, 8 + NG + 8], I32)
        meta_s = sb("meta_s", [P, NG, GJ, 2])

        arena_n = 13056
        arena = sb("arena", [P, arena_n])
        at = [0]

        def carve(n):
            v = arena[:, at[0]:at[0] + n]
            at[0] += n
            assert at[0] <= arena_n, at[0]
            return v

        rbf = carve(2 * COLS * RBF).rearrange("p (s c n) -> p s c n", s=2, c=COLS)
        rbfT = carve(2 * 2 * P).rearrange("p (s c e) -> p s c e", s=2, c=2)
        hidT = carve(2 * 4 * 2 * P).rearrange("p (s m h e) -> p s m h e", s=2, m=2, h=2)
        rows_at = at[0]
        recA = carve(4 * 4 * REC).rearrange("p (s c n) -> p s c n", s=4, c=4)
        src_i = carve(CC).bitcast(I32)
        dst_i = carve(CC).bitcast(I32)
        cut_in = carve(CC)
        part_i = carve(CC).bitcast(I32)
        pos_f = carve(CC)
        zrows = carve(GJ * REC)
        meta_in = carve(4 * CC).rearrange("p (c n) -> p c n", n=4)
        at[0] = rows_at
        kvx_st = carve(4 * KVX).rearrange("p (s n) -> p s n", s=4)
        xnT = carve(2 * H).rearrange("p (s c e) -> p s c e", s=2, c=2)
        ended = carve(2 * NG).rearrange("p (s n) -> p s n", s=2)
        assert at[0] <= rows_at + 4 * 4 * REC
        at[0] = 0
        recB = carve(8 * GJ * REC).rearrange("p (s c n) -> p s c n", s=8, c=GJ)
        kvx_g = carve(4 * GJ * KVX).rearrange("p (s c n) -> p s c n", s=4, c=GJ)
        prod = carve(GJ * H).rearrange("p (c n) -> p c n", c=GJ)
        msgP = carve(2 * GJ * H).rearrange("p (s c n) -> p s c n", s=2, c=GJ)
        msgA = carve(2 * GJ * H).rearrange("p (s c n) -> p s c n", s=2, c=GJ)
        at[0] = 0
        aT = carve(2 * H).rearrange("p (s c e) -> p s c e", s=2, c=2)
        h2 = carve(2 * H).rearrange("p (s n) -> p s n", s=2)
        isnan = carve(2 * H).bitcast(I32).rearrange("p (s n) -> p s n", s=2)
        zeros = carve(H)
        row1 = carve(4 * HR).rearrange("p (s n) -> p s n", s=4)
        hrp = carve(NT * (ROW1 - HR)).rearrange("p (t n) -> p t n", t=NT)
        hr_rest = carve(2 * NT * NH1).rearrange("p (s t n) -> p s t n", s=2, t=NT)
        hal = carve(2 * H).rearrange("p (s n) -> p s n", s=2)
        har = carve(2 * H).rearrange("p (s n) -> p s n", s=2)
        row1_g = carve(8 * GJ * ROW1).rearrange("p (s c n) -> p s c n", s=8, c=GJ)
        msg1 = carve(2 * GJ * NH1 * HE).rearrange("p (s c n) -> p s c n", s=2, c=GJ)
        pen = carve(2 * GJ * P // 2).bitcast(BF16).rearrange("p (s n) -> p s n", s=2)
        onehT4 = carve(4 * GJ * P).rearrange("p (s c n) -> p s c n", s=4, c=GJ)

        idxA = sb("idxA", [P, 4, 4], I32)
        idxB = sb("idxB", [P, 4, GJ], I32)
        srcB = sb("srcB", [P, 4, GJ])
        behind = NT * (H + NH1 * HE)
        oneh = work[:, behind:behind + 8 * GJ * P].rearrange("p (s c n) -> p s c n", s=8, c=GJ)
        behind += 8 * GJ * P
        onehT = work[:, behind:behind + 2 * GJ * P].rearrange("p (s c n) -> p s c n", s=2, c=GJ)
        away = sb("away", [P, 2, GJ, P])
        sc = sb("sc", [P, 2, GJ, NH0])
        smax = sb("smax", [P, 2, GJ])
        pe_ = sb("pe_", [P, 2, GJ, NH0])
        psum_ = sb("psum_", [P, 2, GJ])
        prec = sb("prec", [P, GJ])
        attn = sb("attn", [P, GJ, NH0])
        gmax = sb("gmax", [P, GJ, NH1])
        zz = sb("zz", [P, NH1])
        hm = sb("hm", [P, 4, 2 * NH1])
        mdiff = sb("mdiff", [P, 8, NH1])
        mscale = sb("mscale", [P, 8, NH1])
        ez = sb("ez", [P, GJ, NH1])
        el = sb("el", [P, GJ, NH1])
        es = sb("es", [P, GJ, NH1])
        em = sb("em", [P, 2, GJ, NH1])
        ew = sb("ew", [P, 2, GJ, NH1])

        ps = ctx.enter_context(nc.psum_tensor("ps", [P, 8, 512], F32))
        tr = (ps[:, 0, 0:2 * P], ps[:, 7, 0:2 * P])

        S = {}

        def s(name):
            if name not in S:
                S[name] = sem(name)
            return S[name]

        block = ctx.enter_context(nc.Block())

        def alone(eng):
            eng.sem_inc(s("waited_" + ("pool" if eng is nc.gpsimd else "dve")), 1)

        def tiles_of(eng, k, lag, count=8):
            _, values = nc.values_load_multi_w_load_instructions(
                gt_i[0:1, bass.ds(k * 8 + (8 - lag), count)], engines=(eng,), min_val=0, max_val=NT - 1,
                skip_runtime_bounds_check_because="the table's values are bounded by the minimum with NT - 1")
            return values

        def heads_of(rows, st):
            return rows[:, st.slot(4), :].rearrange("p (h d) -> p h d", d=HE)[:, :, 0:HD1]

        def row_bc(v, n):
            return v.partition_broadcast(P)

        @block.sync
        def _(sp):
            def chunks(w):
                return w.rearrange("(c p) n -> p c n", p=P)

            sp.wait_ge(s("edge_fill"), 3)
            whole = (NBLK - 1) * P * COLS
            for t, v in ((src_i, src), (dst_i, dst), (cut_in, edge_weight)):
                tv = t[:, :].rearrange("p (b j) -> p b j", j=COLS)
                sp.dma_start(tv[:, 0:NBLK - 1, :],
                             v[0:whole].rearrange("(b p j) -> p b j", p=P, j=COLS)).then_inc(s("edges_in"), 16)
                sp.dma_start(tv[0:RP, NBLK - 1, :],
                             v[whole:whole + RP * COLS].rearrange("(p j) -> p j", j=COLS)).then_inc(s("edges_in"), 16)
                sp.dma_start(tv[RP:RP + 1, NBLK - 1, 0:RR],
                             v[whole + RP * COLS:E].rearrange("(p j) -> p j", p=1)).then_inc(s("edges_in"), 16)
            sp.wait_ge(s("x_fill"), 1)
            sp.dma_start(xs[:, 0:NT - 1, :], x[0:(NT - 1) * P, :].rearrange("(t p) n -> p t n", p=P)).then_inc(s("x_in"), 16)
            sp.dma_start(xs[0:NLAST, NT - 1, :], x[(NT - 1) * P:N, :]).then_inc(s("x_in"), 16)
            for i, w in enumerate((wk, wv, wq)):
                sp.dma_start(wqkv[:, :, i * H:(i + 1) * H], chunks(w)).then_inc(s("w_in"), 16)
            for i, v in enumerate((bk, bv, bq)):
                sp.dma_start(bqkv[:, i * H:(i + 1) * H], row_bc(v, H)).then_inc(s("w_in"), 16)
            for t, v in ((b2_bc, b2), (lnw_bc, ln_w), (lnb_bc, ln_b), (bo_bc, bo)):
                sp.dma_start(t[:, :], row_bc(v, H)).then_inc(s("w_in"), 16)
            for t, v in ((al_bc, a_l), (ar_bc, a_r)):
                sp.dma_start(t[:, :], row_bc(v.rearrange("a h d -> (a h d)"), H)).then_inc(s("w_in"), 16)
            for t, w in ((w2_sb, w2), (wo_sb, wo), (W_sb, W)):
                sp.dma_start(t[:, :, :], chunks(w)).then_inc(s("w_in"), 16)
            for half in range(2):
                sp.dma_start(w1_sb[half * RBF:(half + 1) * RBF, :], w1[:, :]).then_inc(s("w_in"), 16)
            with nc.allow_non_contiguous_dma(reason="256 values, once"):
                sp.dma_start(b1_sb[:, :], b1.rearrange("(c p) -> p c", p=P)).then_inc(s("w_in"), 16)
            sp.dma_start(gate_bc[:, :], row_bc(gate, 1)).then_inc(s("w_in"), 16)

            sp.wait_ge(s("const"), 3)
            sp.dma_start(rec_dram[MINUSED * GE:NS, :].rearrange("(g p j) n -> p g (j n)", p=P, j=GJ),
                         zrows[:, :].unsqueeze(1).to_broadcast([P, NG - MINUSED, GJ * REC])).then_inc(s("zeroed"), 16)

            def load_rbf(st):
                if not st.first(2):
                    sp.wait_ge(s("rbf_used"), 4 * st.n - 4)
                sp.dma_start(rbf[:, st.slot(2), :, :],
                             edge_attr_64[bass.ds(st.n * (P * COLS), P * COLS), :].rearrange(
                                 "(p j) n -> p j n", j=COLS)).then_inc(s(f"rbf_in{st.slot(2)}"), 16)

            for i in range(2):
                load_rbf(Step(0, i, 2, NBLK - 1))

            def store_kvx(st):
                i = st.n
                sp.wait_ge(s("xn_ready"), i + 1)
                sp.wait_ge(s("kv_ready"), i + 1)
                rows = NLAST if isinstance(i, int) and i == NT - 1 else P
                sp.dma_start(kvx_dram[bass.ds(i * P, rows), :], kvx_st[0:rows, st.slot(4), :]).then_inc(
                    s(f"kvx_out{st.slot(4)}"), 16)
                g = sp.value_load(zg_i[0:1, bass.ds(i, 1)], min_val=0, max_val=NG + NT - 1)
                sp.dma_start(rec_dram[bass.ds(g * GE, GE), :].rearrange("(p j) n -> p (j n)", j=GJ),
                             zrows[:, :]).then_inc(s("zeroed"), 16)

            sp.wait_ge(s("zg_ready"), 1)
            run(sp, NT, 4, 0, lambda st: store_kvx(st) if st.real() else None)

            for i in range(2, NBLK - 1):
                load_rbf(Step(i // 2, i % 2, 2, NBLK - 1))
            last = (NBLK - 1) % 2
            sp.wait_ge(s("rbf_used"), 4 * (NBLK - 1) - 4)
            sp.dma_start(rbf[0:RP, last, :, :],
                         edge_attr_64[whole:whole + RP * COLS, :].rearrange("(p j) n -> p j n", j=COLS)).then_inc(
                             s(f"rbf_in{last}"), 16)
            sp.dma_start(rbf[RP:RP + 1, last, 0:RR, :],
                         edge_attr_64[whole + RP * COLS:E, :].rearrange("(p j) n -> p j n", p=1)).then_inc(
                             s(f"rbf_in{last}"), 16)

            for r in range(4):
                sp.wait_ge(s(f"scattered{r}"), 16 * 4 * (QUADS // 4))

            def load_rec(st):
                if not st.first(8):
                    sp.wait_ge(s("msgP0_ready"), st.n - 7)
                    sp.wait_ge(s("msgP1_ready"), st.n - 7)
                sp.dma_start(recB[:, st.slot(8), :, :].rearrange("p c n -> p (c n)"),
                             rec_dram[bass.ds(st.n * GE, GE), :].rearrange("(p j) n -> p (j n)", j=GJ)).then_inc(
                                 s(f"rec_in{st.slot(8)}"), 16)

            run(sp, NG, 8, 0, load_rec)

            def store_row1(st):
                i = st.n
                sp.wait_ge(s("row1_ready"), i + 1)
                rows = NLAST if isinstance(i, int) and i == NT - 1 else P
                sp.dma_start(row1_dram[bass.ds(i * P, rows), 0:HR], row1[0:rows, st.slot(4), :]).then_inc(
                    s(f"row1_out{st.slot(4)}"), 16)

            run(sp, NT, 4, 0, lambda st: store_row1(st) if st.real() else None)
            sp.wait_ge(s("hr_parts"), 1)
            sp.dma_start(row1_dram[0:(NT - 1) * P, HR:ROW1].rearrange("(t p) n -> p t n", p=P),
                         hrp[:, 0:NT - 1, :]).then_inc(s("hr_out"), 16)
            sp.dma_start(row1_dram[(NT - 1) * P:N, HR:ROW1], hrp[0:NLAST, NT - 1, :]).then_inc(s("hr_out"), 16)

            for i in range(0, NT - 1, 4):
                sp.wait_ge(s("out_ready"), i + 4)
                sp.dma_start(out[i * P:(i + 4) * P, :].rearrange("(t p) n -> p t n", p=P),
                             xs[:, i:i + 4, :]).then_inc(s("out_stored"), 16)
            sp.wait_ge(s("out_ready"), NT)
            sp.dma_start(out[(NT - 1) * P:N, :], xs[0:NLAST, NT - 1, :]).then_inc(s("out_stored"), 16)
            sp.wait_ge(s("out_stored"), 16 * (NT // 4 + 1))

        @block.gpsimd
        def _(pool):
            pool.memset(src_i[:, :], NT * P + P).then_inc(s("edge_fill"), 1)
            pool.memset(dst_i[:, :], 0).then_inc(s("edge_fill"), 1)
            pool.memset(cut_in[:, :], 0.0).then_inc(s("edge_fill"), 1)
            pool.memset(xs[:, NT - 1, :], 0.0).then_inc(s("x_fill"), 1)
            pool.iota(iota1[:, :], [[1, P]], base=1, channel_multiplier=0,
                      allow_small_or_imprecise_dtypes=True).then_inc(s("iota"), 1)
            pool.iota(row_no[:, :], [[0, 1]], base=1, channel_multiplier=1,
                      allow_small_or_imprecise_dtypes=True).then_inc(s("iota"), 1)
            pool.iota(iota_g[:, :], [[1, NG]], base=0, channel_multiplier=0,
                      allow_small_or_imprecise_dtypes=True).then_inc(s("iota"), 1)
            pool.memset(ones[:, :], 1.0).then_inc(s("const"), 1)
            pool.memset(gt_i[:, :], 0).then_inc(s("gt_fill"), 1)
            pool.memset(zrows[:, :], 0.0).then_inc(s("const"), 1)
            pool.memset(meta_in[:, :, :], 0.0).then_inc(s("const"), 1)

            def residual(st):
                i = st.n
                pool.wait_ge(s("h_ready"), i + 1)
                alone(pool)
                pool.tensor_tensor(xs[:, bass.ds(i, 1), :].rearrange("p a n -> p (a n)"),
                                   xs[:, bass.ds(i, 1), :].rearrange("p a n -> p (a n)"),
                                   hq[:, bass.ds(i, 1), :].rearrange("p a n -> p (a n)"), ALU.add).then_inc(
                                       s("xh"), 1)

            run(pool, NT, 5, 0, residual)
            pool.wait_ge(s("w_in"), 16 * 19)

            def affine(st):
                i = st.n
                xn = kvx_st[:, st.slot(4), 2 * H:3 * H]
                pool.wait_ge(s("xn_norm"), i + 1)
                alone(pool)
                pool.tensor_tensor(xn, xn, lnw_bc[:, :], ALU.mult).then_inc(s("xn_w"), 1)
                pool.wait_ge(s("xn_w"), i + 1)
                alone(pool)
                pool.tensor_tensor(xn, xn, lnb_bc[:, :], ALU.add).then_inc(s("xn_ready"), 1)

            run(pool, NT, 4, 0, lambda st: affine(st) if st.real() else None)

            pool.wait_ge(s("pos_ready"), 1)
            pool.memset(acc0[:, :, :], 0.0).then_inc(s("acc_zero"), 1)
            pool.memset(acc1[:, :, :], 0.0).then_inc(s("acc_zero"), 1)
            pool.memset(hrmax[:, :, :], -BIG).then_inc(s("acc_zero"), 1)
            pool.memset(mrun[:, :, :], -BIG).then_inc(s("acc_zero"), 1)

            pool.wait_ge(s("zeroed"), 16 * (NT + 1))

            def scatter(st):
                st = st.back(2)
                if not st.real():
                    return
                pool.wait_ge(s("idxA_ready"), st.n + 1)
                pool.wait_ge(s("rows_cut"), st.n + 1)
                alone(pool)
                for c in range(4):
                    pool.indirect_dma_start(
                        rec_dram[:, :], bass.IndirectOffsetOnAxis(ap=idxA[:, st.slot(4), c:c + 1], axis=0),
                        recA[:, st.slot(4), c, :], None, bounds_check=NS - 1, oob_is_err=False).then_inc(
                            s(f"scattered{st.slot(4)}"), 16)

            run(pool, QUADS, 4, 2, scatter)

            for r in range(4):
                pool.wait_ge(s(f"kvx_out{r}"), 16 * ((NT - r + 3) // 4))
            for r in range(4):
                pool.wait_ge(s(f"scattered{r}"), 16 * 4 * (QUADS // 4))

            def gather0(st):
                b = st.back(4)
                if b.real():
                    pool.wait_ge(s(f"kvx_in{b.slot(4)}"), 32 * b.turn(4) + 32)
                    if not b.first(2):
                        pool.wait_ge(s("agg0_ready"), b.n - 1)
                    alone(pool)
                    pool.tensor_tensor(msgP[:, b.slot(2), 1, :], recB[:, b.slot(8), 1, 0:H],
                                       kvx_g[:, b.slot(4), 1, 2 * H:3 * H], ALU.mult).then_inc(s("msgP1_ready"), 1)
                if not st.real():
                    return
                pool.wait_ge(s("idxB_ready"), st.n + 1)
                if not st.first(4):
                    pool.wait_ge(s("msgP0_ready"), st.n - 3)
                    pool.wait_ge(s("msgP1_ready"), st.n - 3)
                    pool.wait_ge(s("msgA_ready"), st.n - 3)
                alone(pool)
                for j in range(GJ):
                    pool.indirect_dma_start(
                        kvx_g[:, st.slot(4), j, :], None, kvx_dram[:, :],
                        bass.IndirectOffsetOnAxis(ap=idxB[:, st.slot(4), j:j + 1], axis=0)).then_inc(
                            s(f"kvx_in{st.slot(4)}"), 16)

            run(pool, NG, 8, 4, gather0)

            pool.wait_ge(s("acc0_done"), NG)
            for r in range(4):
                pool.memset(row1[:, r, :].rearrange("p (h d) -> p h d", d=HE)[:, :, HD1:HE], 1.0).then_inc(
                    s("row1_fill"), 1)
            pool.memset(zeros, 0.0).then_inc(s("row1_fill"), 1)

            def products(st):
                i, r = st.n, st.slot(2)
                if not st.first(2):
                    pool.wait_ge(s("hl_ready"), i - 1)
                pool.wait_ge(s("row1_ready"), i + 1)
                alone(pool)
                pool.tensor_tensor(hal[:, r, :].rearrange("p (h d) -> p h d", d=HD1), heads_of(row1, st),
                                   al_bc[:, :].rearrange("p (h d) -> p h d", d=HD1), ALU.mult).then_inc(s("hal"), 1)

            run(pool, NT, 4, 0, lambda st: products(st) if st.real() else None)

            for r in range(4):
                pool.wait_ge(s(f"row1_out{r}"), 16 * ((NT - r + 3) // 4))
            pool.wait_ge(s("hr_out"), 32)

            def gather1(st):
                c = st.back(7)
                if c.real():
                    pool.wait_ge(s("exp1"), c.n + 1)
                    if not c.first(2):
                        pool.wait_ge(s("agg1_ready"), c.n - 1)
                    alone(pool)
                    pool.tensor_tensor(msg1[:, c.slot(2), 1, :].rearrange("p (h d) -> p h d", d=HE),
                                       row1_g[:, c.slot(8), 1, 0:HR].rearrange("p (h d) -> p h d", d=HE),
                                       ew[:, c.slot(2), 1, :].unsqueeze(2).to_broadcast([P, NH1, HE]),
                                       ALU.mult).then_inc(s("msg1b_ready"), 1)
                if not st.real():
                    return
                pool.wait_ge(s("idxC_ready"), st.n + 1)
                if not st.first(8):
                    pool.wait_ge(s("msg1_ready"), st.n - 7)
                    pool.wait_ge(s("msg1b_ready"), st.n - 7)
                alone(pool)
                for j in range(GJ):
                    pool.indirect_dma_start(
                        row1_g[:, st.slot(8), j, :], None, row1_dram[:, :],
                        bass.IndirectOffsetOnAxis(ap=idxB[:, st.slot(4), j:j + 1], axis=0)).then_inc(
                            s(f"row1_in{st.slot(8)}"), 16)

            run(pool, NG, 8, 7, gather1)

        @block.scalar
        def _(act):
            act.wait_ge(s("var"), 1)
            act.activation(rstd[:, :], rstd[:, :], ACT.Sqrt).then_inc(s("std"), 1)
            act.wait_ge(s("nmr"), 1)

            def relu_h(st):
                i = st.n
                act.activation(hq[:, bass.ds(i, 1), :].rearrange("p a n -> p (a n)"),
                               xs[:, bass.ds(i, 1), :].rearrange("p a n -> p (a n)"), ACT.Relu,
                               bias=nmr[:, bass.ds(i, 1)], scale=rstd[:, bass.ds(i, 1)]).then_inc(s("h_ready"), 1)

            run(act, NT, 5, 0, relu_h)
            act.wait_ge(s("var"), 2)
            act.activation(rstd[:, :], rstd[:, :], ACT.Sqrt).then_inc(s("std"), 1)
            act.wait_ge(s("nmr"), 2)

            def node0(st):
                b = st.back(2)
                if b.real():
                    act.wait_ge(s("xn_tr"), b.n + 1)
                    if not b.first(2):
                        act.wait_ge(s("qkv_mm"), b.n - 1)
                    act.copy(xnT[:, b.slot(2), :, :], tr[b.slot(2)].rearrange(
                        "p (c e) -> p c e", c=2)).then_inc(s("xnT"), 1)
                if st.real():
                    i, r = st.n, st.slot(4)
                    if not st.first(4):
                        act.wait_ge(s(f"kvx_out{r}"), 16 * st.turn(4))
                    act.activation(kvx_st[:, r, 2 * H:3 * H], hq[:, bass.ds(i, 1), :].rearrange("p a n -> p (a n)"),
                                   ACT.Identity, bias=nmr[:, bass.ds(i, 1)], scale=rstd[:, bass.ds(i, 1)]).then_inc(
                                       s("xn_norm"), 1)

            run(act, NT, 4, 2, node0)

            act.wait_ge(s("pos_ready"), 1)

            def mlp(st):
                if st.real():
                    if not st.first(4):
                        act.wait_ge(s(f"scattered{st.slot(4)}"), 64 * st.turn(4))
                    act.copy(idxA[:, st.slot(4), :], pos_i[:, bass.ds(st.n * 4, 4)]).then_inc(s("idxA_ready"), 1)
                c = st.back(2)
                st = st.back(1)
                if st.real():
                    act.wait_ge(s("hid_mm"), st.n + 1)
                    if not st.first(2):
                        act.wait_ge(s("row_mm"), 2 * st.n - 2)
                    for m in range(2):
                        bank = 1 + 2 * st.slot(2)
                        act.activation(hidT[:, st.slot(2), m, :, :], ps[:, bank:bank + 2, m * 256:m * 256 + 256],
                                       ACT.Silu, bias=b1_sb[:, m:m + 1]).then_inc(s("hidT"), 1)
                if c.real():
                    act.wait_ge(s("metaA_ready"), c.n + 1)
                    for t in range(2):
                        act.wait_ge(s("recA_ready"), 2 * c.n + t + 1)
                        for i in (2 * t, 2 * t + 1):
                            row = recA[:, c.slot(4), i, :]
                            ins = act.activation(row[:, 0:H], row[:, 0:H], ACT.Copy, scale=row[:, H:H + 1])
                    ins.then_inc(s("rows_cut"), 1)

            run(act, QUADS, 4, 2, mlp)

            def one_hot_away(st, src_ready, away_ready):
                act.wait_ge(src_ready, st.n + 1)
                for j in range(GJ):
                    act.activation(away[:, st.slot(2), j, :], iota1[:, :], ACT.Abs, bias=srcB[:, st.slot(4), j:j + 1],
                                   scale=-1.0).then_inc(away_ready, 1)

            def one_hot_near(st, away_ready, made, used):
                act.wait_ge(away_ready, 2 * st.n + 2)
                if not st.first(8):
                    act.wait_ge(used, st.n - 7)
                act.activation(oneh[:, st.slot(8), :, :], away[:, st.slot(2), :, :], ACT.Relu, bias=1.0,
                               scale=-1.0).then_inc(made, 1)

            act.wait_ge(s("acc_zero"), 4)

            def layer0(st):
                if st.real():
                    r, r8 = st.slot(4), st.slot(8)
                    act.wait_ge(s(f"rec_in{r8}"), 16 * st.turn(8) + 16)
                    if not st.first(4):
                        act.wait_ge(s(f"kvx_in{r}"), 32 * st.turn(4))
                    act.copy(idxB[:, r, :], recB[:, r8, :, H + 2]).then_inc(s("idxB_ready"), 1)
                    act.copy(srcB[:, r, :], recB[:, r8, :, H + 1]).then_inc(s("srcB_ready"), 1)
                e = st.back(4)
                if e.real():
                    act.wait_ge(s("sc_ready"), e.n + 1)
                    if not e.first(2):
                        act.wait_ge(s("attn"), e.n - 1)
                    r = e.slot(2)
                    for j in range(GJ):
                        ins = act.activation(pe_[:, r, j, :], sc[:, r, j, :], ACT.Exp, bias=smax[:, r, j:j + 1],
                                             accum_out=psum_[:, r, j:j + 1])
                    ins.then_inc(s("exp0"), 1)
                if st.real():
                    act.copy(meta_s[:, bass.ds(st.n, 1), :, :].rearrange("p a c n -> p (a c) n"),
                             recB[:, r8, :, H + 1:H + 3]).then_inc(s("meta_s"), 1)
                    one_hot_away(st, s("srcB_ready"), s("away0"))
                    one_hot_near(st, s("away0"), s("oneh0"), s("agg0_ready"))
                c = st.back(1)
                if c.real():
                    act.wait_ge(s("oneh_tr0"), c.n + 1)
                    if not c.first(2):
                        act.wait_ge(s("qe_ready"), c.n - 1)
                    r = c.slot(2)
                    act.copy(onehT[:, r, :, :], tr[r].rearrange("p (c e) -> p c e", c=GJ)).then_inc(s("onehT0"), 1)
                a = st.back(3)
                if a.real():
                    act.wait_ge(s("qk_sum"), a.n + 1)
                    for j in range(GJ):
                        v = sc[:, a.slot(2), j, :]
                        ins = act.activation(v, v, ACT.Copy, scale=recB[:, a.slot(8), j, H + 3:H + 4])
                    ins.then_inc(s("qk_cut"), 1)

            run(act, NG, 8, 7, layer0)

            def copy_aT(st):
                act.wait_ge(s("a_tr"), st.n + 1)
                if not st.first(2):
                    act.wait_ge(s("wo_mm"), st.n - 1)
                act.copy(aT[:, st.slot(2), :, :], tr[st.slot(2)].rearrange(
                    "p (c e) -> p c e", c=2)).then_inc(s("aT"), 1)

            run(act, NT, 2, 0, lambda st: copy_aT(st) if st.real() else None)
            act.wait_ge(s("var"), 3)
            act.activation(rstd[:, :], rstd[:, :], ACT.Sqrt).then_inc(s("std"), 1)
            act.wait_ge(s("nmr"), 3)

            def node1(st):
                if st.real():
                    i, r = st.n, st.slot(2)
                    if not st.first(2):
                        act.wait_ge(s("h2_tr"), i - 1)
                    act.activation(h2[:, r, :], xs[:, bass.ds(i, 1), :].rearrange("p a n -> p (a n)"), ACT.Relu,
                                   bias=nmr[:, bass.ds(i, 1)], scale=rstd[:, bass.ds(i, 1)]).then_inc(s("h2"), 1)
                b = st.back(1)
                if b.real():
                    act.wait_ge(s("h2_tr"), b.n + 1)
                    if not b.first(2):
                        act.wait_ge(s("w_mm"), b.n - 1)
                    act.copy(aT[:, b.slot(2), :, :], tr[b.slot(2)].rearrange(
                        "p (c e) -> p c e", c=2)).then_inc(s("h2T"), 1)
                c = st.back(2)
                if c.real():
                    act.wait_ge(s("w_mm"), c.n + 1)
                    if not c.first(4):
                        act.wait_ge(s(f"row1_out{c.slot(4)}"), 16 * c.turn(4))
                        act.wait_ge(s("hl_ready"), c.n - 3)
                    act.copy(heads_of(row1, c), ps[:, 1 + c.slot(2), 0:H].rearrange("p (h d) -> p h d", d=HD1)).then_inc(
                        s("h2c"), 1)

            run(act, NT, 4, 2, node1)

            act.wait_ge(s("meta_s"), NG)

            act_tiles = {}

            def layer1(st):
                if st.real():
                    r = st.slot(4)
                    if not st.first(4):
                        old = st.back(4)
                        act.wait_ge(s(f"row1_in{old.slot(8)}"), 32 * old.turn(8) + 32)
                    m = meta_s[:, bass.ds(st.n, 1), :, :].rearrange("p a c n -> p (a c) n")
                    act.copy(idxB[:, r, :], m[:, :, 1]).then_inc(s("idxC_ready"), 1)
                    act.copy(srcB[:, r, :], m[:, :, 0]).then_inc(s("srcC_ready"), 1)
                e = st.back(6)
                if e.real():
                    act.wait_ge(s("em"), e.n + 1)
                    if not e.first(2):
                        act.wait_ge(s("msg1_ready"), e.n - 1)
                        act.wait_ge(s("msg1b_ready"), e.n - 1)
                    r = e.slot(2)
                    act.activation(ew[:, r, :, :], em[:, r, :, :], ACT.Exp).then_inc(s("exp1"), 1)
                if st.real():
                    one_hot_away(st, s("srcC_ready"), s("away1"))
                if st.u == 0:
                    act_tiles[8] = tiles_of(ACT_ENGINE, st.k, 8)
                d = st.back(8)
                if d.real():
                    act.wait_ge(s("mscale"), d.n + 1)
                    if not d.first(1):
                        act.wait_ge(s("acc1_done"), d.n)
                    for h in range(NH1):
                        v = acc1[:, bass.ds(act_tiles[8][st.u], 1), h * HE:(h + 1) * HE].rearrange("p a n -> p (a n)")
                        ins = act.activation(v, v, ACT.Copy, scale=mscale[:, d.slot(8), h:h + 1])
                    ins.then_inc(s("acc1_scaled"), 1)
                if st.real():
                    one_hot_near(st, s("away1"), s("oneh1"), s("agg1_ready"))
                e = st.back(6)
                if e.real():
                    act.wait_ge(s("mdiff"), e.n + 1)
                    if not e.first(8):
                        act.wait_ge(s("acc1_scaled"), e.n - 7)
                    act.activation(mscale[:, e.slot(8), :], mdiff[:, e.slot(8), :], ACT.Exp).then_inc(
                        s("mscale"), 1)
                c = st.back(1)
                if c.real():
                    r = c.slot(2)
                    act.wait_ge(s("oneh_tr1"), c.n + 1)
                    if not c.first(2):
                        act.wait_ge(s("hr_mm"), 2 * c.n - 2)
                    act.activation(pen[:, r, :], tr[r], ACT.Copy, bias=-BIG, scale=BIG).then_inc(s("pen"), 1)
                    if not c.first(4):
                        act.wait_ge(s("hm_mm"), c.n - 3)
                    act.copy(onehT4[:, c.slot(4), :, :], tr[r].rearrange("p (c e) -> p c e", c=GJ)).then_inc(
                        s("onehT1"), 1)

            run(act, NG, 8, 8, layer1)

        @block.vector
        def _(dve):
            made = [0]

            def link(ins):
                made[0] += 1
                ins.then_inc(s("chain"), 1)
                dve.wait_ge(s("chain"), made[0])

            dve.wait_ge(s("iota"), 3)
            dve.tensor_scalar(ident[:, :], iota1[:, :], row_no[:, 0:1], None, ALU.is_equal).then_inc(s("ident"), 1)
            dve.tensor_scalar(ident_b[:, :], iota1[:, :], row_no[:, 0:1], None, ALU.is_equal).then_inc(s("ident"), 1)
            dve.tensor_scalar(upper[:, :], iota1[:, :], row_no[:, 0:1], None, ALU.is_gt).then_inc(s("ident"), 1)

            def tile(t, i):
                return t[:, bass.ds(i, 1), :].rearrange("p a n -> p (a n)")

            def aggregate(turn):
                dve.wait_ge(s("row_stats"), turn * NT)
                for i in range(NT):
                    ins = dve.bn_aggr(mv[:, i, :], st6[:, i, :])
                link(ins)

            def stats(turn, source, ready):
                def one(st):
                    if ready is not None:
                        dve.wait_ge(ready, st.n + 1)
                    dve.bn_stats(tile(st6, st.n), tile(source, st.n)).then_inc(s("row_stats"), 1)

                run(dve, NT, 5, 0, one)
                aggregate(turn)

            def rstds(n):
                dve.tensor_scalar(rstd[:, :], mv[:, :, 1], EPS, None, ALU.add).then_inc(s("var"), 1)
                dve.wait_ge(s("std"), n)
                link(dve.reciprocal(rstd[:, :], rstd[:, :]))
                dve.scalar_tensor_tensor(nmr[:, :], mv[:, :, 0], -1.0, rstd[:, :], ALU.mult, ALU.mult).then_inc(
                    s("nmr"), 1)
                dve.wait_ge(s("nmr"), n)

            dve.wait_ge(s("edges_in"), 16 * 9)
            dve.wait_ge(s("const"), 3)
            link(dve.tensor_single_scalar(part_i[:, :], src_i[:, :], 7, ALU.arith_shift_right))
            link(dve.tensor_copy(tile_f[:, :], part_i[:, :]))
            link(dve.tensor_single_scalar(part_i[:, :], src_i[:, :], P - 1, ALU.bitwise_and))
            dve.tensor_scalar(meta_in[:, :, 1], part_i[:, :], 1.0, None, ALU.add).then_inc(s("meta_in"), 1)
            dve.tensor_copy(meta_in[:, :, 2], dst_i[:, :]).then_inc(s("meta_in"), 1)
            dve.tensor_copy(meta_in[:, :, 0], cut_in[:, :]).then_inc(s("meta_in"), 1)
            dve.tensor_scalar(meta_in[:, :, 3], cut_in[:, :], float(HD0) ** -0.5, None, ALU.mult).then_inc(s("meta_in"), 1)
            for b in range(NT):
                ins = dve.tensor_scalar(oh[:, b, :], tile_f[:, :], float(b), None, ALU.is_equal)
            link(ins)
            dve.wait_ge(s("x_in"), 32)
            stats(1, xs, None)
            rstds(1)

            for b in range(NT):
                ins = dve.tensor_tensor_scan(rank[:, b, :], oh[:, b, :], oh[:, b, :], 0.0, ALU.add, ALU.max)
            link(ins)
            dve.tensor_copy(cnt[:, :], rank[:, :, CC - 1]).then_inc(s("cnt_ready"), 1)

            stats(2, hq, s("h_ready"))
            dve.wait_ge(s("h_ready"), NT)
            rstds(2)
            dve.wait_ge(s("cnt_mm"), 1)
            tot, pre = ps[:, 5, 0:NT], ps[:, 5, NT:2 * NT]
            link(dve.tensor_scalar(tot_i[:, :], tot, float(GE - 1), None, ALU.add))
            link(dve.tensor_single_scalar(tot_i[:, :], tot_i[:, :], 8, ALU.arith_shift_right))
            link(dve.tensor_copy(nch[:, :], tot_i[:, :]))
            link(dve.tensor_tensor_scan(gend[:, :], nch[:, :], nch[:, :], 0.0, ALU.add, ALU.max))
            link(dve.tensor_tensor(off[:, :], gend[:, :], nch[:, :], ALU.subtract))
            link(dve.scalar_tensor_tensor(off[:, :], off[:, :], float(GE), pre, ALU.mult, ALU.add))
            spare, keep = zg_f[:, NT:2 * NT], zg_f[:, 2 * NT:3 * NT]
            dve.tensor_scalar(spare, iota_g[:, 0:NT], float(NG), None, ALU.add)
            dve.tensor_scalar(keep, nch[:, :], 1.0, None, ALU.min)
            link(dve.tensor_scalar(zg_f[:, 0:NT], gend[:, :], -1.0, None, ALU.add))
            link(dve.scalar_tensor_tensor(keep, zg_f[:, 0:NT], float(MINUSED), keep, ALU.is_lt, ALU.mult))
            link(dve.tensor_tensor(zg_f[:, 0:NT], zg_f[:, 0:NT], spare, ALU.subtract))
            link(dve.tensor_tensor(zg_f[:, 0:NT], zg_f[:, 0:NT], keep, ALU.mult))
            dve.tensor_tensor(zg_i[:, :], zg_f[:, 0:NT], spare, ALU.add).then_inc(s("zg_ready"), 1)
            for b in range(2):
                dve.tensor_scalar(ended[:, b, :], iota_g[:, :], gend[:, b:b + 1], None, ALU.is_ge).then_inc(s("ended"), 1)
            for b in range(2, NT):
                dve.wait_ge(s("ended"), b - 1)
                dve.scalar_tensor_tensor(ended[:, b % 2, :], iota_g[:, :], gend[:, b:b + 1], ended[:, b % 2, :],
                                         ALU.is_ge, ALU.add).then_inc(s("ended"), 1)
            dve.wait_ge(s("ended"), NT)
            link(dve.tensor_tensor(gt_f[:, :], ended[:, 0, :], ended[:, 1, :], ALU.add))
            dve.wait_ge(s("gt_fill"), 1)
            dve.tensor_scalar(gt_i[:, 8:8 + NG], gt_f[:, :], float(NT - 1), None, ALU.min).then_inc(s("gt_ready"), 1)
            dve.wait_ge(s("gt_ready"), 1)
            link(dve.tensor_scalar(tile_f[:, :], tile_f[:, :], float(NT) - 0.5, SKIP, ALU.is_gt, ALU.mult))

            dve.wait_ge(s("w_in"), 16 * 19)

            def slots(c):
                part = rank[:, :, bass.ds(c * COLS, COLS)]
                yield dve.tensor_tensor(part, part, off[:, :].unsqueeze(2).to_broadcast([P, NT, COLS]),
                                        ALU.add).then_inc(s("slot_steps"), 1)
                dve.wait_ge(s("slot_steps"), 2 * c + 1)
                yield dve.tensor_tensor(part, part, oh[:, :, bass.ds(c * COLS, COLS)], ALU.mult).then_inc(
                    s("slot_steps"), 1)
                dve.wait_ge(s("slot_steps"), 2 * c + 2)
                yield dve.reduce_sum(pos_f[:, bass.ds(c * COLS, COLS)], part.rearrange("p b c -> p c b"),
                                     axis=AX.X).then_inc(s("slots"), 1)

            def node0(st):
                i, r = st.n, st.slot(2)
                steps = slots(i)
                next(steps)
                dve.wait_ge(s("qkv_mm"), i + 1)
                dve.tensor_tensor(kvx_st[:, st.slot(4), 0:2 * H], ps[:, 1 + r, :], bqkv[:, 0:2 * H],
                                  ALU.add).then_inc(s("kv_ready"), 1)
                next(steps)
                dve.wait_ge(s("xh"), i + 1)
                dve.tensor_tensor(tile(hq, i), ps[:, 3 + r, 0:H], bqkv[:, 2 * H:3 * H], ALU.add).then_inc(
                    s("q_ready"), 1)
                next(steps)

            run(dve, NT, 4, 0, lambda st: node0(st) if st.real() else None)
            for c in range(NT, CC // COLS):
                for _ in slots(c):
                    pass
            dve.wait_ge(s("slots"), CC // COLS)
            dve.scalar_tensor_tensor(pos_i[:, :], pos_f[:, :], -1.0, tile_f[:, :], ALU.add, ALU.add).then_inc(
                s("pos_ready"), 1)

            def mlp(st):
                if st.real():
                    r = st.slot(2)
                    dve.wait_ge(s("rbf_used"), st.n + 1)
                    if not st.first(2):
                        dve.wait_ge(s("hid_mm"), st.n - 1)
                    dve.tensor_copy(rbfT[:, r, :, :], tr[r].rearrange(
                        "p (c e) -> p c e", c=2)).then_inc(s("rbfT"), 1)
                st = st.back(2)
                if st.real():
                    r = st.slot(4)
                    if not st.first(4):
                        dve.wait_ge(s(f"scattered{r}"), 64 * st.turn(4))
                    dve.tensor_copy(recA[:, r, :, H:REC], meta_in[:, bass.ds(st.n * 4, 4), :]).then_inc(
                        s("metaA_ready"), 1)
                    for t in range(2):
                        dve.wait_ge(s("row_mm"), 2 * st.n + t + 1)
                        dve.tensor_tensor(recA[:, r, 2 * t:2 * t + 2, 0:H],
                                          ps[:, 5 + t, :].rearrange("p (c n) -> p c n", c=2),
                                          b2_bc[:, :].unsqueeze(1).to_broadcast([P, 2, H]),
                                          ALU.add).then_inc(s("recA_ready"), 1)

            dve.wait_ge(s("meta_in"), 4)
            for r in range(4):
                dve.wait_ge(s(f"kvx_out{r}"), 16 * ((NT - r + 3) // 4))
            run(dve, QUADS, 4, 2, mlp)

            dve.tensor_tensor(xs[:, :, :], xs[:, :, :], bo_bc[:, :].unsqueeze(1).to_broadcast([P, NT, H]),
                              ALU.add).then_inc(s("xhb"), 1)
            dve.wait_ge(s("acc_zero"), 4)

            def heads(v):
                return v.rearrange("p c (h d) -> p c h d", d=HD0)

            tiles = {}

            def layer0(st):
                a, b, c = st.back(3), st.back(4), st.back(6)
                if a.real():
                    ra, na = a.slot(2), a.n
                    dve.wait_ge(s("qe_ready"), na + 1)
                    dve.wait_ge(s(f"kvx_in{a.slot(4)}"), 32 * a.turn(4) + 32)
                    dve.tensor_tensor(prod[:, :, :], ps[:, 1 + ra, :].rearrange("p (c n) -> p c n", c=GJ),
                                      kvx_g[:, a.slot(4), :, 0:H], ALU.mult).then_inc(s("qk"), 1)
                if b.real():
                    rb, nb = b.slot(2), b.n
                    v_b = kvx_g[:, b.slot(4), :, H:2 * H]
                    if not b.first(2):
                        dve.wait_ge(s("agg0_ready"), nb - 1)
                    dve.tensor_tensor(msgP[:, rb, 0, :], recB[:, b.slot(8), 0, 0:H], kvx_g[:, b.slot(4), 0, 2 * H:3 * H],
                                      ALU.mult).then_inc(s("msgP0_ready"), 1)
                if st.u == 0:
                    tiles[6] = tiles_of(DVE, st.k, 6)
                if a.real():
                    dve.wait_ge(s("qk"), na + 1)
                    dve.reduce_sum(sc[:, ra, :, :], heads(prod), axis=AX.X).then_inc(s("qk_sum"), 1)
                if b.real():
                    dve.wait_ge(s("exp0"), nb + 1)
                    dve.reciprocal(prec[:, :], psum_[:, rb, :]).then_inc(s("prec"), 1)
                if c.real():
                    acc = tile(acc0, tiles[6][st.u])
                    if not b.real():
                        dve.wait_ge(s("acc0_done"), c.n)
                    dve.wait_ge(s("agg0_ready"), c.n + 1)
                    dve.tensor_tensor(acc, acc, ps[:, 3 + c.slot(2), 0:H], ALU.add).then_inc(s("acc0_done"), 1)
                if b.real():
                    dve.wait_ge(s("prec"), nb + 1)
                    dve.scalar_tensor_tensor(attn[:, :, :], pe_[:, rb, :, :], gate_bc[:, 0:1],
                                             prec[:, :].unsqueeze(2).to_broadcast([P, GJ, NH0]),
                                             ALU.mult, ALU.mult).then_inc(s("attn"), 1)
                if b.real():
                    dve.wait_ge(s("attn"), nb + 1)
                    dve.tensor_tensor(heads(msgA[:, rb, :, :]), heads(v_b),
                                      attn[:, :, :].unsqueeze(3).to_broadcast([P, GJ, NH0, HD0]),
                                      ALU.mult).then_inc(s("msgA_ready"), 1)
                if a.real():
                    dve.wait_ge(s("qk_cut"), na + 1)
                    dve.tensor_reduce(smax[:, ra, :], sc[:, ra, :, :], AX.X, ALU.max, negate=True).then_inc(
                        s("sc_ready"), 1)

            run(dve, NG, 8, 7, layer0)

            dve.wait_ge(s("xhb"), 1)

            def node1(st):
                if st.real():
                    i = st.n
                    dve.wait_ge(s("wo_mm"), i + 1)
                    dve.tensor_tensor(tile(xs, i), tile(xs, i), ps[:, 1 + st.slot(2), 0:H], ALU.add).then_inc(s("x1"), 1)
                st = st.back(1)
                if st.real():
                    dve.wait_ge(s("x1"), st.n + 1)
                    dve.bn_stats(tile(st6, st.n), tile(xs, st.n)).then_inc(s("row_stats"), 1)

            run(dve, NT, 4, 1, node1)
            aggregate(3)
            rstds(3)

            def node2(st):
                a, b = st, st.back(1)
                if a.real():
                    row, nan = heads_of(row1, a), isnan[:, a.slot(2), :].rearrange("p (h d) -> p h d", d=HD1)
                    dve.wait_ge(s("h2c"), a.n + 1)
                    dve.tensor_tensor(nan, row, row, ALU.not_equal).then_inc(s("isnan"), 1)
                if b.real():
                    r = b.slot(2)
                    dve.wait_ge(s("row1_ready"), b.n + 1)
                    dve.tensor_tensor(har[:, r, :].rearrange("p (h d) -> p h d", d=HD1), heads_of(row1, b),
                                      ar_bc[:, :].rearrange("p (h d) -> p h d", d=HD1), ALU.mult).then_inc(s("har"), 1)
                if a.real():
                    dve.wait_ge(s("isnan"), a.n + 1)
                    alone(dve)
                    dve.copy_predicated(row, nan, zeros.rearrange("p (h d) -> p h d", d=HD1)).then_inc(
                        s("row1_ready"), 1)
                if b.real():
                    dve.wait_ge(s("har"), b.n + 1)
                    dve.reduce_sum(hrp[:, bass.ds(b.n, 1), 0:NH1].rearrange("p a n -> p (a n)"),
                                   har[:, r, :].rearrange("p (h d) -> p h d", d=HD1), axis=AX.X).then_inc(
                                       s("hr_ready"), 1)
                    dve.wait_ge(s("hal"), b.n + 1)
                    dve.reduce_sum(tile(hl, b.n), hal[:, r, :].rearrange("p (h d) -> p h d", d=HD1),
                                   axis=AX.X).then_inc(s("hl_ready"), 1)

            dve.wait_ge(s("row1_fill"), 5)
            run(dve, NT, 4, 1, node2)
            dve.wait_ge(s("hl_ready"), NT)
            dve.wait_ge(s("hr_ready"), NT)
            parts = hrp[:, :, NH1:ROW1 - HR].bitcast(BF16)
            left = hrp[:, :, 0:NH1]
            for part in range(3):
                piece = parts[:, :, part * NH1:(part + 1) * NH1]
                link(dve.tensor_copy(piece, left))
                if part < 2:
                    link(dve.tensor_tensor(hr_rest[:, part, :, :], left, piece, ALU.subtract))
                    left = hr_rest[:, part, :, :]
            dve.sem_inc(s("hr_parts"), 1)

            def layer1(st):
                a, b, c, d = st.back(3), st.back(5), st.back(6), st.back(8)
                if a.real():
                    na = a.n
                    m_a = hm[:, a.slot(4), NH1:2 * NH1]
                    dve.wait_ge(s("hr_mm"), 2 * na + 1)
                    dve.reduce_max(gmax[:, 0, :], ps[:, 1, :].rearrange("p (h e) -> p h e", h=NH1), axis=AX.X).then_inc(
                        s("gmax"), 1)
                p = st.back(4)
                if p.real():
                    dve.wait_ge(s("mdiff"), p.n + 1)
                if b.real():
                    nb, rb = b.n, b.slot(2)
                    hme = ps[:, 3 + rb, 0:2 * GJ * NH1].rearrange("p (c n) -> p c n", c=GJ)
                    dve.wait_ge(s("hm_mm"), nb + 1)
                    dve.tensor_tensor(ez[:, :, :], hme[:, :, 0:NH1], row1_g[:, b.slot(8), :, HR:HP],
                                      ALU.add).then_inc(s("ez"), 1)
                if st.u == 0:
                    tiles[8] = tiles_of(DVE, st.k, 8, 13)
                ta = tiles[8][st.u + 5]
                if p.real():
                    dve.tensor_copy(tile(mrun, tiles[8][st.u + 4]), hm[:, p.slot(4), NH1:2 * NH1])
                if a.real():
                    dve.tensor_copy(hm[:, a.slot(4), 0:NH1], tile(hl, ta))
                    dve.wait_ge(s("gmax"), 2 * na + 1)
                    dve.tensor_tensor(tile(hrmax, ta), tile(hrmax, ta), gmax[:, 0, :], ALU.max).then_inc(s("hrmax"), 1)
                if b.real():
                    dve.wait_ge(s("ez"), nb + 1)
                    dve.scalar_tensor_tensor(el[:, :, :], ez[:, :, :], SLOPE, ez[:, :, :], ALU.mult,
                                             ALU.max).then_inc(s("el"), 1)
                if a.real():
                    dve.wait_ge(s("hr_mm"), 2 * na + 2)
                    dve.reduce_max(gmax[:, 1, :], ps[:, 2, :].rearrange("p (h e) -> p h e", h=NH1), axis=AX.X).then_inc(
                        s("gmax"), 1)
                if b.real():
                    dve.wait_ge(s("el"), nb + 1)
                    dve.tensor_tensor(es[:, :, :], el[:, :, :], hme[:, :, NH1:2 * NH1], ALU.subtract).then_inc(
                        s("es"), 1)
                if a.real():
                    dve.wait_ge(s("gmax"), 2 * na + 2)
                    dve.tensor_tensor(tile(hrmax, ta), tile(hrmax, ta), gmax[:, 1, :], ALU.max).then_inc(s("hrmax"), 1)
                if b.real():
                    dve.wait_ge(s("es"), nb + 1)
                    dve.tensor_scalar(em[:, rb, :, :], es[:, :, :], 0.0, None, ALU.min).then_inc(s("em"), 1)
                if a.real():
                    dve.wait_ge(s("hrmax"), 2 * na + 2)
                    dve.tensor_tensor(zz[:, :], tile(hrmax, ta), tile(hl, ta), ALU.add).then_inc(s("zz"), 1)
                if d.real():
                    acc = tile(acc1, tiles[8][st.u])
                    dve.wait_ge(s("agg1_ready"), d.n + 1)
                    dve.wait_ge(s("acc1_scaled"), d.n + 1)
                    dve.tensor_tensor(acc, acc, ps[:, 5 + d.slot(2), 0:NH1 * HE], ALU.add).then_inc(
                        s("acc1_done"), 1)
                if a.real():
                    dve.wait_ge(s("zz"), na + 1)
                    dve.scalar_tensor_tensor(m_a, zz[:, :], SLOPE, zz[:, :], ALU.mult, ALU.max).then_inc(
                        s("hm_ready"), 1)
                if c.real():
                    dve.wait_ge(s("exp1"), c.n + 1)
                    dve.tensor_tensor(msg1[:, c.slot(2), 0, :].rearrange("p (h d) -> p h d", d=HE),
                                      row1_g[:, c.slot(8), 0, 0:HR].rearrange("p (h d) -> p h d", d=HE),
                                      ew[:, c.slot(2), 0, :].unsqueeze(2).to_broadcast([P, NH1, HE]),
                                      ALU.mult).then_inc(s("msg1_ready"), 1)
                if a.real():
                    dve.wait_ge(s("hm_ready"), na + 1)
                    dve.tensor_tensor(mdiff[:, a.slot(8), :], tile(mrun, ta), m_a, ALU.subtract).then_inc(
                        s("mdiff"), 1)

            run(dve, NG, 8, 8, layer1)
            dve.wait_ge(s("acc1_done"), NG)

            accv = acc1.rearrange("p t (h d) -> p t h d", d=HE)
            link(dve.tensor_scalar(den[:, :, :], accv[:, :, :, HD1], TINY, None, ALU.add))
            link(dve.reciprocal(den[:, :, :], den[:, :, :]))

            def finish(st):
                i = st.n
                for h in range(NH1):
                    cols = slice(h * HD1, (h + 1) * HD1)
                    ins = dve.scalar_tensor_tensor(tile(xs, i)[:, cols], tile(acc1, i)[:, h * HE:h * HE + HD1],
                                                   tile(den, i)[:, h:h + 1], tile(xs, i)[:, cols], ALU.mult, ALU.add)
                ins.then_inc(s("out_ready"), 1)

            run(dve, NT, 5, 0, finish)

        @block.tensor
        def _(pe):
            def transposes(r, a, b, done):
                pe.transpose(tr[r][:, 0:P], a, ident[:, :])
                pe.transpose(tr[r][:, P:2 * P], b, ident[:, :]).then_inc(done, 1)

            pe.wait_ge(s("ident"), 3)
            pe.wait_ge(s("cnt_ready"), 1)
            pe.wait_ge(s("const"), 3)
            pe.matmul(ps[:, 5, 0:NT], ones[:, :], cnt[:, :], start=True, stop=True)
            pe.matmul(ps[:, 5, NT:2 * NT], upper[:, :], cnt[:, :], start=True, stop=True).then_inc(s("cnt_mm"), 1)

            pe.wait_ge(s("w_in"), 16 * 19)

            def node0(st):
                if st.real():
                    i, r = st.n, st.slot(2)
                    pe.wait_ge(s("xn_ready"), i + 1)
                    if not st.first(2):
                        pe.wait_ge(s("xnT"), i - 1)
                    xn = kvx_st[:, st.slot(4), 2 * H:3 * H]
                    transposes(r, xn[:, 0:P], xn[:, P:2 * P], s("xn_tr"))
                st = st.back(1)
                if st.real():
                    i, r = st.n, st.slot(2)
                    pe.wait_ge(s("xnT"), i + 1)
                    if not st.first(2):
                        pe.wait_ge(s("q_ready"), i - 1)
                    for c in range(2):
                        pe.matmul(ps[:, 1 + r, :], xnT[:, r, c, :], wqkv[:, c, 0:2 * H], start=c == 0, stop=c == 1)
                    for c in range(2):
                        ins = pe.matmul(ps[:, 3 + r, 0:H], xnT[:, r, c, :], wqkv[:, c, 2 * H:3 * H],
                                        start=c == 0, stop=c == 1)
                    ins.then_inc(s("qkv_mm"), 1)

            run(pe, NT, 4, 1, node0)

            pe.wait_ge(s("q_ready"), NT)

            def mlp8(k2, u):
                st = Step(k2, u, 8, QUADS)
                q = st
                if q.real():
                    n, r = q.n, q.slot(2)
                    par, qq = u // 4 % 2, u % 4
                    if qq == 0:
                        last = isinstance(k2, int) and n == QUADS - 4
                        pe.wait_ge(s(f"rbf_in{par}"), k2 * 16 + 16 + (16 if last else 0))
                    if not q.first(2):
                        pe.wait_ge(s("rbfT"), n - 1)
                    transposes(r, rbf[:, par, 4 * qq:4 * qq + 2, :].rearrange("p c n -> p (c n)"),
                               rbf[:, par, 4 * qq + 2:4 * qq + 4, :].rearrange("p c n -> p (c n)"), s("rbf_used"))
                mlp_rest(st)

            def mlp_rest(st):
                st1 = st.back(1)
                if st1.real():
                    n, r = st1.n, st1.slot(2)
                    pe.wait_ge(s("rbfT"), n + 1)
                    if not st1.first(2):
                        pe.wait_ge(s("hidT"), 2 * n - 2)
                    for m in range(2):
                        for half in range(2):
                            rows = slice(half * RBF, (half + 1) * RBF)
                            ins = pe.matmul(ps[:, 1 + 2 * r + half, m * 256:m * 256 + 256],
                                            w1_sb[rows, m * P:(m + 1) * P],
                                            rbfT[rows, r, :, :].rearrange("p c e -> p (c e)"),
                                            start=True, stop=True)
                    ins.then_inc(s("hid_mm"), 1)
                st2 = st.back(2)
                if st2.real():
                    n, r = st2.n, st2.slot(2)
                    pe.wait_ge(s("hidT"), 2 * n + 2)
                    for t in range(2):
                        if not st2.first(1):
                            pe.wait_ge(s("recA_ready"), 2 * n + t - 1)
                        for half in range(2):
                            for m in range(2):
                                ins = pe.matmul(ps[:, 5 + t, half * H:(half + 1) * H],
                                                hidT[:, r, m, half, t * P:(t + 1) * P], w2_sb[:, m, :],
                                                start=m == 0, stop=m == 1)
                        ins.then_inc(s("row_mm"), 1)

            run8(pe, QUADS, mlp8)

            pe.wait_ge(s("recA_ready"), 2 * QUADS)
            pe.wait_ge(s("hidT"), 2 * QUADS)
            pe.wait_ge(s("gt_ready"), 1)

            def one_hot_T(st, made, copied, done):
                n, r, r8 = st.n, st.slot(2), st.slot(8)
                pe.wait_ge(made, n + 1)
                if not st.first(2):
                    pe.wait_ge(copied, n - 1)
                transposes(r, oneh[:, r8, 0, :], oneh[:, r8, 1, :], done)

            def layer0(st):
                a = st.back(1)
                if a.real():
                    one_hot_T(a, s("oneh0"), s("onehT0"), s("oneh_tr0"))
                if st.u == 0:
                    q_tiles[2] = tiles_of(PE, st.k, 2)
                c = st.back(5)
                if c.real():
                    n, r, r8 = c.n, c.slot(2), c.slot(8)
                    pe.wait_ge(s("msgP0_ready"), n + 1)
                    pe.wait_ge(s("msgP1_ready"), n + 1)
                    if not c.first(2):
                        pe.wait_ge(s("acc0_done"), n - 1)
                    for j in range(GJ):
                        pe.matmul(ps[:, 3 + r, 0:H], oneh[:, r8, j, :], msgP[:, r, j, :], start=j == 0, stop=False)
                    pe.wait_ge(s("msgA_ready"), n + 1)
                    for j in range(GJ):
                        ins = pe.matmul(ps[:, 3 + r, 0:H], oneh[:, r8, j, :], msgA[:, r, j, :], start=False,
                                        stop=j == GJ - 1)
                    ins.then_inc(s("agg0_ready"), 1)
                b = st.back(2)
                if b.real():
                    n, r = b.n, b.slot(2)
                    t = q_tiles[2][st.u]
                    pe.wait_ge(s("onehT0"), n + 1)
                    if not b.first(2):
                        pe.wait_ge(s("qk"), n - 1)
                    for j in range(GJ):
                        ins = pe.matmul(ps[:, 1 + r, j * H:(j + 1) * H], onehT[:, r, j, :],
                                        hq[:, bass.ds(t, 1), :].rearrange("p a n -> p (a n)"), start=True, stop=True)
                    ins.then_inc(s("qe_ready"), 1)

            q_tiles = {}

            run(pe, NG, 8, 7, layer0)

            pe.wait_ge(s("acc0_done"), NG)

            def proj(src_of, tr_ready, copied, tr_done, w, mm_done, bank_free):
                def body(st):
                    if st.real():
                        i, r = st.n, st.slot(2)
                        if tr_ready is not None:
                            pe.wait_ge(tr_ready, i + 1)
                        if not st.first(2):
                            pe.wait_ge(copied, i - 1)
                        v = src_of(st)
                        transposes(r, v[0], v[1], tr_done)
                    st = st.back(1)
                    if st.real():
                        i, r = st.n, st.slot(2)
                        pe.wait_ge(copied, i + 1)
                        if not st.first(2):
                            pe.wait_ge(bank_free, i - 1)
                        for c in range(2):
                            ins = pe.matmul(ps[:, 1 + r, 0:H], aT[:, r, c, :], w[:, c, :], start=c == 0,
                                            stop=c == 1)
                        ins.then_inc(mm_done, 1)
                return body

            def h2_of(st):
                return h2[:, st.slot(2), 0:P], h2[:, st.slot(2), P:2 * P]

            def transpose_acc(st):
                i = st.n
                return acc0[:, i, 0:P], acc0[:, i, P:2 * P]

            body = proj(transpose_acc, None, s("aT"), s("a_tr"), wo_sb, s("wo_mm"), s("x1"))
            for i in range(NT + 1):
                body(Step(i // 2, i % 2, 2, NT))
            pe.wait_ge(s("x1"), NT)
            run(pe, NT, 4, 1, proj(h2_of, s("h2"), s("h2T"), s("h2_tr"), W_sb, s("w_mm"), s("h2c")))

            pe.wait_ge(s("h2c"), NT)

            def spread_hr(b, j):
                n, r, r8 = b.n, b.slot(2), b.slot(8)
                if j == 0:
                    pe.wait_ge(s(f"row1_in{r8}"), 32 * b.turn(8) + 32)
                    pe.wait_ge(s("pen"), n + 1)
                if not b.first(1):
                    pe.wait_ge(s("gmax"), 2 * n + j - 1)
                bank = ps[:, 1 + j, :]
                parts = row1_g[:, r8, j, HP:ROW1].bitcast(BF16)
                for h in range(NH1):
                    for part in range(3):
                        i = part * NH1 + h
                        pe.matmul(bank[:, h * P:(h + 1) * P], parts[:, i:i + 1].to_broadcast([P, P]), ident_b[:, :],
                                  start=h == 0 and part == 0, stop=False)
                pe.matmul(bank.rearrange("p (h e) -> p h e", h=NH1), ident_b[:, :],
                          pen[:, r, j * P:(j + 1) * P].unsqueeze(1).to_broadcast([P, NH1, P]),
                          start=False, stop=True).then_inc(s("hr_mm"), 1)

            def layer1(st):
                a = st.back(1)
                if a.real():
                    one_hot_T(a, s("oneh1"), s("onehT1"), s("oneh_tr1"))
                b = st.back(2)
                if b.real():
                    spread_hr(b, 0)
                c = st.back(4)
                if c.real():
                    n, r, r4 = c.n, c.slot(2), c.slot(4)
                    pe.wait_ge(s("onehT1"), n + 1)
                    pe.wait_ge(s("hm_ready"), n + 1)
                    if not c.first(2):
                        pe.wait_ge(s("es"), n - 1)
                    for j in range(GJ):
                        ins = pe.matmul(ps[:, 3 + r, j * 8:j * 8 + 8], onehT4[:, r4, j, :],
                                        hm[:, r4, :], start=True, stop=True)
                    ins.then_inc(s("hm_mm"), 1)
                if b.real():
                    spread_hr(b, 1)
                d = st.back(7)
                if d.real():
                    n, r, r8 = d.n, d.slot(2), d.slot(8)
                    pe.wait_ge(s("msg1_ready"), n + 1)
                    pe.wait_ge(s("msg1b_ready"), n + 1)
                    if not d.first(2):
                        pe.wait_ge(s("acc1_done"), n - 1)
                    for j in range(GJ):
                        ins = pe.matmul(ps[:, 5 + r, 0:NH1 * HE], oneh[:, r8, j, :], msg1[:, r, j, :],
                                        start=j == 0, stop=j == GJ - 1)
                    ins.then_inc(s("agg1_ready"), 1)

            run(pe, NG, 8, 8, layer1)


def run8(eng, total, body):
    for u in range(8):
        body(0, u)
    with eng.Fori(1, total // 8 - 1) as k:
        for u in range(8):
            body(k, u)
    for t in range(total // 8 * 8 - 8, total + 2):
        body(t // 8, t % 8)


_INS = ["x", "src", "dst", "edge_attr_64", "edge_weight", "L0_gnn_w1", "L0_gnn_b1", "L0_gnn_w2", "L0_gnn_b2",
        "L0_gnn_ln_w", "L0_gnn_ln_b", "L0_gnn_wq", "L0_gnn_bq", "L0_gnn_wk", "L0_gnn_bk", "L0_gnn_wv",
        "L0_gnn_bv", "L0_gnn_wo", "L0_gnn_bo", "L0_gnn_gate", "L1_gnn_W", "L1_gnn_a_l", "L1_gnn_a_r"]


def kernel(**inputs):
    import concourse.bacc as _bacc
    from concourse.bass_utils import run_bass_kernel_spmd as _run

    nc = _bacc.Bacc("TRN2", target_bir_lowering=False, num_devices=1)
    arrays, args = {}, []
    for name in _INS:
        a = np.ascontiguousarray(inputs[name])
        arrays[f"in_{name}"] = a
        args.append(nc.dram_tensor(f"in_{name}", a.shape, mybir.dt.from_np(a.dtype), kind="ExternalInput").ap())
    shape = inputs["x"].shape
    o = nc.dram_tensor("out_0", shape, F32, kind="ExternalOutput").ap()
    gnn_kernel(nc, *args, o)
    r = _run(nc, [arrays], core_ids=[0])
    return r.results[0]["out_0"]
```
